# Optimizing a Trainium2 kernel written in Bass

```python
import numpy as np
import jax
import jax.numpy as jnp

def _softmax(x, axis=-1):
    return jax.nn.softmax(x, axis=axis)
def _gelu(x):
    return jax.nn.gelu(x, approximate=True)
def _silu(x):
    return jax.nn.silu(x)
def _sigmoid(x):
    return jax.nn.sigmoid(x)
def _layernorm(x, axis=-1, eps=1e-5):
    m = jnp.mean(x, axis=axis, keepdims=True)
    v = jnp.var(x, axis=axis, keepdims=True)
    return (x - m) / jnp.sqrt(v + eps)
def _scatter_add(tgt, idx, src, axis=0):
    return tgt.at[idx].add(src)
def _segment_sum(src, seg, n):
    return jax.ops.segment_sum(src, seg, n)

kernel_name = 'mk_metaformer_d2_conv_nchw128_f54d9c'

def setup_inputs(seed: int = 0):
    np.random.seed(seed)
    _w = jnp.asarray
    def _rec_inputs():
        import jax
        import jax.numpy as jnp
        _gk = jax.random.key(seed)
        x = -0.0003929 + 0.9999 * jax.random.normal(jax.random.fold_in(_gk, 1), (8, 128, 128, 128), jnp.float32)
        return x
    x = _rec_inputs()
    def _L0_conv_setup():
        import jax, jax.numpy as jnp
        import numpy as np
        K = 3
        DIL = 2
        PAD = 2
        EPS = 1e-05
        key = jax.random.key(seed)
        ks = jax.random.split(key, 6)
        b, c, h, w = (8, 128, 128, 128)
        c_red = c // 8
        k2 = K * K
        x = jax.random.normal(ks[0], (b, c, h, w), dtype=jnp.float32)
        w1 = jax.random.normal(ks[1], (c_red, c), dtype=jnp.float32) * (1.0 / np.sqrt(c))
        in_gamma = jnp.ones((c_red,), dtype=jnp.float32)
        in_beta = jnp.zeros((c_red,), dtype=jnp.float32)
        w2 = jax.random.normal(ks[2], (k2 * c, c_red), dtype=jnp.float32) * (1.0 / np.sqrt(c_red))
        b2 = jnp.zeros((k2 * c,), dtype=jnp.float32)
        return {'x': x, 'w1': w1, 'in_gamma': in_gamma, 'in_beta': in_beta, 'w2': w2, 'b2': b2}
    _L0_conv_all = _L0_conv_setup()
    _L0_conv_in = {k: v for k, v in _L0_conv_all.items() if k in ('w1', 'in_gamma', 'in_beta', 'w2', 'b2', )}
    del _L0_conv_all

    def _L0_ffn_setup():
        import jax, jax.numpy as jnp
        import numpy as np
        B, S, D, E, H, O, K = (512, 2048, 128, 64, 512, 128, 8)
        key = jax.random.key(seed)
        k0, k1, k2, k3 = jax.random.split(key, 4)
        x = jax.random.normal(k0, (B, S, D), dtype=jnp.float32)
        gate_w = jax.random.normal(k1, (E, D), dtype=jnp.float32) * (1.0 / np.sqrt(D))
        gate_b = jnp.zeros((E,), dtype=jnp.float32)
        weight1 = jax.random.uniform(k2, (E, D + 1, H), dtype=jnp.float32, minval=-1.0, maxval=1.0) * (1.0 / np.sqrt(D + 1))
        weight2 = jax.random.uniform(k3, (E, H + 1, O), dtype=jnp.float32, minval=-1.0, maxval=1.0) * (1.0 / np.sqrt(H + 1))
        return {'x': x, 'gate_w': gate_w, 'gate_b': gate_b, 'weight1': weight1, 'weight2': weight2}
    _L0_ffn_all = _L0_ffn_setup()
    _L0_ffn_in = {k: v for k, v in _L0_ffn_all.items() if k in ('gate_w', 'gate_b', 'weight1', 'weight2', )}
    del _L0_ffn_all

    def _L1_conv_setup():
        import jax, jax.numpy as jnp
        from jax import lax
        import numpy as np
        UP = 2
        DOWN = 2
        PAD_LO = 11
        PAD_HI = 10
        SLOPE = 0.2
        GAIN = np.sqrt(2.0).astype(np.float32)

        def _kaiser_beta(atten):
            if atten > 50:
                return 0.1102 * (atten - 8.7)
            if atten > 21:
                return 0.5842 * (atten - 21.0) ** 0.4 + 0.07886 * (atten - 21.0)
            return 0.0

        def _firwin(numtaps, cutoff, width, fs):
            nyq = fs / 2.0
            atten = 2.285 * (numtaps - 1) * np.pi * (width / nyq) + 7.95
            beta = _kaiser_beta(atten)
            m = np.arange(numtaps) - (numtaps - 1) / 2.0
            fc = cutoff / nyq
            h = fc * np.sinc(fc * m) * np.kaiser(numtaps, beta)
            h = h / h.sum()
            return h.astype(np.float32)

        def _depthwise_conv1d(x, f, axis, stride=1, lhs_dilation=1, padding=(0, 0)):
            C = x.shape[1]
            k = f.shape[0]
            fr = f[::-1]
            if axis == 2:
                kern = jnp.broadcast_to(fr.reshape(1, 1, k, 1), (C, 1, k, 1))
                strides, ld, pads = ((stride, 1), (lhs_dilation, 1), [padding, (0, 0)])
            else:
                kern = jnp.broadcast_to(fr.reshape(1, 1, 1, k), (C, 1, 1, k))
                strides, ld, pads = ((1, stride), (1, lhs_dilation), [(0, 0), padding])
            return lax.conv_general_dilated(x, kern, window_strides=strides, padding=pads, lhs_dilation=ld, dimension_numbers=('NCHW', 'OIHW', 'NCHW'), feature_group_count=C)
        key = jax.random.key(seed)
        k1, k2 = jax.random.split(key)
        x = jax.random.normal(k1, (32, 128, 64, 64), dtype=jnp.float32)
        bias = jax.random.normal(k2, (128,), dtype=jnp.float32) * 0.1
        up_filter = jnp.asarray(_firwin(12, 28.0, 8.0, 128.0))
        down_filter = jnp.asarray(_firwin(12, 28.0, 8.0, 128.0))
        return {'x': x, 'bias': bias, 'up_filter': up_filter, 'down_filter': down_filter}
    _L1_conv_all = _L1_conv_setup()
    _L1_conv_in = {k: v for k, v in _L1_conv_all.items() if k in ('bias', 'up_filter', 'down_filter', )}
    del _L1_conv_all

    def _L1_ffn_setup():
        import jax, jax.numpy as jnp
        import numpy as np
        B, N, D, C, E, K = (8, 8192, 128, 128, 8, 2)
        key = jax.random.key(seed)
        k0, k1, k2 = jax.random.split(key, 3)
        x = jax.random.normal(k0, (B, N, D), dtype=jnp.float32)
        router_w = jax.random.normal(k1, (D, E), dtype=jnp.float32) * 0.05
        router_b = jnp.zeros((E,), dtype=jnp.float32)
        expert_w = jax.random.normal(k2, (E, D, C), dtype=jnp.float32) * (1.0 / np.sqrt(D))
        expert_b = jnp.zeros((E, C), dtype=jnp.float32)
        return {'x': x, 'router_w': router_w, 'router_b': router_b, 'expert_w': expert_w, 'expert_b': expert_b}
    _L1_ffn_all = _L1_ffn_setup()
    _L1_ffn_in = {k: v for k, v in _L1_ffn_all.items() if k in ('router_w', 'router_b', 'expert_w', 'expert_b', )}
    del _L1_ffn_all

    return {
        "x": x,
        "L0_conv_w1": _L0_conv_in["w1"],
        "L0_conv_in_gamma": _L0_conv_in["in_gamma"],
        "L0_conv_in_beta": _L0_conv_in["in_beta"],
        "L0_conv_w2": _L0_conv_in["w2"],
        "L0_conv_b2": _L0_conv_in["b2"],
        "L0_ffn_gate_w": _L0_ffn_in["gate_w"],
        "L0_ffn_gate_b": _L0_ffn_in["gate_b"],
        "L0_ffn_weight1": _L0_ffn_in["weight1"],
        "L0_ffn_weight2": _L0_ffn_in["weight2"],
        "L1_conv_bias": _L1_conv_in["bias"],
        "L1_conv_up_filter": _L1_conv_in["up_filter"],
        "L1_conv_down_filter": _L1_conv_in["down_filter"],
        "L1_ffn_router_w": _L1_ffn_in["router_w"],
        "L1_ffn_router_b": _L1_ffn_in["router_b"],
        "L1_ffn_expert_w": _L1_ffn_in["expert_w"],
        "L1_ffn_expert_b": _L1_ffn_in["expert_b"],
    }

def reference(x, L0_conv_w1, L0_conv_in_gamma, L0_conv_in_beta, L0_conv_w2, L0_conv_b2, L0_ffn_gate_w, L0_ffn_gate_b, L0_ffn_weight1, L0_ffn_weight2, L1_conv_bias, L1_conv_up_filter, L1_conv_down_filter, L1_ffn_router_w, L1_ffn_router_b, L1_ffn_expert_w, L1_ffn_expert_b):
    import jax
    import jax.numpy as jnp
    def _L0_conv_ref(x, w1, in_gamma, in_beta, w2, b2):
        import jax, jax.numpy as jnp
        import numpy as np
        K = 3
        DIL = 2
        PAD = 2
        EPS = 1e-05
        b, c, h, w = x.shape
        k2 = K * K
        t = jnp.einsum('oc,bchw->bohw', w1, x)
        mean = t.mean(axis=(2, 3), keepdims=True)
        var = t.var(axis=(2, 3), keepdims=True)
        t = (t - mean) * jax.lax.rsqrt(var + EPS)
        t = t * in_gamma[None, :, None, None] + in_beta[None, :, None, None]
        t = jax.nn.relu(t)
        wgt = jnp.einsum('oc,bchw->bohw', w2, t) + b2[None, :, None, None]
        wgt = wgt.reshape(b, c, k2, h, w)
        xp = jnp.pad(x, ((0, 0), (0, 0), (PAD, PAD), (PAD, PAD)))
        patches = jnp.stack([xp[:, :, DIL * i:DIL * i + h, DIL * j:DIL * j + w] for i in range(K) for j in range(K)], axis=2)
        return (wgt * patches).sum(axis=2)

    def _L0_ffn_ref(x, gate_w, gate_b, weight1, weight2):
        import jax, jax.numpy as jnp
        import numpy as np
        B, S, D, E, H, O, K = (512, 2048, 128, 64, 512, 128, 8)
        Bn, Sn, Dn = x.shape
        logits = jnp.einsum('bsd,ed->bse', x, gate_w) + gate_b
        probs = jax.nn.softmax(logits, axis=1)
        vals, idx = jax.lax.top_k(probs.transpose(0, 2, 1), K)
        topv = vals.transpose(0, 2, 1)
        topi = idx.transpose(0, 2, 1)
        flat_idx = topi.reshape(Bn, K * E)
        gathered = jnp.take_along_axis(x, flat_idx[:, :, None], axis=1)
        gathered = gathered.reshape(Bn, K, E, Dn)
        pooled = jnp.einsum('bked,bke->bed', gathered, topv)
        ones = jnp.ones((E, Bn, 1), dtype=x.dtype)
        h = jnp.concatenate([pooled.transpose(1, 0, 2), ones], axis=-1)
        h = jax.nn.gelu(jnp.einsum('ebd,edh->ebh', h, weight1), approximate=False)
        h = jnp.concatenate([h, ones], axis=-1)
        out = jnp.einsum('ebh,eho->ebo', h, weight2)
        out = out.transpose(1, 0, 2)
        weighted = jnp.einsum('beo,bke->bkeo', out, topv).reshape(Bn, K * E, O)
        outputs = jnp.zeros((Bn, Sn, O), dtype=x.dtype)
        outputs = outputs.at[jnp.arange(Bn)[:, None], flat_idx].add(weighted)
        return outputs

    def _L1_conv_ref(x, bias, up_filter, down_filter):
        import jax, jax.numpy as jnp
        from jax import lax
        import numpy as np
        UP = 2
        DOWN = 2
        PAD_LO = 11
        PAD_HI = 10
        SLOPE = 0.2
        GAIN = np.sqrt(2.0).astype(np.float32)

        def _kaiser_beta(atten):
            if atten > 50:
                return 0.1102 * (atten - 8.7)
            if atten > 21:
                return 0.5842 * (atten - 21.0) ** 0.4 + 0.07886 * (atten - 21.0)
            return 0.0

        def _firwin(numtaps, cutoff, width, fs):
            nyq = fs / 2.0
            atten = 2.285 * (numtaps - 1) * np.pi * (width / nyq) + 7.95
            beta = _kaiser_beta(atten)
            m = np.arange(numtaps) - (numtaps - 1) / 2.0
            fc = cutoff / nyq
            h = fc * np.sinc(fc * m) * np.kaiser(numtaps, beta)
            h = h / h.sum()
            return h.astype(np.float32)

        def _depthwise_conv1d(x, f, axis, stride=1, lhs_dilation=1, padding=(0, 0)):
            C = x.shape[1]
            k = f.shape[0]
            fr = f[::-1]
            if axis == 2:
                kern = jnp.broadcast_to(fr.reshape(1, 1, k, 1), (C, 1, k, 1))
                strides, ld, pads = ((stride, 1), (lhs_dilation, 1), [padding, (0, 0)])
            else:
                kern = jnp.broadcast_to(fr.reshape(1, 1, 1, k), (C, 1, 1, k))
                strides, ld, pads = ((1, stride), (1, lhs_dilation), [(0, 0), padding])
            return lax.conv_general_dilated(x, kern, window_strides=strides, padding=pads, lhs_dilation=ld, dimension_numbers=('NCHW', 'OIHW', 'NCHW'), feature_group_count=C)
        fu = up_filter * UP
        pad = (PAD_LO, PAD_HI + UP - 1)
        y = _depthwise_conv1d(x, fu, axis=2, lhs_dilation=UP, padding=pad)
        y = _depthwise_conv1d(y, fu, axis=3, lhs_dilation=UP, padding=pad)
        y = y + bias[None, :, None, None]
        y = jnp.where(y >= 0, y, SLOPE * y) * GAIN
        y = _depthwise_conv1d(y, down_filter, axis=2, stride=DOWN)
        y = _depthwise_conv1d(y, down_filter, axis=3, stride=DOWN)
        return y

    def _L1_ffn_ref(x, router_w, router_b, expert_w, expert_b):
        import jax, jax.numpy as jnp
        import numpy as np
        B, N, D, C, E, K = (8, 8192, 128, 128, 8, 2)
        router_probs = jax.nn.softmax(x @ router_w + router_b, axis=-1)
        top_p, top_i = jax.lax.top_k(router_probs, K)
        top_p = top_p / jnp.sum(top_p, axis=-1, keepdims=True)
        expert_out = jnp.einsum('bnd,edc->bnec', x, expert_w) + expert_b
        gathered = jnp.take_along_axis(expert_out, top_i[..., None], axis=2)
        return jnp.einsum('bnk,bnkc->bnc', top_p, gathered)

    def _gn(v, G=32, eps=1e-5):
        B_, C_, H_, W_ = v.shape
        g = v.reshape(B_, G, C_ // G, H_, W_)
        m = jnp.mean(g, axis=(2, 3, 4), keepdims=True)
        s = jnp.var(g, axis=(2, 3, 4), keepdims=True)
        return ((g - m) / jnp.sqrt(s + eps)).reshape(v.shape)

    def _ln_c(v, eps=1e-6):
        m = jnp.mean(v, axis=1, keepdims=True)
        s = jnp.var(v, axis=1, keepdims=True)
        return (v - m) / jnp.sqrt(s + eps)

    def _ln_t(v, eps=1e-5):
        m = jnp.mean(v, axis=-1, keepdims=True)
        s = jnp.var(v, axis=-1, keepdims=True)
        return (v - m) / jnp.sqrt(s + eps)

    def _to_tokens(v):
        B_, C_, H_, W_ = v.shape
        return v.reshape(B_, C_, H_ * W_).transpose(0, 2, 1)
    def _from_tokens(t, like):
        B_, C_, H_, W_ = like.shape
        return t.transpose(0, 2, 1).reshape(B_, C_, H_, W_)

    x = x + _L0_conv_ref(_ln_c(x), L0_conv_w1, L0_conv_in_gamma, L0_conv_in_beta, L0_conv_w2, L0_conv_b2)
    t = _to_tokens(x)
    t = t + _L0_ffn_ref(_ln_t(t), L0_ffn_gate_w, L0_ffn_gate_b, L0_ffn_weight1, L0_ffn_weight2)
    x = _from_tokens(t, x)
    x = x + _L1_conv_ref(_ln_c(x), L1_conv_bias, L1_conv_up_filter, L1_conv_down_filter)
    t = _to_tokens(x)
    t = t + _L1_ffn_ref(_ln_t(t), L1_ffn_router_w, L1_ffn_router_b, L1_ffn_expert_w, L1_ffn_expert_b)
    x = _from_tokens(t, x)
    return x


_drawn_inputs = setup_inputs


def setup_inputs(seed=0):
    import zlib

    import numpy as np

    out = dict(_drawn_inputs(seed))
    spreads = {'L0_conv_in_gamma': (1.0, 0.2),
     'L0_conv_in_beta': (0.0, 0.1),
     'L0_conv_b2': (0.0, 0.1),
     'L0_ffn_gate_b': (0.0, 0.1),
     'L1_ffn_router_b': (0.0, 0.1),
     'L1_ffn_expert_b': (0.0, 0.34)}
    factors = {'L0_ffn_gate_w': 8.0, 'L0_ffn_weight1': 8.0, 'L0_ffn_weight2': 8.0}
    for name, (base, spread) in spreads.items():
        noise = np.random.default_rng([zlib.crc32(name.encode()), seed]).standard_normal(out[name].shape)
        drawn = base * np.exp(spread * noise) if base else spread * noise
        out[name] = jnp.asarray(drawn.astype(out[name].dtype))
    for name, factor in factors.items():
        out[name] = (out[name] * factor).astype(out[name].dtype)
    return out
```

```python
from contextlib import ExitStack

import numpy as np

import concourse.bass as bass
from concourse import mybir

F32 = mybir.dt.float32
BF16 = mybir.dt.bfloat16
U32 = mybir.dt.uint32
ALU = mybir.AluOpType
ACT = mybir.ActivationFunctionType
AX_X = mybir.AxisListType.X

B, C, H, W = 8, 128, 128, 128
TOKENS = H * W
ROWS = 4
TILE = ROWS * W
TILES = H // ROWS
RED = 16
TAPS = 9
PAD = 2
HP = H + 2 * PAD
E0, K0, HID = 64, 8, 512
HALF = TOKENS // 2
NEG, BIG = -3.0e38, 2.0 ** 127
FT = 12
UPN = 2 * H + 10
REM = UPN - 2 * H
GC = 8
GROUPS = C // GC
RP = GC * REM
EDGE = 5
SLOPE, GAIN = 0.2, float(np.sqrt(2.0).astype(np.float32))
E1 = 8
ACT_EXPERTS = 4
DVE_EXPERTS = E1 - ACT_EXPERTS

CREDIT = 16


def done(n):
    return n + (CREDIT + 1)


def rounds(n):
    return (n + 1) * 16


def item(i, u, lag):
    d = u - lag
    p = d % 2
    half = i + (d - p) // 2
    return half * 2 + p, p, half


def settle(eng, passed):
    eng.sem_inc(passed, 1)


def walk(eng, passed, step, count, lag, parts=1):
    head = (lag + 1) // 2
    size = count // 2 // parts
    for part in range(parts):
        for i in range(part * size, part * size + head):
            for u in range(2):
                step(i, u, part)
        settle(eng, passed)
        with eng.Fori(part * size + head, (part + 1) * size) as i:
            for u in range(2):
                step(i, u, part)
    for s in range(count, count + lag):
        step(s // 2, s % 2, parts)


def live(j, count):
    return not isinstance(j, int) or 0 <= j < count


class Chain:

    def __init__(self, eng, sem, base):
        self.eng, self.sem, self.base, self.n = eng, sem, base, 0

    def __call__(self, ins):
        self.n += 1
        ins.then_inc(self.sem, 1)
        self.eng.wait_ge(self.sem, self.base + self.n)


def metaformer_kernel(nc, x, w1, in_gamma, in_beta, w2, b2, gate_w, gate_b, ew1, ew2,
                      conv_bias, up_filter, down_filter, router_w, router_b, expert_w, expert_b, out):
    x1_dram = nc.dram_tensor("x1_dram", (B, C, H, W), F32).ap()
    xT_dram = nc.dram_tensor("xT_dram", (TOKENS, C), F32).ap()
    rA_dram = nc.dram_tensor("rA_dram", (3, TOKENS), BF16).ap()
    rB_dram = nc.dram_tensor("rB_dram", (3, 2, HALF), BF16).ap()
    S_dram = nc.dram_tensor("S_dram", (B, E0, TOKENS), F32).ap()

    with ExitStack() as ctx:
        def sb(name, shape, dt=F32):
            return ctx.enter_context(nc.sbuf_tensor(name, shape, dt))

        def sem(name):
            return ctx.enter_context(nc.semaphore(name))

        bank = [ctx.enter_context(nc.psum_tensor(f"bank{i}", [128, 512], F32)) for i in range(4)]
        duo = [ctx.enter_context(nc.psum_tensor(f"duo{i}", [128, 2, 512], F32)) for i in range(2)]

        ident = sb("ident", [128, 128])
        center = sb("center", [128, 128])
        mean_col = sb("mean_col", [128, 1])
        eps6 = sb("eps6", [128, 1])
        eps5 = sb("eps5", [128, 1])
        ones3 = sb("ones3", [3, 128], BF16)
        sel6 = sb("sel6", [6, 128], BF16)
        w1rep = sb("w1rep", [128, 128])
        gamma_rep = sb("gamma_rep", [128, 1])
        beta_rep = sb("beta_rep", [128, 1])
        wstack = sb("wstack", [128, TAPS, 128], BF16)
        gateT = sb("gateT", [128, E0])
        gate_bias = sb("gate_bias", [E0, 1])
        slots16 = sb("slots16", [E0, 16])
        up_mat = sb("up_mat", [128, UPN])
        down_mat = sb("down_mat", [128, 2, 128])
        down_edge = sb("down_edge", [RP, GC, EDGE])
        down_edge1 = sb("down_edge1", [RP, EDGE])
        block_mask = sb("block_mask", [RP, GC, REM])
        bias_all = sb("bias_all", [128, C])
        bias_rem = sb("bias_rem", [RP, GROUPS])
        router = sb("router", [128, E1])
        router_b_all = sb("router_b_all", [128, E1])
        desc8 = sb("desc8", [128, E1])
        ebias = sb("ebias", [ROWS * E1, ROWS, 128])
        pooledT = sb("pooledT", [128, B, E0])
        moeT = sb("moeT", [128, E0, B])
        rsum_all = sb("rsum_all", [E0, B])

        s_fill = sem("s_fill")
        s_load = sem("s_load")
        s_dve0 = sem("s_dve0")
        s_pe0 = sem("s_pe0")

        passed = sem("passed")

        def credit(eng, *names):
            for s in names:
                eng.sem_inc(s, CREDIT)

        with ExitStack() as tmp:
            def tb(name, shape, dt=F32):
                return tmp.enter_context(nc.sbuf_tensor(name, shape, dt))

            w1x = tb("w1x", [128, 128])
            gw = tb("gw", [E0, 128])
            gwT = tb("gwT", [128, E0])
            w2n = tb("w2n", [128, TAPS, RED])
            b2n = tb("b2n", [128, TAPS, 1])
            part16 = tb("part16", [128, TAPS, RED + 1], BF16)
            rest = tb("rest", [128, TAPS, RED + 1])
            rest2 = tb("rest2", [128, TAPS, RED + 1])
            stack_rows = tb("stack_rows", [128, TAPS, 128])
            fu = tb("fu", [128, FT])
            fd = tb("fd", [128, FT])
            cb = tb("cb", [128, C])
            up_tap = tb("up_tap", [128, FT, UPN])
            down_tap = tb("down_tap", [128, 2, FT, 128])
            edge_tap = tb("edge_tap", [RP, FT, GC, EDGE])
            edge_sum = tb("edge_sum", [RP, GC, EDGE])
            brem = tb("brem", [RP, GROUPS, GC])
            ones_t = tb("ones_t", [128, 128])
            zeros_t = tb("zeros_t", [128, 128])
            ones_b = tb("ones_b", [6, 128], BF16)
            sel_b = tb("sel_b", [6, 128], BF16)
            ones_m = tb("ones_m", [RP, GC, REM])
            ones_m2 = tb("ones_m2", [RP, GC, REM])
            slots_i = tb("slots_i", [E0, 16], mybir.dt.int32)
            desc_i = tb("desc_i", [128, E1], mybir.dt.int32)

            n_zero = 9
            small = [(gw, gate_w), (w2n, w2.rearrange("(c k) o -> c k o", k=TAPS)),
                     (b2n, b2.rearrange("(c k a) -> c k a", k=TAPS, a=1)),
                     (gate_bias, gate_b.rearrange("(e a) -> e a", a=1)),
                     (fu, up_filter.partition_broadcast(128)), (fd, down_filter.partition_broadcast(128)),
                     (cb, conv_bias.partition_broadcast(128)), (router, router_w),
                     (router_b_all, router_b.partition_broadcast(128))]
            groups = [0, 1, 2, 4, 5, 6, 7]
            n_loads = len(small) + 3 * len(groups) + ROWS
            filled = n_zero + 11 + 4 * FT
            dve_steps = []
            with nc.Block() as block:
                @block.gpsimd
                def _(pool):
                    g = nc.gpsimd
                    for t, v in ((w1x, 0.0), (gamma_rep, 0.0), (beta_rep, 1.0), (ebias, 0.0), (stack_rows, 0.0),
                                 (ones_t, 1.0), (zeros_t, 0.0), (ones_b, 1.0), (ones_m, 1.0)):
                        g.memset(t[:], v).then_inc(s_fill, 1)
                    pool.wait_ge(s_fill, n_zero)
                    g.memset(mean_col[:], 1.0 / C).then_inc(s_fill, 1)
                    g.memset(eps6[:], 1e-6).then_inc(s_fill, 1)
                    g.memset(eps5[:], 1e-5).then_inc(s_fill, 1)
                    g.memset(ones3[:], 1.0).then_inc(s_fill, 1)
                    g.affine_select(out=ident[:], in_=zeros_t[:], compare_op=ALU.not_equal, fill=1.0, base=0,
                                    pattern=[[-1, 128]], channel_multiplier=1).then_inc(s_fill, 1)
                    g.affine_select(out=sel_b[:, 0:64], in_=ones_b[:, 0:64], compare_op=ALU.is_ge, fill=0.0, base=2,
                                    pattern=[[0, 64]], channel_multiplier=-1).then_inc(s_fill, 1)
                    g.affine_select(out=sel_b[:, 64:128], in_=ones_b[:, 64:128], compare_op=ALU.is_ge, fill=0.0,
                                    base=-3, pattern=[[0, 64]], channel_multiplier=1).then_inc(s_fill, 1)
                    g.iota(slots_i[:], pattern=[[1, 16]], base=0, channel_multiplier=0).then_inc(s_fill, 1)
                    g.iota(desc_i[:], pattern=[[-1, E1]], base=E1, channel_multiplier=0).then_inc(s_fill, 1)
                    g.affine_select(out=ones_m2[:], in_=ones_m[:], compare_op=ALU.is_ge, fill=0.0, base=0,
                                    pattern=[[-REM, GC], [0, REM]], channel_multiplier=1).then_inc(s_fill, 1)
                    pool.wait_ge(s_fill, n_zero + 10)
                    g.affine_select(out=block_mask[:], in_=ones_m2[:], compare_op=ALU.is_ge, fill=0.0, base=REM - 1,
                                    pattern=[[REM, GC], [0, REM]], channel_multiplier=-1).then_inc(s_fill, 1)
                    pool.wait_ge(s_load, 16 * n_loads)
                    for t in range(FT):
                        g.affine_select(out=up_tap[:, t, :], in_=fu[:, t:t + 1].to_broadcast([128, UPN]),
                                        compare_op=ALU.is_equal, fill=0.0, base=-t, pattern=[[1, UPN]],
                                        channel_multiplier=-2).then_inc(s_fill, 1)
                        for m in range(2):
                            g.affine_select(out=down_tap[:, m, t, :], in_=fd[:, t:t + 1].to_broadcast([128, 128]),
                                            compare_op=ALU.is_equal, fill=0.0, base=128 * m - (FT - 1) + t,
                                            pattern=[[-2, 128]], channel_multiplier=1).then_inc(s_fill, 1)
                        first = 2 * H - (FT - 1) + t - 2 * (128 - EDGE)
                        g.affine_select(out=edge_tap[:, t, :, :],
                                        in_=fd[0:RP, t:t + 1].unsqueeze(2).to_broadcast([RP, GC, EDGE]),
                                        compare_op=ALU.is_equal, fill=0.0, base=first,
                                        pattern=[[-REM, GC], [-2, EDGE]], channel_multiplier=1).then_inc(s_fill, 1)

                @block.sync
                def _(sp):
                    for dst, src in small:
                        sp.dma_start(dst[:], src).then_inc(s_load, 16)
                    sp.wait_ge(s_fill, n_zero)
                    for q in groups:
                        at = slice(RED * q, RED * q + RED)
                        sp.dma_start(w1x[at, :], w1).then_inc(s_load, 16)
                        sp.dma_start(gamma_rep[at, :], in_gamma.rearrange("(e a) -> e a", a=1)).then_inc(s_load, 16)
                        sp.dma_start(beta_rep[at, :], in_beta.rearrange("(e a) -> e a", a=1)).then_inc(s_load, 16)
                    for q in range(ROWS):
                        sp.dma_start(ebias[q * E1:q * E1 + E1, q, :], expert_b).then_inc(s_load, 16)

                @block.vector
                def _(dve):
                    v = nc.vector
                    link = Chain(dve, s_dve0, 0)
                    dve.wait_ge(s_fill, filled)
                    dve.wait_ge(s_load, 16 * n_loads)
                    link(v.tensor_scalar(center[:], ident[:], -1.0 / C, None, ALU.add))
                    link(v.tensor_copy(slots16[:], slots_i[:]))
                    link(v.tensor_copy(desc8[:], desc_i[:]))
                    link(v.tensor_copy(sel6[:], sel_b[:]))
                    link(v.tensor_copy(rest[:, :, 0:RED], w2n[:]))
                    link(v.tensor_copy(rest[:, :, RED:RED + 1], b2n[:]))
                    for n, (cols, bcol) in enumerate((((0, 64, 96), 48), ((16, 80), 49), ((32,), 50))):
                        link(v.tensor_copy(part16[:], rest[:]))
                        for c0 in cols:
                            link(v.tensor_copy(stack_rows[:, :, c0:c0 + RED], part16[:, :, 0:RED]))
                        link(v.tensor_copy(stack_rows[:, :, bcol:bcol + 1], part16[:, :, RED:RED + 1]))
                        link(v.tensor_tensor(rest2[:], rest[:], part16[:], ALU.subtract))
                        link(v.tensor_copy(rest[:], rest2[:]))
                    link(v.tensor_scalar(up_mat[:], up_tap[:, 0, :], 1.0, None, ALU.mult))
                    for t in range(1, FT):
                        link(v.tensor_tensor(up_mat[:], up_mat[:], up_tap[:, t, :], ALU.add))
                    link(v.tensor_scalar(up_mat[:], up_mat[:], 2.0, None, ALU.mult))
                    link(v.tensor_copy(down_mat[:], down_tap[:, :, 0, :]))
                    for t in range(1, FT):
                        link(v.tensor_tensor(down_mat[:], down_mat[:], down_tap[:, :, t, :], ALU.add))
                    link(v.tensor_copy(edge_sum[:], edge_tap[:, 0]))
                    for t in range(1, FT):
                        link(v.tensor_tensor(edge_sum[:], edge_sum[:], edge_tap[:, t], ALU.add))
                    link(v.tensor_tensor(down_edge[:], edge_sum[:], block_mask[:, :, 0:EDGE], ALU.mult))
                    link(v.tensor_reduce(down_edge1[:], down_edge[:].rearrange("p c j -> p j c"), AX_X, ALU.add))
                    link(v.tensor_scalar(bias_all[:], cb[:], GAIN, None, ALU.mult))
                    link(v.tensor_tensor(brem[:], bias_all[0:RP, :].rearrange("p (g c) -> p g c", c=GC),
                                         block_mask[:, :, 0:1].rearrange("p c a -> p a c")
                                         .to_broadcast([RP, GROUPS, GC]), ALU.mult))
                    link(v.tensor_reduce(bias_rem[:], brem[:], AX_X, ALU.add))
                    for k in range(TAPS):
                        dve.wait_ge(s_pe0, k + 1)
                        link(v.tensor_copy(wstack[:, k, :], bank[k % 2][:, 0:128]))
                    dve.wait_ge(s_pe0, TAPS + 1)
                    link(v.tensor_copy(w1rep[:], bank[TAPS % 2][:, 0:128]))
                    dve.wait_ge(s_pe0, TAPS + 2)
                    link(v.tensor_copy(gwT[:], bank[(TAPS + 1) % 2][:, 0:E0]))
                    dve.wait_ge(s_pe0, TAPS + 3)
                    link(v.tensor_copy(gateT[:], bank[TAPS % 2][:, 0:E0]))
                    dve_steps.append(link.n)

                @block.tensor
                def _(pe):
                    t = nc.tensor
                    before = dve_steps[0] - TAPS - 3
                    for k in range(TAPS):
                        pe.wait_ge(s_dve0, before + max(k - 1, 0))
                        t.transpose(bank[k % 2][:, 0:128], stack_rows[:, k, :], ident[:]).then_inc(s_pe0, 1)
                    pe.wait_ge(s_dve0, before + TAPS - 1)
                    t.transpose(bank[TAPS % 2][:, 0:128], w1x[:], ident[:]).then_inc(s_pe0, 1)
                    pe.wait_ge(s_dve0, before + TAPS)
                    t.transpose(bank[(TAPS + 1) % 2][:, 0:E0], gw[:], ident[0:E0, 0:E0]).then_inc(s_pe0, 1)
                    pe.wait_ge(s_dve0, before + TAPS + 2)
                    t.matmul(bank[TAPS % 2][:, 0:E0], center[:], gwT[:], start=True, stop=True).then_inc(s_pe0, 1)

        with ExitStack() as tmp:
            def tb(name, shape, dt=F32):
                return tmp.enter_context(nc.sbuf_tensor(name, shape, dt))

            def pair(name, shape, dt=F32):
                return [tb(f"{name}{u}", shape, dt) for u in range(2)]

            xn = tb("xn", [128, HP, HP])
            logits = tb("logits", [128, HALF + 8])
            picked = tb("picked", [128, HALF + 8], BF16)
            x_in = pair("x_in", [128, TILE])
            std = tb("std", [128, H])
            rstd = tb("rstd", [128, H])
            var_all = tb("var_all", [128, H])
            r_part = [tb(f"r_part{k}", [128, W], BF16) for k in range(3)]
            r_rest = tb("r_rest", [128, W])
            rA = pair("rA", [3, TILE], BF16)
            rB = pair("rB", [6, TILE], BF16)
            t_stats = tb("t_stats", [128, TILES * 6])
            t_mv = tb("t_mv", [128, 2])
            t_tmp = tb("t_tmp", [128, 2])
            t_scale = tb("t_scale", [128, 1])
            t_bias = tb("t_bias", [128, 1])
            stack = pair("stack", [128, TILE], BF16)
            t_full = pair("t_full", [128, TILE])
            t_high = pair("t_high", [128, TILE], BF16)
            t_rest = pair("t_rest", [128, TILE])
            square = t_rest
            prod_all = tb("prod_all", [128, TAPS, TILE])
            prod = [prod_all[:, k, :] for k in range(TAPS)]
            psum_in = [pair(f"part_sum{k}", [128, TILE]) for k in range(4)]
            x_res = pair("x_res", [128, TILE])
            x1 = pair("x1", [128, TILE])
            x1T = pair("x1T", [128, ROWS, C])
            sq_junk = tb("sq_junk", [128, ROWS, C], BF16)
            var4 = pair("var4", [128, ROWS])
            top_half = tb("top_half", [128, 8])
            idx_half = tb("idx_half", [128, 8], U32)
            idxf_half = tb("idxf_half", [128, 8])
            cand = tb("cand", [E0, 16])
            cand_idx = tb("cand_idx", [E0, 16])
            top = tb("top", [E0, 8])
            pos = tb("pos", [E0, 8], U32)
            posf = tb("posf", [E0, 8])
            cand_mark = tb("cand_mark", [E0, 16])
            kept = tb("kept", [E0, 16])
            kept2 = tb("kept2", [E0, 16])
            lists = tb("lists", [E0, 17])
            find = tb("find", [128, 9])
            token_eq = tb("token_eq", [E0, K0, 16])
            token_f = tb("token_f", [E0, K0])
            token = tb("token", [E0, K0], U32)
            zsum = tb("zsum", [128, 1])
            zsum2 = tb("zsum2", [E0, 1])
            zinv = tb("zinv", [E0, 1])
            rsum_b = tb("rsum_b", [E0, 1])
            top_exp = tb("top_exp", [E0, K0])
            rows = prod_all[0:E0, 0:2, :].rearrange("e a (k c) -> e (a k) c", c=C)
            rows_sq = prod_all[0:E0, 2:4, :].rearrange("e a (k c) -> e (a k) c", c=C)
            row_var = tb("row_var", [E0, K0])
            row_std = tb("row_std", [E0, K0])
            row_w = tb("row_w", [E0, K0])
            pooled = tb("pooled", [E0, C])

            centre_ps, rb_ps = bank[0:2], bank[0:2]
            t_ps, raw_ps = bank[2], bank[3]
            wgt_ps = [bank[0], bank[1], duo[0][:, 0]]
            acc_ps, xT_ps = duo[0][:, 1], duo[1][:, 0]
            var_ps = [bank[2 + u][:, 0:ROWS] for u in range(2)]
            turn_ps = duo[1][:, 1, 128:256]
            pool_ps = duo[1][:, 1, 256:256 + E0]

            def nsem(name):
                return tmp.enter_context(nc.semaphore(name))

            ld_x = [nsem(f"ld_x{u}") for u in range(2)]
            centred = nsem("centred")
            squared = nsem("squared")
            varied = nsem("varied")
            var_kept = nsem("var_kept")
            std_ready = nsem("std_ready")
            split_chain = nsem("split_chain")
            turned = nsem("turned")
            st_r = [nsem(f"st_r{k}") for k in range(3)]
            ld_rA = [nsem(f"ld_rA{u}") for u in range(2)]
            ld_rB = [[nsem(f"ld_rB{u}{h}") for h in range(2)] for u in range(2)]
            rb_ready = nsem("rb_ready")
            scaled = nsem("scaled")
            t_ready = nsem("t_ready")
            t_counted = nsem("t_counted")
            norm_chain = nsem("norm_chain")
            norm_std = nsem("norm_std")
            t2_ready = nsem("t2_ready")
            relu_chain = nsem("relu_chain")
            mid_ready = nsem("mid_ready")
            part_chain = nsem("part_chain")
            sum_chain = nsem("sum_chain")
            wgt_ready = nsem("wgt_ready")
            mul_done = nsem("mul_done")
            pair_chain = nsem("pair_chain")
            acc_ready = nsem("acc_ready")
            x1_ready = nsem("x1_ready")
            ld_res = [nsem(f"ld_res{u}") for u in range(2)]
            st_x1 = [nsem(f"st_x1{u}") for u in range(2)]
            st_xT = [nsem(f"st_xT{u}") for u in range(2)]
            xT_ready = nsem("xT_ready")
            raw_ready = nsem("raw_ready")
            raw_kept = nsem("raw_kept")
            xT_kept = nsem("xT_kept")
            var4_ready = nsem("var4_ready")
            var4_kept = nsem("var4_kept")
            std2_ready = nsem("std2_ready")
            turned2 = nsem("turned2")
            rb2_ready = nsem("rb2_ready")
            normed = nsem("normed")
            pick_chain = nsem("pick_chain")
            mv_cand = [nsem(f"mv_cand{k}") for k in range(2)]
            mv_list = [nsem(f"mv_list{k}") for k in range(2)]
            mv_sum = nsem("mv_sum")
            exp_all = nsem("exp_all")
            st_S = [nsem(f"st_S{k}") for k in range(2)]
            ld_rows = [nsem(f"ld_rows{k}") for k in range(K0)]
            pool_turned = nsem("pool_turned")
            pool_kept = nsem("pool_kept")
            border = nsem("border")

            SPLITS = 6
            NORMS = 5
            PICKS = 34
            half_tiles = TILES // 2

            def pick(b, n):
                return b * PICKS + (n + 1)

            def tile_of(ap, b, j):
                return ap[bass.ds(b, 1), :, bass.ds(j * ROWS, ROWS), :].rearrange("a c h w -> (a c) h w")

            def inner(j):
                return xn[:, bass.ds(j * ROWS + PAD, ROWS), PAD:PAD + W]

            def grid(ap):
                return ap.rearrange("p (h w) -> p h w", h=ROWS)

            with nc.Block() as block:
                @block.sync
                def _(sp):
                    for s in (*st_x1, *st_xT, *st_S):
                        sp.sem_inc(s, 16)

                    def store_r(base, views):
                        for k in range(3):
                            sp.wait_ge(split_chain, base + (3, 5, 6)[k])
                            sp.dma_start(views[k], r_part[k][:]).then_inc(st_r[k], 16)

                    with sp.Fori(0, B) as b:
                        with sp.Fori(0, half_tiles) as i:
                            for u in range(2):
                                n = b * TILES + i * 2 + u
                                sp.wait_ge(centred, done(n - 2))
                                sp.dma_start(grid(x_in[u][:]), tile_of(x, b, i * 2 + u)).then_inc(ld_x[u], 16)
                        store_r(b * 2 * SPLITS, [rA_dram[k].rearrange("(h w) -> h w", w=W) for k in range(3)])
                        for k in range(3):
                            sp.wait_ge(st_r[k], b * 32 + 16)
                        settle(sp, passed)
                        with sp.Fori(0, half_tiles) as i:
                            for u in range(2):
                                n = b * TILES + i * 2 + u
                                sp.wait_ge(rb_ready, done(n - 2))
                                sp.dma_start(rA[u][:], rA_dram[:, bass.ds((i * 2 + u) * TILE, TILE)])\
                                  .then_inc(ld_rA[u], 16)

                        sp.wait_ge(pick_chain, pick(b, 0))
                        settle(sp, passed)

                        def step(i, u, part):
                            j, p, half = item(i, u, 0)
                            if live(j, TILES):
                                sp.wait_ge(x1_ready, done(b * TILES + j - 2))
                                sp.dma_start(grid(x_res[p][:]), tile_of(x, b, j)).then_inc(ld_res[p], 16)
                            j, p, half = item(i, u, 3)
                            if live(j, TILES):
                                n = b * TILES + j
                                sp.wait_ge(x1_ready, done(n))
                                sp.dma_start(tile_of(x1_dram, b, j), grid(x1[p][:])).then_inc(st_x1[p], 16)
                                sp.wait_ge(xT_kept, done(n))
                                sp.dma_start(
                                    xT_dram[bass.ds(j * TILE, TILE), :].rearrange("(q p) c -> p q c", p=128),
                                    x1T[p][:]).then_inc(st_xT[p], 16)

                        walk(sp, passed, step, TILES, 3, parts=2)
                        store_r((b * 2 + 1) * SPLITS,
                                [rB_dram[k].rearrange("s t -> (s t)").rearrange("(h w) -> h w", w=W)
                                 for k in range(3)])
                        for k in range(3):
                            sp.wait_ge(st_r[k], b * 32 + 32)
                        settle(sp, passed)
                        with sp.Fori(0, half_tiles // 2) as i:
                            for u in range(2):
                                n = b * half_tiles + i * 2 + u
                                sp.wait_ge(rb2_ready, done(n - 2))
                                for h in range(2):
                                    sp.dma_start(rB[u][3 * h:3 * h + 3, :],
                                                 rB_dram[:, h, bass.ds((i * 2 + u) * TILE, TILE)])\
                                      .then_inc(ld_rB[u][h], 16)
                        sp.wait_ge(pick_chain, pick(b, 3))
                        sp.dma_start(cand[:, 8:16], top_half[64:128, :]).then_inc(mv_cand[0], 16)
                        sp.dma_start(cand_idx[:, 8:16], idxf_half[64:128, :]).then_inc(mv_cand[1], 16)
                        sp.wait_ge(pick_chain, pick(b, 15))
                        sp.dma_start(find[64:128, 0:8], lists[:, 8:16]).then_inc(mv_list[0], 16)
                        sp.dma_start(find[64:128, 8:9], lists[:, 16:17]).then_inc(mv_list[1], 16)
                        sp.wait_ge(exp_all, b * 3 + 1)
                        sp.dma_start(zsum2[:], zsum[64:128, :]).then_inc(mv_sum, 16)
                        sp.wait_ge(pick_chain, pick(b, 26))
                        for h in range(2):
                            sp.dma_start(
                                S_dram[bass.ds(b, 1), :, h * HALF:(h + 1) * HALF].rearrange("a e t -> (a e) t"),
                                logits[64 * h:64 * h + 64, 0:HALF]).then_inc(st_S[h], 16)
                    for s, n in ((st_x1, B * half_tiles), (st_xT, B * half_tiles), (st_S, B)):
                        for q in s:
                            sp.wait_ge(q, rounds(n))
                    for q in st_r:
                        sp.wait_ge(q, 32 * B)

                @block.tensor
                def _(pe):
                    t = nc.tensor
                    credit(pe, centred, varied, rb_ready, t_ready, t2_ready, wgt_ready, acc_ready, xT_ready,
                           raw_ready, rb2_ready)
                    with pe.Fori(0, B) as b:
                        with pe.Fori(0, half_tiles) as i:
                            for u in range(2):
                                n = b * TILES + i * 2 + u
                                pe.wait_ge(ld_x[u], (b * half_tiles + i + 1) * 16)
                                pe.wait_ge(squared, done(n - 2))
                                t.matmul(centre_ps[u][:], center[:], x_in[u][:], start=True, stop=True)\
                                 .then_inc(centred, 1)
                            for u in range(2):
                                n = b * TILES + i * 2 + u
                                pe.wait_ge(squared, done(n))
                                pe.wait_ge(var_kept, done(n - 2))
                                for q in range(ROWS):
                                    mm = t.matmul(var_ps[u][:, q:q + 1], square[u][:, q * 128:q * 128 + 128],
                                                  mean_col[:], start=True, stop=True)
                                mm.then_inc(varied, 1)
                        pe.wait_ge(split_chain, b * 2 * SPLITS + 1)
                        t.transpose(turn_ps, rstd[:], ident[:]).then_inc(turned, 1)
                        settle(pe, passed)
                        with pe.Fori(0, half_tiles) as i:
                            for u in range(2):
                                n = b * TILES + i * 2 + u
                                pe.wait_ge(ld_rA[u], (b * half_tiles + i + 1) * 16)
                                pe.wait_ge(scaled, done(n - 2))
                                t.matmul(rb_ps[u][:], ones3[:], rA[u][:], start=True, stop=True)\
                                 .then_inc(rb_ready, 1)
                            for u in range(2):
                                n = b * TILES + i * 2 + u
                                pe.wait_ge(scaled, done(n))
                                pe.wait_ge(t_counted, done(n - 2))
                                t.matmul(bank[2 + u][:], w1rep[:], inner(i * 2 + u), start=True, stop=True)\
                                 .then_inc(t_ready, 1)
                        pe.wait_ge(t_counted, done(b * TILES + TILES - 1))

                        def step(i, u, part):
                            j, p, half = item(i, u, 0)
                            if live(j, TILES):
                                n = b * TILES + j
                                pe.wait_ge(relu_chain, n * 3 - 3 + 3 + CREDIT)
                                t.matmul(t_ps[:], w1rep[:], inner(j), start=True, stop=True).then_inc(t2_ready, 1)
                            j, p, half = item(i, u, 1)
                            if live(j, TILES):
                                n = b * TILES + j
                                pe.wait_ge(part_chain, n * 2 + 2 + CREDIT * 2)
                                for k in range(TAPS):
                                    pe.wait_ge(mul_done, done(n * TAPS + k - 3))
                                    t.matmul(wgt_ps[k % 3][:], wstack[:, k, :], stack[p][:], start=True, stop=True)\
                                     .then_inc(wgt_ready, 1)
                            j, p, half = item(i, u, 2)
                            if live(j, TILES):
                                n = b * TILES + j
                                pe.wait_ge(sum_chain, n * 3 + 3 + CREDIT * 3)
                                pe.wait_ge(pair_chain, n * 2 + 2 + CREDIT * 2)
                                pe.wait_ge(x1_ready, done(n - 1))
                                for k in range(4):
                                    mm = t.matmul(acc_ps, ident[:], psum_in[k][p][:], start=(k == 0), stop=(k == 3))
                                mm.then_inc(acc_ready, 1)
                            j, p, half = item(i, u, 3)
                            if live(j, TILES):
                                n = b * TILES + j
                                pe.wait_ge(x1_ready, done(n))
                                pe.wait_ge(raw_kept, done(n - 1))
                                h = j // half_tiles if isinstance(j, int) else part
                                t.matmul(raw_ps[64 * h:64 * h + 64, :], gateT[:], x1[p][:], start=True, stop=True)\
                                 .then_inc(raw_ready, 1)
                                pe.wait_ge(var4_ready, done(n - 1))
                                for q in range(ROWS):
                                    mm = t.matmul(xT_ps[:, q * 128:q * 128 + 128], x1[p][:, q * 128:q * 128 + 128],
                                                  center[:], start=True, stop=True)
                                mm.then_inc(xT_ready, 1)

                        walk(pe, passed, step, TILES, 3, parts=2)
                        pe.wait_ge(split_chain, (b * 2 + 1) * SPLITS + 1)
                        t.transpose(turn_ps, rstd[:], ident[:]).then_inc(turned2, 1)
                        settle(pe, passed)
                        with pe.Fori(0, half_tiles // 2) as i:
                            for u in range(2):
                                n = b * half_tiles + i * 2 + u
                                for h in range(2):
                                    pe.wait_ge(ld_rB[u][h], (b * (half_tiles // 2) + i + 1) * 16)
                                pe.wait_ge(normed, done(n - 2))
                                t.matmul(rb_ps[u][:], sel6[:], rB[u][:], start=True, stop=True)\
                                 .then_inc(rb2_ready, 1)
                        pe.wait_ge(pick_chain, pick(b, PICKS))
                        settle(pe, passed)
                        t.transpose(pool_ps, pooled[:], ident[0:E0, 0:E0]).then_inc(pool_turned, 1)

                @block.scalar
                def _(act):
                    a = nc.scalar
                    credit(act, squared, raw_kept, xT_kept, var4_ready, mid_ready)
                    act.sem_inc(relu_chain, CREDIT)
                    with act.Fori(0, B) as b:
                        act.wait_ge(mul_done, done(b * TILES * TAPS - 1))
                        act.wait_ge(border, 2)
                        settle(act, passed)
                        with act.Fori(0, half_tiles) as i:
                            for u in range(2):
                                n = b * TILES + i * 2 + u
                                act.wait_ge(centred, done(n))
                                a.activation(inner(i * 2 + u), grid(centre_ps[u][:]), ACT.Copy)
                                act.wait_ge(varied, done(n - 2))
                                a.activation(square[u][:], centre_ps[u][:], ACT.Square).then_inc(squared, 1)
                        act.wait_ge(var_kept, done(b * TILES + TILES - 1))
                        a.activation(std[:], var_all[:], ACT.Sqrt, bias=eps6[:]).then_inc(std_ready, 1)
                        act.wait_ge(norm_chain, b * NORMS + 1)
                        a.activation(t_tmp[:, 0:1], t_mv[:, 1:2], ACT.Sqrt, bias=eps5[:]).then_inc(norm_std, 1)
                        act.wait_ge(norm_chain, b * NORMS + NORMS)
                        act.wait_ge(st_S[0], rounds(b))
                        act.wait_ge(st_S[1], rounds(b))

                        def step(i, u, part):
                            j, p, half = item(i, u, 0)
                            if live(j, TILES):
                                n = b * TILES + j
                                r0 = n * 3 + CREDIT
                                act.wait_ge(t2_ready, done(n))
                                act.wait_ge(wgt_ready, done(n * TAPS - TAPS - 1))
                                a.activation(stack[p][0:64, :], t_ps[0:64, :], ACT.Relu, scale=t_scale[0:64, :],
                                             bias=t_bias[0:64, :]).then_inc(relu_chain, 1)
                                a.activation(t_full[p][64:128, :], t_ps[64:128, :], ACT.Relu,
                                             scale=t_scale[64:128, :], bias=t_bias[64:128, :])\
                                 .then_inc(relu_chain, 1)
                                act.wait_ge(relu_chain, r0 + 2)
                                a.activation(t_high[p][64:128, :], t_full[p][64:128, :], ACT.Copy)\
                                 .then_inc(relu_chain, 1)
                            j3, p3, half3 = item(i, u, 3)
                            if live(j3, TILES):
                                n = b * TILES + j3
                                h = j3 // half_tiles if isinstance(j3, int) else part
                                act.wait_ge(raw_ready, done(n))
                                a.activation(
                                    logits[64 * h:64 * h + 64, bass.ds((j3 - h * half_tiles) * TILE, TILE)],
                                    raw_ps[64 * h:64 * h + 64, :], ACT.Copy).then_inc(raw_kept, 1)
                                act.wait_ge(xT_ready, done(n))
                                act.wait_ge(st_xT[p3], rounds(b * half_tiles + half3))
                                a.activation(x1T[p3][:], xT_ps.rearrange("p (q c) -> p q c", q=ROWS), ACT.Copy)\
                                 .then_inc(xT_kept, 1)
                                act.wait_ge(var4_kept, done(n - 2))
                                for q in range(ROWS):
                                    ins = a.activation(sq_junk[:, q, :], xT_ps[:, q * 128:q * 128 + 128], ACT.Square,
                                                       accum_out=var4[p3][:, q:q + 1])
                                ins.then_inc(var4_ready, 1)
                            j, p, half = item(i, u, 0)
                            if live(j, TILES):
                                n = b * TILES + j
                                act.wait_ge(part_chain, n * 2 + 1 + CREDIT * 2)
                                a.activation(stack[p][64:128, :], t_rest[p][64:128, :], ACT.Copy)\
                                 .then_inc(mid_ready, 1)

                        walk(act, passed, step, TILES, 3, parts=2)
                        act.wait_ge(var4_kept, done(b * TILES + TILES - 1))
                        a.activation(std[:], var_all[:], ACT.Sqrt, bias=eps5[:], scale=1.0 / C)\
                         .then_inc(std2_ready, 1)
                        act.wait_ge(pick_chain, pick(b, 18))
                        a.activation(logits[:, 0:HALF], logits[:, 0:HALF], ACT.Exp, bias=find[:, 8:9],
                                     accum_out=zsum[:]).then_inc(exp_all, 1)
                        a.activation(top_exp[:], top[:], ACT.Exp, bias=find[0:E0, 8:9]).then_inc(exp_all, 1)
                        act.wait_ge(pick_chain, pick(b, 28))
                        a.activation(row_std[:], row_var[:], ACT.Sqrt, bias=eps5[0:E0, :], scale=1.0 / C)\
                         .then_inc(exp_all, 1)

                @block.gpsimd
                def _(pool):
                    g = nc.gpsimd
                    pool.sem_inc(part_chain, CREDIT * 2)
                    pool.sem_inc(sum_chain, CREDIT * 3)
                    with pool.Fori(0, B) as b:
                        def step(i, u, part):
                            j, p, half = item(i, u, 0)
                            if live(j, TILES):
                                n = b * TILES + j
                                pool.wait_ge(relu_chain, n * 3 + 3 + CREDIT)
                                g.tensor_tensor(t_rest[p][64:128, :], t_full[p][64:128, :], t_high[p][64:128, :],
                                                ALU.subtract).then_inc(part_chain, 1)
                                pool.wait_ge(mid_ready, done(n))
                                g.tensor_tensor(stack[p][96:128, :], t_rest[p][96:128, :], stack[p][96:128, :],
                                                ALU.subtract).then_inc(part_chain, 1)
                                pool.wait_ge(part_chain, n * 2 + 2 + CREDIT * 2)
                            j, p, half = item(i, u, 1)
                            if live(j, TILES):
                                n = b * TILES + j
                                pool.wait_ge(acc_ready, done(n - 2))
                                for k in range(3):
                                    pool.wait_ge(mul_done, done(n * TAPS + 2 * k + 1))
                                    g.tensor_tensor(psum_in[k][p][:], prod[2 * k], prod[2 * k + 1], ALU.add)\
                                     .then_inc(sum_chain, 1)
                                pool.wait_ge(sum_chain, n * 3 + 3 + CREDIT * 3)

                        walk(pool, passed, step, TILES, 1)
                        for u in range(2):
                            pool.wait_ge(st_xT[u], rounds((b + 1) * half_tiles))
                        pool.wait_ge(pick_chain, pick(b, 23))
                        settle(pool, passed)
                        for k in range(K0):
                            g.indirect_dma_start(rows[:, k, :], None, xT_dram[:, :],
                                                 bass.IndirectOffsetOnAxis(ap=token[:, k:k + 1], axis=0))\
                             .then_inc(ld_rows[k], 16)

                @block.vector
                def _(dve):
                    v = nc.vector
                    credit(dve, var_kept, scaled, t_counted, mul_done, x1_ready, var4_kept, normed)
                    dve.sem_inc(pair_chain, CREDIT * 2)
                    dve.sem_inc(pick_chain, 1)
                    v.memset(xn[:], 0.0).then_inc(border, 1)
                    v.memset(logits[:, HALF:HALF + 8], NEG).then_inc(border, 1)

                    def split_r(link, turned_sem, b):
                        link(v.reciprocal(rstd[:], std[:]))
                        dve.wait_ge(turned_sem, b + 1)
                        link(v.tensor_copy(r_rest[:], turn_ps))
                        link(v.tensor_copy(r_part[0][:], r_rest[:]))
                        link(v.tensor_tensor(r_rest[:], r_rest[:], r_part[0][:], ALU.subtract))
                        link(v.tensor_copy(r_part[1][:], r_rest[:]))
                        link(v.tensor_tensor(r_part[2][:], r_rest[:], r_part[1][:], ALU.subtract))
                        assert link.n == SPLITS

                    with dve.Fori(0, B) as b:
                        with dve.Fori(0, half_tiles) as i:
                            for u in range(2):
                                dve.wait_ge(varied, done(b * TILES + i * 2 + u))
                                v.tensor_copy(var_all[:, bass.ds((i * 2 + u) * ROWS, ROWS)], var_ps[u])\
                                 .then_inc(var_kept, 1)
                        dve.wait_ge(std_ready, b + 1)
                        split_r(Chain(dve, split_chain, b * 2 * SPLITS), turned, b)
                        settle(dve, passed)
                        with dve.Fori(0, half_tiles) as i:
                            for u in range(2):
                                n = b * TILES + i * 2 + u
                                dve.wait_ge(rb_ready, done(n))
                                v.tensor_tensor(inner(i * 2 + u), inner(i * 2 + u), grid(rb_ps[u][:]), ALU.mult)\
                                 .then_inc(scaled, 1)
                            for u in range(2):
                                n = b * TILES + i * 2 + u
                                dve.wait_ge(t_ready, done(n))
                                v.bn_stats(t_stats[:, bass.ds((i * 2 + u) * 6, 6)], bank[2 + u][:])\
                                 .then_inc(t_counted, 1)
                        dve.wait_ge(t_counted, done(b * TILES + TILES - 1))
                        dve.wait_ge(border, 2)
                        link = Chain(dve, norm_chain, b * NORMS)
                        settle(dve, passed)
                        link(v.bn_aggr(t_mv[:], t_stats[:]))
                        dve.wait_ge(norm_std, b + 1)
                        link(v.reciprocal(t_tmp[:, 1:2], t_tmp[:, 0:1]))
                        link(v.tensor_tensor(t_scale[:], t_tmp[:, 1:2], gamma_rep[:], ALU.mult))
                        link(v.tensor_tensor(t_tmp[:, 1:2], t_mv[:, 0:1], t_scale[:], ALU.mult))
                        link(v.tensor_tensor(t_bias[:], beta_rep[:], t_tmp[:, 1:2], ALU.subtract))
                        assert link.n == NORMS

                        def step(i, u, part):
                            j, p, half = item(i, u, 1)
                            if live(j, TILES):
                                n = b * TILES + j
                                for k in range(TAPS):
                                    dve.wait_ge(wgt_ready, done(n * TAPS + k))
                                    if k < 6:
                                        dve.wait_ge(sum_chain, n * 3 - 2 + k // 2 + CREDIT * 3)
                                    elif k == 6:
                                        dve.wait_ge(pair_chain, n * 2 + CREDIT * 2)
                                    v.tensor_tensor(
                                        grid(prod[k]), grid(wgt_ps[k % 3][:]),
                                        xn[:, bass.ds(j * ROWS + 2 * (k // 3), ROWS), 2 * (k % 3):2 * (k % 3) + W],
                                        ALU.mult).then_inc(mul_done, 1)
                                dve.wait_ge(mul_done, done(n * TAPS + 7))
                                v.tensor_tensor(prod[6], prod[6], prod[7], ALU.add).then_inc(pair_chain, 1)
                                dve.wait_ge(pair_chain, n * 2 + 1 + CREDIT * 2)
                                dve.wait_ge(mul_done, done(n * TAPS + 8))
                                dve.wait_ge(acc_ready, done(n - 2))
                                v.tensor_tensor(psum_in[3][p][:], prod[6], prod[8], ALU.add)\
                                 .then_inc(pair_chain, 1)
                            j, p, half = item(i, u, 2)
                            if live(j, TILES):
                                n = b * TILES + j
                                dve.wait_ge(acc_ready, done(n))
                                dve.wait_ge(ld_res[p], (b * half_tiles + half + 1) * 16)
                                dve.wait_ge(st_x1[p], rounds(b * half_tiles + half))
                                dve.wait_ge(xT_ready, done(n - 2))
                                v.tensor_tensor(x1[p][:], acc_ps, x_res[p][:], ALU.add).then_inc(x1_ready, 1)
                            j, p, half = item(i, u, 3)
                            if live(j, TILES):
                                n = b * TILES + j
                                dve.wait_ge(var4_ready, done(n))
                                v.tensor_copy(var_all[:, bass.ds(j * ROWS, ROWS)], var4[p][:]).then_inc(var4_kept, 1)

                        walk(dve, passed, step, TILES, 3, parts=2)
                        dve.wait_ge(std2_ready, b + 1)
                        split_r(Chain(dve, split_chain, (b * 2 + 1) * SPLITS), turned2, b)
                        dve.wait_ge(raw_kept, done(b * TILES + TILES - 1))
                        settle(dve, passed)
                        with dve.Fori(0, half_tiles // 2) as i:
                            for u in range(2):
                                at = bass.ds((i * 2 + u) * TILE, TILE)
                                dve.wait_ge(rb2_ready, done(b * half_tiles + i * 2 + u))
                                v.tensor_tensor(logits[:, at], logits[:, at], rb_ps[u][:], ALU.mult)\
                                 .then_inc(normed, 1)
                        dve.wait_ge(normed, done(b * half_tiles + half_tiles - 1))
                        link = Chain(dve, pick_chain, pick(b, 0))
                        dve.wait_ge(border, 2)
                        settle(dve, passed)
                        link(v.max(top_half[:], logits[:]))
                        settle(dve, passed)
                        link(v.max_index(idx_half[:], top_half[:], logits[:]))
                        link(v.tensor_copy(idxf_half[:], idx_half[:]))
                        link(v.tensor_copy(cand[:, 0:8], top_half[0:64, :]))
                        link(v.tensor_copy(cand_idx[:, 0:8], idxf_half[0:64, :]))
                        dve.wait_ge(mv_cand[0], b * 16 + 16)
                        dve.wait_ge(mv_cand[1], b * 16 + 16)
                        link(v.tensor_scalar(cand_idx[:, 8:16], cand_idx[:, 8:16], float(HALF), None, ALU.add))
                        settle(dve, passed)
                        link(v.max(top[:], cand[:]))
                        settle(dve, passed)
                        link(v.max_index(pos[:], top[:], cand[:]))
                        settle(dve, passed)
                        link(v.match_replace(cand_mark[:], top[:], cand[:], BIG))
                        link(v.tensor_scalar(kept[:], cand_mark[:], BIG, None, ALU.is_equal))
                        link(v.tensor_tensor(kept2[:], kept[:], cand[:], ALU.mult))
                        link(v.tensor_scalar(kept[:], kept[:], -1.0, -NEG, ALU.add, ALU.mult))
                        link(v.tensor_tensor(lists[:, 0:16], kept2[:], kept[:], ALU.add))
                        link(v.tensor_tensor(zinv[:], top[:, 0:1], gate_bias[:], ALU.add))
                        link(v.tensor_tensor(lists[:, 16:17], gate_bias[:], zinv[:], ALU.subtract))
                        link(v.tensor_copy(find[0:E0, 0:8], lists[:, 0:8]))
                        link(v.tensor_copy(find[0:E0, 8:9], lists[:, 16:17]))
                        dve.wait_ge(mv_list[0], b * 16 + 16)
                        dve.wait_ge(mv_list[1], b * 16 + 16)
                        settle(dve, passed)
                        link(v.match_replace(picked[:], find[:, 0:8], logits[:], BIG))
                        link(v.tensor_copy(posf[:], pos[:]))
                        link(v.tensor_tensor(token_eq[:], slots16[:].unsqueeze(1).to_broadcast([E0, K0, 16]),
                                             posf[:].unsqueeze(2).to_broadcast([E0, K0, 16]), ALU.is_equal))
                        link(v.tensor_tensor(token_eq[:], token_eq[:],
                                             cand_idx[:].unsqueeze(1).to_broadcast([E0, K0, 16]), ALU.mult))
                        link(v.tensor_reduce(token_f[:], token_eq[:], AX_X, ALU.add))
                        link(v.tensor_copy(token[:], token_f[:]))
                        dve.wait_ge(mv_sum, b * 16 + 16)
                        dve.wait_ge(exp_all, b * 3 + 2)
                        link(v.tensor_tensor(zinv[:], zsum[0:E0, :], zsum2[:], ALU.add))
                        link(v.reciprocal(rsum_b[:], zinv[:]))
                        link(v.scalar_tensor_tensor(out=logits[:, 0:HALF], in0=picked[:, 0:HALF], scalar=BIG,
                                                    in1=logits[:, 0:HALF], op0=ALU.is_equal, op1=ALU.mult))
                        for k in range(K0 - 1):
                            dve.wait_ge(ld_rows[k], b * 16 + 16)
                        dve.wait_ge(ld_rows[K0 - 1], b * 16 + 16)
                        link(v.tensor_tensor(rows_sq, rows, rows, ALU.mult))
                        link(v.tensor_reduce(row_var[:], rows_sq, AX_X, ALU.add))
                        dve.wait_ge(exp_all, b * 3 + 3)
                        link(v.reciprocal(row_w[:], row_std[:]))
                        link(v.tensor_tensor(row_w[:], row_w[:], top_exp[:], ALU.mult))
                        link(v.tensor_scalar(row_w[:], row_w[:], rsum_b[:], None, ALU.mult))
                        link(v.tensor_copy(rsum_all[:, bass.ds(b, 1)], rsum_b[:]))
                        link(v.tensor_tensor(rows, rows, row_w[:].unsqueeze(2).to_broadcast([E0, K0, C]),
                                             ALU.mult))
                        link(v.tensor_reduce(pooled[:], rows.rearrange("e k c -> e c k"), AX_X, ALU.add))
                        assert link.n == PICKS
                        dve.wait_ge(pool_turned, b + 1)
                        v.tensor_copy(pooledT[:, bass.ds(b, 1), :], pool_ps.unsqueeze(1)).then_inc(pool_kept, 1)
                        dve.wait_ge(pool_kept, b + 1)
        with ExitStack() as tmp:
            def tb(name, shape, dt=F32):
                return tmp.enter_context(nc.sbuf_tensor(name, shape, dt))

            def pair(name, shape, dt=F32):
                return [tb(f"{name}{u}", shape, dt) for u in range(2)]

            def nsem(name):
                return tmp.enter_context(nc.semaphore(name))

            HC = HID // 128
            first_w = [tb(f"first_w{u}", [128, HID]) for u in range(4)]
            second_w = [tb(f"second_w{u}", [128, HC, C]) for u in range(4)]
            first_b = tb("first_b", [E0, HID])
            second_b = tb("second_b", [E0, C])
            first_bT = tb("first_bT", [128, E0, HC])
            second_bT = tb("second_bT", [128, E0])
            hid = pair("hid", [128, HC, B])
            act_hid = pair("act_hid", [128, HC, B])
            ld_b = nsem("ld_b")
            ld_w = [[nsem(f"ld_w{u}{k}") for k in range(2)] for u in range(4)]
            bias_turned = nsem("bias_turned")
            bias_kept = nsem("bias_kept")
            hid_ready = nsem("hid_ready")
            hid_biased = nsem("hid_biased")
            hid_act = nsem("hid_act")
            moe_ready = nsem("moe_ready")
            moe_kept = nsem("moe_kept")
            hid_ps = [bank[u][:, 0:HC * B].rearrange("p (c b) -> p c b", b=B) for u in range(2)]
            moe_ps = [bank[2 + u][:, 0:B] for u in range(2)]

            with nc.Block() as block:
                @block.sync
                def _(sp):
                    sp.dma_start(first_b[:], ew1[:, C, :]).then_inc(ld_b, 16)
                    sp.dma_start(second_b[:], ew2[:, HID, :]).then_inc(ld_b, 16)
                    with sp.Fori(0, E0 // 4) as i:
                        for u in range(4):
                            sp.wait_ge(moe_ready, done(i * 4 + u - 4))
                            sp.dma_start(first_w[u][:], ew1[bass.ds(i * 4 + u, 1), 0:C, :]
                                         .rearrange("a d h -> (a d) h")).then_inc(ld_w[u][0], 16)
                            sp.dma_start(second_w[u][:], ew2[bass.ds(i * 4 + u, 1), 0:HID, :]
                                         .rearrange("a (p c) o -> (a p) c o", c=HC)).then_inc(ld_w[u][1], 16)

                @block.tensor
                def _(pe):
                    t = nc.tensor
                    credit(pe, hid_ready, moe_ready)
                    pe.wait_ge(ld_b, 32)
                    for c in range(HC):
                        if c >= 2:
                            pe.wait_ge(bias_kept, c - 1)
                        t.transpose(bank[c % 2][:, 0:E0], first_b[:, c:HID:HC], ident[0:E0, 0:E0])\
                         .then_inc(bias_turned, 1)
                    pe.wait_ge(bias_kept, HC - 1)
                    t.transpose(bank[0][:, 0:E0], second_b[:], ident[0:E0, 0:E0]).then_inc(bias_turned, 1)
                    pe.wait_ge(bias_kept, HC + 1)

                    def four(i):
                        for u in range(4):
                            for lag, n in ((0, i * 4 + u), (1, i * 4 + u - 1)):
                                if not live(n, E0):
                                    continue
                                w, p = (u - lag) % 4, (u - lag) % 2
                                if lag == 0:
                                    for k in range(2):
                                        pe.wait_ge(ld_w[w][k], (i + 1) * 16)
                                    pe.wait_ge(hid_biased, done(n - 2))
                                    for c in range(HC):
                                        mm = t.matmul(hid_ps[p][:, c, :], first_w[w][:, c:HID:HC],
                                                      pooledT[:, :, bass.ds(n, 1)].rearrange("p b a -> p (b a)"),
                                                      start=True, stop=True)
                                    mm.then_inc(hid_ready, 1)
                                else:
                                    pe.wait_ge(hid_act, done(n))
                                    pe.wait_ge(moe_kept, done(n - 2))
                                    for c in range(HC):
                                        mm = t.matmul(moe_ps[p], second_w[w][:, c, :], act_hid[p][:, c, :],
                                                      start=(c == 0), stop=(c == HC - 1))
                                    mm.then_inc(moe_ready, 1)

                    four(0)
                    with pe.Fori(1, E0 // 4) as i:
                        four(i)
                    pe.wait_ge(hid_act, done(E0 - 1))
                    pe.wait_ge(moe_kept, done(E0 - 3))
                    for c in range(HC):
                        mm = t.matmul(moe_ps[1], second_w[3][:, c, :], act_hid[1][:, c, :],
                                      start=(c == 0), stop=(c == HC - 1))
                    mm.then_inc(moe_ready, 1)

                @block.scalar
                def _(act):
                    credit(act, hid_act)
                    with act.Fori(0, E0 // 2) as i:
                        for u in range(2):
                            n = i * 2 + u
                            act.wait_ge(hid_biased, done(n))
                            act.wait_ge(moe_ready, done(n - 2))
                            nc.scalar.activation(act_hid[u][:], hid[u][:], ACT.Gelu).then_inc(hid_act, 1)

                @block.vector
                def _(dve):
                    v = nc.vector
                    credit(dve, hid_biased, moe_kept)
                    for c in range(HC):
                        dve.wait_ge(bias_turned, c + 1)
                        v.tensor_copy(first_bT[:, :, c:c + 1], bank[c % 2][:, 0:E0].unsqueeze(2)).then_inc(bias_kept, 1)
                    dve.wait_ge(bias_turned, HC + 1)
                    v.tensor_copy(second_bT[:], bank[0][:, 0:E0]).then_inc(bias_kept, 1)
                    dve.wait_ge(bias_kept, HC + 1)

                    def step(i, u, part):
                        j, p, half = item(i, u, 0)
                        if live(j, E0):
                            dve.wait_ge(hid_ready, done(j))
                            dve.wait_ge(hid_act, done(j - 2))
                            v.tensor_tensor(hid[p][:], hid_ps[p],
                                            first_bT[:, bass.ds(j, 1), :].rearrange("p a c -> p (a c)")
                                            .unsqueeze(2).to_broadcast([128, HC, B]), ALU.add)\
                             .then_inc(hid_biased, 1)
                        j, p, half = item(i, u, 1)
                        if live(j, E0):
                            dve.wait_ge(moe_ready, done(j))
                            v.tensor_tensor(moeT[:, bass.ds(j, 1), :].rearrange("p a b -> p (a b)"), moe_ps[p],
                                            second_bT[:, bass.ds(j, 1)].to_broadcast([128, B]), ALU.add)\
                             .then_inc(moe_kept, 1)

                    walk(dve, passed, step, E0, 1)
                    dve.wait_ge(moe_kept, done(E0 - 1))
        with ExitStack() as tmp:
            def tb(name, shape, dt=F32):
                return tmp.enter_context(nc.sbuf_tensor(name, shape, dt))

            def pair(name, shape, dt=F32):
                return [tb(f"{name}{u}", shape, dt) for u in range(2)]

            def nsem(name):
                return tmp.enter_context(nc.semaphore(name))

            experts = tb("experts", [128, E1, 128])
            img = tb("img", [128, H, C])
            moe_b = tb("moe_b", [128, E0])
            moe_w = tb("moe_w", [E0, C])
            rs_b = tb("rs_b", [E0, 1])
            x1_in = pair("x1_in", [128, TILE])
            S_in = pair("S_in", [E0, TILE])
            x2 = pair("x2", [128, TILE])
            stat4 = pair("stat4", [128, ROWS, 6])
            mv4 = pair("mv4", [128, ROWS, 2])
            mv_all = tb("mv_all", [128, H, 2])
            std_all = tb("std_all", [128, H])
            rstd_all = tb("rstd_all", [128, H])
            bias_g = pair("bias_g", [128, GC])
            brem_g = pair("brem_g", [RP, 1])
            grp = pair("grp", [128, GC, H])
            upc = pair("upc", [128, GC, UPN])
            act_in = pair("act_in", [128, GC, 2, UPN])
            upc_rem = pair("upc_rem", [128, RP])
            act_rem = pair("act_rem", [128, 2, RP])
            rem_in = pair("rem_in", [RP, UPN])
            rem_blk = pair("rem_blk", [RP, GC, REM])
            dnc = pair("dnc", [128, 2, GC, W])
            rem_dn = pair("rem_dn", [RP, W])
            xm = pair("xm", [128, ROWS, C])
            xh = pair("xh", [128, TILE])
            lg = pair("lg", [128, ROWS, E1])
            mx = tb("mx", [128, ROWS])
            prb = pair("prb", [128, ROWS, E1])
            pr2 = tb("pr2", [128, ROWS, E1])
            sm = tb("sm", [128, ROWS])
            eq = tb("eq", [128, ROWS, E1])
            first = tb("first", [128, ROWS, E1])
            second = tb("second", [128, ROWS, E1])
            p1 = tb("p1", [128, ROWS])
            p2 = tb("p2", [128, ROWS])
            gate = pair("gate", [128, ROWS, E1])
            gateTs = pair("gateTs", [ROWS * E1, 128])
            acc = pair("acc", [128, ROWS, C])
            ya = [t[:].rearrange("p q (a c) w -> p (q a) c w", a=2) for t in dnc]
            ys = pair("ys", [128, ROWS, C])
            res = pair("res", [128, TILE])

            blocks = TILES
            ht = TILES // 2
            moe_got = nsem("moe_got")
            moe_turned = nsem("moe_turned")
            moe_scaled = nsem("moe_scaled")
            ld_experts = nsem("ld_experts")
            ld_x1 = [nsem(f"ld_x1{u}") for u in range(2)]
            ld_S = [nsem(f"ld_S{u}") for u in range(2)]
            add_ready = nsem("add_ready")
            x2_ready = nsem("x2_ready")
            img_turned = nsem("img_turned")
            img_kept = nsem("img_kept")
            stat_chain = nsem("stat_chain")
            mv_std = nsem("mv_std")
            mv_rstd = nsem("mv_rstd")
            grp_chain = nsem("grp_chain")
            bias_got = nsem("bias_got")
            up1_ready = nsem("up1_ready")
            up1_kept = nsem("up1_kept")
            up2_ready = nsem("up2_ready")
            up2_kept = nsem("up2_kept")
            leaky = nsem("leaky")
            rem_ready = nsem("rem_ready")
            down_ready = nsem("down_ready")
            down_kept = nsem("down_kept")
            conv_added = nsem("conv_added")
            xm_chain = nsem("xm_chain")
            xm_turned = nsem("xm_turned")
            xh_ready = nsem("xh_ready")
            lg_ready = nsem("lg_ready")
            route = nsem("route")
            exp_ready = nsem("exp_ready")
            gate_turned = nsem("gate_turned")
            gate_kept = nsem("gate_kept")
            exp_out = nsem("exp_out")
            act_part = nsem("act_part")
            dve_part = nsem("dve_part")
            y_chain = nsem("y_chain")
            acc_done = nsem("acc_done")
            out_ready = nsem("out_ready")
            out_kept = nsem("out_kept")
            st_out = [nsem(f"st_out{u}") for u in range(2)]

            ROUTES = 22
            ROUTE0 = 2 * CREDIT
            add_ps = bank[0:2]
            turn_ps = bank[2:4]
            up1_ps = bank[0:2]
            up2_ps = duo
            down_ps = bank[2:4]
            xm_ps = bank[0]
            lg_ps = bank[1][:, 0:ROWS * E1].rearrange("p (q e) -> p q e", e=E1)
            gT_ps = bank[2][0:ROWS * E1, 0:128]
            out_ps = bank[3]
            exp_ps = duo

            def rows_of(j):
                return bass.ds(j * ROWS, ROWS)

            def chan(ap, c0, n):
                return ap[:, :, bass.ds(c0, n)].rearrange("p h c -> p c h")

            def groups_of(eng, up, down):
                up(0, 0)
                up(1, 1)
                down(0, 0)
                settle(eng, passed)
                with eng.Fori(1, GROUPS // 2) as i:
                    up(i * 2, 0)
                    down(i * 2 - 1, 1)
                    up(i * 2 + 1, 1)
                    down(i * 2, 0)
                down(GROUPS - 1, 1)

            with nc.Block() as block:
                @block.sync
                def _(sp):
                    for s in st_out:
                        sp.sem_inc(s, 16)
                    sp.dma_start(experts[:], expert_w.rearrange("e d c -> d e c")).then_inc(ld_experts, 16)
                    with sp.Fori(0, B) as b:
                        with sp.Fori(0, ht) as i:
                            for u in range(2):
                                j = i * 2 + u
                                n = b * TILES + j
                                sp.wait_ge(x2_ready, done(n - 2))
                                sp.dma_start(x1_in[u][:].rearrange("p (h w) -> p h w", w=W),
                                             x1_dram[bass.ds(b, 1), :, rows_of(j), :]
                                             .rearrange("a c h w -> (a c) h w")).then_inc(ld_x1[u], 16)
                                sp.wait_ge(add_ready, done(n - 2))
                                sp.dma_start(S_in[u][:],
                                             S_dram[bass.ds(b, 1), :, bass.ds(j * TILE, TILE)]
                                             .rearrange("a e t -> (a e) t")).then_inc(ld_S[u], 16)
                        settle(sp, passed)
                        with sp.Fori(0, ht) as i:
                            for u in range(2):
                                j = i * 2 + u
                                sp.wait_ge(out_kept, done(b * TILES + j))
                                sp.dma_start(out[bass.ds(b, 1), :, rows_of(j), :].rearrange("a c h w -> (a c) h w"),
                                             res[u][:].rearrange("p (h w) -> p h w", w=W)).then_inc(st_out[u], 16)
                    for s in st_out:
                        sp.wait_ge(s, rounds(B * ht))

                @block.tensor
                def _(pe):
                    t = nc.tensor
                    credit(pe, add_ready, img_turned, up1_ready, up2_ready, down_ready, xm_turned, lg_ready,
                           gate_turned, exp_out, out_ready)
                    pe.wait_ge(ld_experts, 16)
                    with pe.Fori(0, B) as b:
                        pe.wait_ge(moe_got, b * 2 + 2)
                        settle(pe, passed)
                        t.transpose(turn_ps[0][0:E0, 0:128], moe_b[:], ident[:]).then_inc(moe_turned, 1)
                        pe.wait_ge(moe_scaled, b + 1)
                        settle(pe, passed)
                        with pe.Fori(0, ht) as i:
                            for u in range(2):
                                n = b * TILES + i * 2 + u
                                pe.wait_ge(ld_S[u], (b * ht + i + 1) * 16)
                                pe.wait_ge(x2_ready, done(n - 2))
                                t.matmul(add_ps[u][:], moe_w[:], S_in[u][:], start=True, stop=True)\
                                 .then_inc(add_ready, 1)
                            for u in range(2):
                                n = b * TILES + i * 2 + u
                                pe.wait_ge(x2_ready, done(n))
                                pe.wait_ge(img_kept, done(n - 2))
                                for q in range(ROWS):
                                    mm = t.transpose(turn_ps[u][:, q * 128:q * 128 + 128],
                                                     x2[u][:, q * 128:q * 128 + 128], ident[:])
                                mm.then_inc(img_turned, 1)

                        def up(g, p):
                            G = b * GROUPS + g
                            pe.wait_ge(grp_chain, G * 2 + 2 + CREDIT * 2)
                            for c in range(GC + 1):
                                if c < GC:
                                    n = G * GC + c
                                    pe.wait_ge(up1_kept, done(n - 2))
                                    t.matmul(up1_ps[c % 2][:, 0:UPN], grp[p][:, c, :], up_mat[:],
                                             start=True, stop=True).then_inc(up1_ready, 1)
                                if c >= 1:
                                    second_up(G, p, c - 1)
                            second_up(G, p, GC)

                        def second_up(G, p, c):
                            n = G * (GC + 1) + c
                            bankp = (p + c) % 2
                            pe.wait_ge(up2_kept, done(n - 2))
                            if c < GC:
                                pe.wait_ge(up1_kept, done(G * GC + c))
                                for m in range(2):
                                    mm = t.matmul(up2_ps[bankp][:, m, 0:UPN], upc[p][:, c, m * 128:m * 128 + 128],
                                                  up_mat[:], start=True, stop=True)
                            else:
                                pe.wait_ge(rem_ready, G * 3 + 1 + CREDIT * 3)
                                mm = t.matmul(up2_ps[bankp][0:RP, 0, 0:UPN], upc_rem[p][:], up_mat[:],
                                              start=True, stop=True)
                            mm.then_inc(up2_ready, 1)

                        def down(g, p):
                            G = b * GROUPS + g
                            pe.wait_ge(leaky, done(G * (GC + 1) + GC))
                            for k in range(4):
                                m, h = k // 2, k % 2
                                n = G * 7 + k
                                ps = down_ps[(p + k) % 2]
                                drain(G, k)
                                for c in range(4):
                                    ch = 4 * h + c
                                    for q in range(2):
                                        t.matmul(ps[:, c * 128:c * 128 + 128], act_in[p][:, ch, q, m * 128:m * 128 + 128],
                                                 down_mat[:, q, :], start=(c == 0 and q == 0), stop=False,
                                                 skip_group_check=True)
                                mm = t.matmul(ps[:].rearrange("p (c w) -> p c w", w=W)[:, :, W - EDGE:W],
                                              rem_in[p][:, m * 128:m * 128 + 128], down_edge[:, 4 * h:4 * h + 4, :],
                                              start=False, stop=True, skip_group_check=True)
                                mm.then_inc(down_ready, 1)
                            pe.wait_ge(rem_ready, G * 3 + 3 + CREDIT * 3)
                            drain(G, 4)
                            ps = down_ps[p]
                            for q in range(2):
                                t.matmul(ps[0:RP, 0:W], act_rem[p][:, q, :], down_mat[:, q, :],
                                         start=(q == 0), stop=False, skip_group_check=True)
                            t.matmul(ps[0:RP, W - EDGE:W], rem_blk[p][:].rearrange("p c r -> p (c r)"), down_edge1[:],
                                     start=False, stop=True, skip_group_check=True).then_inc(down_ready, 1)
                            pe.wait_ge(down_kept, done(G * 5 + 4))
                            for h in range(2):
                                drain(G, 5 + h)
                                ps = down_ps[(p + 5 + h) % 2]
                                for c in range(4):
                                    for q in range(2):
                                        t.matmul(ps[:, c * 128:c * 128 + 128], dnc[p][:, q, 4 * h + c, :],
                                                 down_mat[:, q, :], start=(c == 0 and q == 0), stop=False,
                                                 skip_group_check=True)
                                t.matmul(ps[:].rearrange("p (c w) -> p c w", w=W)[:, :, W - EDGE:W],
                                         rem_dn[p][:], down_edge[:, 4 * h:4 * h + 4, :], start=False, stop=True,
                                         skip_group_check=True).then_inc(down_ready, 1)

                        def drain(G, k):
                            if k < 2:
                                pe.wait_ge(conv_added, done(G * 2 - 2 + k))
                            else:
                                pe.wait_ge(down_kept, done(G * 5 + k - 2))

                        groups_of(pe, up, down)

                        def step(i, u, part):
                            j, p, half = item(i, u, 0)
                            if live(j, blocks):
                                n = b * blocks + j
                                pe.wait_ge(xm_chain, n * 2 + 2 + CREDIT * 2)
                                pe.wait_ge(xh_ready, done(n - 1))
                                for q in range(ROWS):
                                    mm = t.transpose(xm_ps[:, q * 128:q * 128 + 128], xm[p][:, q, :], ident[:])
                                mm.then_inc(xm_turned, 1)
                            j1, p1_, half1 = item(i, u, 1)
                            if live(j1, blocks):
                                n1 = b * blocks + j1
                                pe.wait_ge(route, n1 * ROUTES + ROUTES + ROUTE0)
                                pe.wait_ge(gate_kept, done(n1 - 1))
                                t.transpose(gT_ps, gate[p1_][:].rearrange("p q e -> p (q e)"), ident[:])\
                                 .then_inc(gate_turned, 1)
                                for q in range(2):
                                    expert_row(n1, p1_, q)
                            if live(j, blocks):
                                pe.wait_ge(xh_ready, done(n))
                                pe.wait_ge(route, n * ROUTES - ROUTES + 1 + ROUTE0)
                                for q in range(ROWS):
                                    mm = t.matmul(lg_ps[:, q, :], xh[p][:, q * 128:q * 128 + 128], router[:],
                                                  start=True, stop=True)
                                mm.then_inc(lg_ready, 1)
                            if live(j1, blocks):
                                for q in range(2, 4):
                                    expert_row(n1, p1_, q)
                            j, p, half = item(i, u, 2)
                            if live(j, blocks):
                                n = b * blocks + j
                                pe.wait_ge(acc_done, done(n))
                                pe.wait_ge(gate_kept, done(n))
                                pe.wait_ge(out_kept, done(n - 1))
                                for q in range(ROWS):
                                    at = slice(q * 128, q * 128 + 128)
                                    t.matmul(out_ps[:, at], acc[p][:, q, :], ident[:], start=True, stop=False)
                                    mm = t.matmul(out_ps[:, at], ebias[:, q, :], gateTs[p][:], start=False, stop=True)
                                mm.then_inc(out_ready, 1)

                        def expert_row(n, p, q):
                            r = n * ROWS + q
                            pe.wait_ge(dve_part, (r - q % 2 - 2 + CREDIT) * DVE_EXPERTS + 2 * DVE_EXPERTS - 1 + q % 2)
                            for h in range(2):
                                if h:
                                    pe.wait_ge(act_part, done(r - 2))
                                mm = t.matmul(exp_ps[q % 2][:, h, :], xh[p][:, q * 128:q * 128 + 128],
                                              experts[:, 4 * h:4 * h + 4, :].rearrange("d e c -> d (e c)"),
                                              start=True, stop=True)
                            mm.then_inc(exp_out, 1)

                        walk(pe, passed, step, blocks, 2)

                @block.scalar
                def _(act):
                    a = nc.scalar
                    credit(act, img_kept, up1_kept, up2_kept, down_kept, xh_ready, act_part, gate_kept, out_kept)
                    with act.Fori(0, B) as b:
                        act.wait_ge(acc_done, done(b * blocks - 1))
                        settle(act, passed)
                        with act.Fori(0, ht) as i:
                            for u in range(2):
                                n = b * TILES + i * 2 + u
                                act.wait_ge(img_turned, done(n))
                                a.activation(img[:, rows_of(i * 2 + u), :],
                                             turn_ps[u][:].rearrange("p (q c) -> p q c", q=ROWS), ACT.Copy)\
                                 .then_inc(img_kept, 1)
                        act.wait_ge(stat_chain, (b * 2 + 1) * TILES * 3 + CREDIT)
                        a.activation(std_all[:], mv_all[:, :, 1], ACT.Sqrt, bias=eps6[:]).then_inc(mv_std, 1)

                        def up(g, p):
                            G = b * GROUPS + g
                            act.wait_ge(bias_got, G * 2 + 2 + CREDIT * 2)
                            act.wait_ge(up2_ready, done(G * (GC + 1) - GC - 2))
                            for c in range(GC + 1):
                                if c < GC:
                                    act.wait_ge(up1_ready, done(G * GC + c))
                                    a.activation(upc[p][:, c, :], up1_ps[c % 2][:, 0:UPN], ACT.Copy)\
                                     .then_inc(up1_kept, 1)
                                if c == 0:
                                    act.wait_ge(down_ready, done(G * 7 - 14 + 4))
                                if c >= 1:
                                    act.wait_ge(up2_ready, done(G * (GC + 1) + c - 1))
                                    a.activation(act_in[p][:, c - 1, :, :], up2_ps[(p + c - 1) % 2][:, :, 0:UPN],
                                                 ACT.Identity, scale=GAIN, bias=bias_g[p][:, c - 1:c])\
                                     .then_inc(up2_kept, 1)
                            act.wait_ge(up2_ready, done(G * (GC + 1) + GC))
                            a.activation(rem_in[p][:], up2_ps[p][0:RP, 0, 0:UPN], ACT.Identity, scale=GAIN,
                                         bias=brem_g[p][:]).then_inc(up2_kept, 1)

                        def down(g, p):
                            G = b * GROUPS + g
                            act.wait_ge(down_ready, done(G * 7 - 14 + 6))
                            for k in range(4):
                                m, h = k // 2, k % 2
                                act.wait_ge(down_ready, done(G * 7 + k))
                                a.activation(dnc[p][:, m, 4 * h:4 * h + 4, :],
                                             down_ps[(p + k) % 2][:].rearrange("p (c w) -> p c w", w=W), ACT.Copy)\
                                 .then_inc(down_kept, 1)
                            act.wait_ge(down_ready, done(G * 7 + 4))
                            a.activation(rem_dn[p][:], down_ps[p][0:RP, 0:W], ACT.Copy).then_inc(down_kept, 1)

                        groups_of(act, up, down)
                        act.wait_ge(stat_chain, (b * 2 + 2) * TILES * 3 + CREDIT)
                        a.activation(std_all[:], mv_all[:, :, 1], ACT.Sqrt, bias=eps5[:]).then_inc(mv_std, 1)

                        def step(i, u, part):
                            j, p, half = item(i, u, 0)
                            if live(j, blocks):
                                n = b * blocks + j
                                act.wait_ge(xm_turned, done(n))
                                act.wait_ge(exp_out, done((n - 1) * ROWS - 1))
                                a.activation(xh[p][:], xm_ps[:], ACT.Copy).then_inc(xh_ready, 1)
                            j1, p1_, half1 = item(i, u, 1)
                            if live(j1, blocks):
                                n1 = b * blocks + j1
                                act.wait_ge(gate_turned, done(n1))
                                act.wait_ge(out_ready, done(n1 - 2))
                                a.activation(gateTs[p1_][:], gT_ps, ACT.Copy).then_inc(gate_kept, 1)
                                act.wait_ge(y_chain, n1 * 2 - 2 + CREDIT * 2)
                                for q in range(2):
                                    weigh(n1, p1_, q)
                            if live(j, blocks):
                                act.wait_ge(route, n * ROUTES + 3 + ROUTE0)
                                a.activation(prb[p][:], lg[p][:], ACT.Exp).then_inc(exp_ready, 1)
                            if live(j1, blocks):
                                for q in range(2, 4):
                                    weigh(n1, p1_, q)
                            j, p, half = item(i, u, 2)
                            if live(j, blocks):
                                n = b * blocks + j
                                act.wait_ge(out_ready, done(n))
                                act.wait_ge(st_out[p], rounds(b * ht + half))
                                a.activation(res[p][:], out_ps[:], ACT.Copy).then_inc(out_kept, 1)

                        def weigh(n, p, q):
                            act.wait_ge(exp_out, done(n * ROWS + q))
                            for e in range(DVE_EXPERTS, E1):
                                ins = a.activation(ya[p][:, q, e - DVE_EXPERTS, :],
                                                   exp_ps[q % 2][:, e // 4, (e % 4) * 128:(e % 4) * 128 + 128],
                                                   ACT.Copy, scale=gate[p][:, q, e:e + 1])
                            ins.then_inc(act_part, 1)

                        walk(act, passed, step, blocks, 2)

                @block.gpsimd
                def _(pool):
                    g_ = nc.gpsimd
                    pool.sem_inc(grp_chain, CREDIT * 2)
                    pool.sem_inc(xm_chain, CREDIT * 2)
                    pool.sem_inc(y_chain, CREDIT * 2)
                    with pool.Fori(0, B) as b:
                        pool.wait_ge(mv_rstd, b * 2 + 1)
                        settle(pool, passed)
                        with pool.Fori(0, GROUPS // 2) as i:
                            for p in range(2):
                                g = i * 2 + p
                                G = b * GROUPS + g
                                pool.wait_ge(up1_ready, done(G * GC - GC - 1))
                                pool.wait_ge(grp_chain, G * 2 + CREDIT * 2)
                                g_.tensor_tensor(grp[p][:], chan(img, g * GC, GC),
                                                 mv_all[:, :, 0].unsqueeze(1).to_broadcast([128, GC, H]),
                                                 ALU.subtract).then_inc(grp_chain, 1)
                                pool.wait_ge(grp_chain, G * 2 + 1 + CREDIT * 2)
                                g_.tensor_tensor(grp[p][:], grp[p][:],
                                                 rstd_all[:].unsqueeze(1).to_broadcast([128, GC, H]),
                                                 ALU.mult).then_inc(grp_chain, 1)
                        pool.wait_ge(mv_rstd, b * 2 + 2)

                        def step(i, u, part):
                            j, p, half = item(i, u, 0)
                            if live(j, blocks):
                                n = b * blocks + j
                                pool.wait_ge(xm_turned, done(n - 2))
                                g_.tensor_tensor(xm[p][:], img[:, rows_of(j), :],
                                                 mv_all[:, rows_of(j), 0:1].to_broadcast([128, ROWS, C]),
                                                 ALU.subtract).then_inc(xm_chain, 1)
                                pool.wait_ge(xm_chain, n * 2 + 1 + CREDIT * 2)
                                g_.tensor_tensor(xm[p][:], xm[p][:],
                                                 rstd_all[:, rows_of(j)].unsqueeze(2).to_broadcast([128, ROWS, C]),
                                                 ALU.mult).then_inc(xm_chain, 1)
                            j, p, half = item(i, u, 1)
                            if live(j, blocks):
                                n = b * blocks + j
                                pool.wait_ge(act_part, done(n * ROWS + ROWS - 1))
                                pool.wait_ge(acc_done, done(n - 2))
                                g_.tensor_tensor(ya[p][:, :, 0:2, :], ya[p][:, :, 0:2, :], ya[p][:, :, 2:4, :], ALU.add)\
                                  .then_inc(y_chain, 1)
                                pool.wait_ge(y_chain, n * 2 + 1 + CREDIT * 2)
                                g_.tensor_tensor(ys[p][:], ya[p][:, :, 0, :], ya[p][:, :, 1, :], ALU.add)\
                                  .then_inc(y_chain, 1)

                        walk(pool, passed, step, blocks, 1)

                @block.vector
                def _(dve):
                    v = nc.vector
                    credit(dve, x2_ready, stat_chain, leaky, conv_added, acc_done)
                    dve.sem_inc(route, ROUTE0)
                    dve.sem_inc(rem_ready, CREDIT * 3)
                    dve.sem_inc(bias_got, CREDIT * 2)
                    dve.sem_inc(dve_part, CREDIT * DVE_EXPERTS)

                    def keep_stats(n, j, u, rows):
                        s0 = n * 3 + CREDIT
                        for q in range(ROWS):
                            ins = v.bn_stats(stat4[u][:, q, :], rows(q))
                        ins.then_inc(stat_chain, 1)
                        dve.wait_ge(stat_chain, s0 + 1)
                        settle(dve, passed)
                        for q in range(ROWS):
                            ins = v.bn_aggr(mv4[u][:, q, :], stat4[u][:, q, :])
                        ins.then_inc(stat_chain, 1)
                        dve.wait_ge(stat_chain, s0 + 2)
                        v.tensor_copy(mv_all[:, rows_of(j), :], mv4[u][:]).then_inc(stat_chain, 1)

                    with dve.Fori(0, B) as b:
                        v.tensor_copy(moe_b[:], moeT[:, :, bass.ds(b, 1)].rearrange("p e a -> p (e a)"))\
                         .then_inc(moe_got, 1)
                        v.tensor_copy(rs_b[:], rsum_all[:, bass.ds(b, 1)]).then_inc(moe_got, 1)
                        dve.wait_ge(moe_turned, b + 1)
                        dve.wait_ge(moe_got, b * 2 + 2)
                        v.tensor_scalar(moe_w[:], turn_ps[0][0:E0, 0:128], rs_b[:], None, ALU.mult)\
                         .then_inc(moe_scaled, 1)
                        settle(dve, passed)
                        with dve.Fori(0, ht) as i:
                            for u in range(2):
                                n = b * TILES + i * 2 + u
                                dve.wait_ge(add_ready, done(n))
                                dve.wait_ge(ld_x1[u], (b * ht + i + 1) * 16)
                                dve.wait_ge(img_turned, done(n - 2))
                                v.tensor_tensor(x2[u][:], add_ps[u][:], x1_in[u][:], ALU.add).then_inc(x2_ready, 1)
                            for u in range(2):
                                j = i * 2 + u
                                dve.wait_ge(img_kept, done(b * TILES + j))
                                keep_stats(b * 2 * TILES + j, j, u,
                                           lambda q: img[:, bass.ds(j * ROWS + q, 1), :]
                                           .rearrange("p a c -> p (a c)"))
                        dve.wait_ge(mv_std, b * 2 + 1)
                        v.reciprocal(rstd_all[:], std_all[:]).then_inc(mv_rstd, 1)

                        def up(g, p):
                            G = b * GROUPS + g
                            dve.wait_ge(up2_kept, done(G * (GC + 1) - GC - 2))
                            v.tensor_copy(bias_g[p][:], bias_all[:, bass.ds(g * GC, GC)]).then_inc(bias_got, 1)
                            v.tensor_copy(brem_g[p][:], bias_rem[:, bass.ds(g, 1)]).then_inc(bias_got, 1)
                            for c in range(GC):
                                n = G * (GC + 1) + c
                                dve.wait_ge(up2_kept, done(n))
                                z = act_in[p][:, c, :, :]
                                v.scalar_tensor_tensor(out=z, in0=z, scalar=SLOPE, in1=z, op0=ALU.mult, op1=ALU.max)\
                                 .then_inc(leaky, 1)
                                if c == GC - 2:
                                    dve.wait_ge(up1_kept, done(G * GC + GC - 1))
                                    v.tensor_copy(upc_rem[p][:].rearrange("p (c r) -> p c r", r=REM),
                                                  upc[p][:, :, 2 * W:UPN]).then_inc(rem_ready, 1)
                            n = G * (GC + 1) + GC
                            dve.wait_ge(leaky, done(n - 1))
                            v.tensor_copy(act_rem[p][:].rearrange("p q (c r) -> p q c r", r=REM),
                                          act_in[p][:, :, :, 2 * H:UPN].rearrange("p c q r -> p q c r"))\
                             .then_inc(rem_ready, 1)
                            dve.wait_ge(up2_kept, done(n))
                            z = rem_in[p][:]
                            v.scalar_tensor_tensor(out=z, in0=z, scalar=SLOPE, in1=z, op0=ALU.mult, op1=ALU.max)\
                             .then_inc(leaky, 1)
                            dve.wait_ge(leaky, done(n))
                            v.tensor_tensor(rem_blk[p][:],
                                            rem_in[p][:, 2 * H:UPN].unsqueeze(1).to_broadcast([RP, GC, REM]),
                                            block_mask[:], ALU.mult).then_inc(rem_ready, 1)

                        def down(g, p):
                            G = b * GROUPS + g
                            for h in range(2):
                                dve.wait_ge(down_ready, done(G * 7 + 5 + h))
                                at = chan(img, g * GC + 4 * h, 4)
                                v.tensor_tensor(at, down_ps[(p + 5 + h) % 2][:].rearrange("p (c h) -> p c h", h=H),
                                                at, ALU.add).then_inc(conv_added, 1)

                        groups_of(dve, up, down)
                        dve.wait_ge(conv_added, done(b * 2 * GROUPS + 2 * GROUPS - 1))
                        settle(dve, passed)
                        with dve.Fori(0, ht) as i:
                            for u in range(2):
                                j = i * 2 + u
                                keep_stats(b * 2 * TILES + TILES + j, j, u,
                                           lambda q: img[:, bass.ds(j * ROWS + q, 1), :]
                                           .rearrange("p a c -> p (a c)"))
                        dve.wait_ge(mv_std, b * 2 + 2)
                        v.reciprocal(rstd_all[:], std_all[:]).then_inc(mv_rstd, 1)

                        def step(i, u, part):
                            j, p, half = item(i, u, 0)
                            j1, p1_, half1 = item(i, u, 1)
                            if live(j1, blocks):
                                n1 = b * blocks + j1
                                dve.wait_ge(out_ready, done(n1 - 2))
                                weigh(n1, j1, p1_, 0)
                            if live(j, blocks):
                                n = b * blocks + j
                                link = Chain(dve, route, n * ROUTES + ROUTE0)
                                dve.wait_ge(lg_ready, done(n))
                                link(v.tensor_tensor(lg[p][:], lg_ps,
                                                     router_b_all[:].unsqueeze(1).to_broadcast([128, ROWS, E1]),
                                                     ALU.add))
                                link(v.tensor_reduce(mx[:], lg[p][:], AX_X, ALU.max))
                                link(v.tensor_tensor(lg[p][:], lg[p][:], spread(mx), ALU.subtract))
                            if live(j1, blocks):
                                weigh(n1, j1, p1_, 2)
                                dve.wait_ge(y_chain, n1 * 2 + 2 + CREDIT * 2)
                                dve.wait_ge(dve_part, (n1 * ROWS + ROWS) * DVE_EXPERTS + CREDIT * DVE_EXPERTS)
                                v.tensor_tensor(acc[p1_][:], acc[p1_][:], ys[p1_][:], ALU.add).then_inc(acc_done, 1)
                            if live(j, blocks):
                                dve.wait_ge(exp_ready, n + 1)
                                P = prb[p][:]
                                link(v.tensor_reduce(sm[:], P, AX_X, ALU.add))
                                link(v.reciprocal(p1[:], sm[:]))
                                link(v.tensor_tensor(P, P, spread(p1), ALU.mult))
                                link(v.tensor_reduce(p1[:], P, AX_X, ALU.max))
                                top_one(link, P, p1, first)
                                link(v.scalar_tensor_tensor(out=pr2[:], in0=first[:], scalar=-2.0, in1=P,
                                                            op0=ALU.mult, op1=ALU.add))
                                link(v.tensor_reduce(p2[:], pr2[:], AX_X, ALU.max))
                                top_one(link, pr2[:], p2, second)
                                link(v.tensor_tensor(sm[:], p1[:], p2[:], ALU.add))
                                link(v.reciprocal(p1[:], sm[:]))
                                link(v.tensor_tensor(first[:], first[:], second[:], ALU.add))
                                link(v.tensor_tensor(P, P, first[:], ALU.mult))
                                link(v.tensor_tensor(gate[p][:], P, spread(p1), ALU.mult))
                                assert link.n == ROUTES, link.n

                        def spread(t):
                            return t[:].unsqueeze(2).to_broadcast([128, ROWS, E1])

                        def top_one(link, P, best, hot):
                            link(v.tensor_tensor(eq[:], P, spread(best), ALU.is_equal))
                            link(v.tensor_tensor(eq[:], eq[:], desc8[:].unsqueeze(1).to_broadcast([128, ROWS, E1]),
                                                 ALU.mult))
                            link(v.tensor_reduce(mx[:], eq[:], AX_X, ALU.max))
                            link(v.tensor_tensor(hot[:], eq[:], spread(mx), ALU.is_equal))

                        def weigh(n, j, p, q0):
                            for q in range(q0, q0 + 2):
                                dve.wait_ge(exp_out, done(n * ROWS + q))
                            for e in range(DVE_EXPERTS):
                                for q in range(q0, q0 + 2):
                                    base = (n * ROWS + q0) * DVE_EXPERTS + CREDIT * DVE_EXPERTS
                                    if e:
                                        dve.wait_ge(dve_part, base + 2 * e - 1 + q - q0)
                                    before = acc[p][:, q, :] if e else \
                                        img[:, bass.ds(j * ROWS + q, 1), :].rearrange("p a c -> p (a c)")
                                    v.scalar_tensor_tensor(
                                        out=acc[p][:, q, :],
                                        in0=exp_ps[q % 2][:, e // 4, (e % 4) * 128:(e % 4) * 128 + 128],
                                        scalar=gate[p][:, q, e:e + 1], in1=before, op0=ALU.mult, op1=ALU.add)\
                                     .then_inc(dve_part, 1)

                        walk(dve, passed, step, blocks, 2)


_INS = ["x", "L0_conv_w1", "L0_conv_in_gamma", "L0_conv_in_beta", "L0_conv_w2", "L0_conv_b2",
        "L0_ffn_gate_w", "L0_ffn_gate_b", "L0_ffn_weight1", "L0_ffn_weight2", "L1_conv_bias",
        "L1_conv_up_filter", "L1_conv_down_filter", "L1_ffn_router_w", "L1_ffn_router_b",
        "L1_ffn_expert_w", "L1_ffn_expert_b"]


def kernel(**inputs):
    import concourse.bacc as _bacc
    from concourse.bass_utils import run_bass_kernel_spmd as _run

    nc = _bacc.Bacc("TRN2", target_bir_lowering=False, num_devices=1)
    arrays, args = {}, []
    for name in _INS:
        a = np.ascontiguousarray(inputs[name])
        arrays[f"in_{name}"] = a
        args.append(nc.dram_tensor(f"in_{name}", a.shape, mybir.dt.from_np(a.dtype), kind="ExternalInput").ap())
    args.append(nc.dram_tensor("out_0", (B, C, H, W), F32, kind="ExternalOutput").ap())
    metaformer_kernel(nc, *args)
    return _run(nc, [arrays], core_ids=[0]).results[0]["out_0"]
```

```python
from contextlib import ExitStack

import numpy as np

import concourse.bass as bass
from concourse import mybir

F32 = mybir.dt.float32
BF16 = mybir.dt.bfloat16
U32 = mybir.dt.uint32
ALU = mybir.AluOpType
ACT = mybir.ActivationFunctionType
AX_X = mybir.AxisListType.X

B, C, H, W = 8, 128, 128, 128
TOKENS = H * W
ROWS = 4
TILE = ROWS * W
TILES = H // ROWS
RED = 16
TAPS = 9
PAD = 2
HP = H + 2 * PAD
E0, K0, HID = 64, 8, 512
HALF = TOKENS // 2
NEG, BIG = -3.0e38, 2.0 ** 127
FT = 12
UPN = 2 * H + 10
REM = UPN - 2 * H
GC = 8
GROUPS = C // GC
RP = GC * REM
EDGE = 5
SLOPE, GAIN = 0.2, float(np.sqrt(2.0).astype(np.float32))
E1 = 8
OCTET = 2 * ROWS
ACT_EXPERTS = 4
DVE_EXPERTS = E1 - ACT_EXPERTS

CREDIT = 16


def done(n):
    return n + (CREDIT + 1)


def rounds(n):
    return (n + 1) * 16


def item(i, u, lag):
    d = u - lag
    p = d % 2
    half = i + (d - p) // 2
    return half * 2 + p, p, half


def settle(eng, passed):
    eng.sem_inc(passed, 1)


def walk(eng, passed, step, count, lag, parts=1):
    head = (lag + 1) // 2
    size = count // 2 // parts
    for part in range(parts):
        for i in range(part * size, part * size + head):
            for u in range(2):
                step(i, u, part)
        settle(eng, passed)
        with eng.Fori(part * size + head, (part + 1) * size) as i:
            for u in range(2):
                step(i, u, part)
    for s in range(count, count + lag):
        step(s // 2, s % 2, parts)


def live(j, count):
    return not isinstance(j, int) or 0 <= j < count


class Chain:

    def __init__(self, eng, sem, base):
        self.eng, self.sem, self.base, self.n = eng, sem, base, 0

    def __call__(self, ins):
        self.n += 1
        ins.then_inc(self.sem, 1)
        self.eng.wait_ge(self.sem, self.base + self.n)


class Braid:

    def __init__(self, eng, sem, base):
        self.eng, self.sem, self.base, self.n, self.waited = eng, sem, base, 0, 0

    def __call__(self, ins):
        self.n += 1
        ins.then_inc(self.sem, 1)

    def ready(self):
        if self.n > self.waited:
            self.eng.wait_ge(self.sem, self.base + self.n)
            self.waited = self.n


def metaformer_kernel(nc, x, w1, in_gamma, in_beta, w2, b2, gate_w, gate_b, ew1, ew2,
                      conv_bias, up_filter, down_filter, router_w, router_b, expert_w, expert_b, out):
    x1_dram = nc.dram_tensor("x1_dram", (B, C, H, W), F32).ap()
    xT_dram = nc.dram_tensor("xT_dram", (TOKENS, C), F32).ap()
    rA_dram = nc.dram_tensor("rA_dram", (3, TOKENS), BF16).ap()
    rB_dram = nc.dram_tensor("rB_dram", (3, 2, HALF), BF16).ap()
    S_dram = nc.dram_tensor("S_dram", (B, E0, TOKENS), F32).ap()

    with ExitStack() as ctx:
        def sb(name, shape, dt=F32):
            return ctx.enter_context(nc.sbuf_tensor(name, shape, dt))

        def sem(name):
            return ctx.enter_context(nc.semaphore(name))

        bank = [ctx.enter_context(nc.psum_tensor(f"bank{i}", [128, 512], F32)) for i in range(4)]
        duo = [ctx.enter_context(nc.psum_tensor(f"duo{i}", [128, 2, 512], F32)) for i in range(2)]

        ident = sb("ident", [128, 128])
        center = sb("center", [128, 128])
        mean_col = sb("mean_col", [128, 1])
        eps6 = sb("eps6", [128, 1])
        eps5 = sb("eps5", [128, 1])
        ones3 = sb("ones3", [3, 128], BF16)
        sel6 = sb("sel6", [6, 128], BF16)
        w1rep = sb("w1rep", [128, 128])
        gamma_rep = sb("gamma_rep", [128, 1])
        beta_rep = sb("beta_rep", [128, 1])
        wstack = sb("wstack", [128, TAPS, 128], BF16)
        gateT = sb("gateT", [128, E0])
        gate_bias = sb("gate_bias", [E0, 1])
        slots16 = sb("slots16", [E0, 16])
        up_mat = sb("up_mat", [128, UPN])
        down_mat = sb("down_mat", [128, 2, 128])
        down_edge = sb("down_edge", [RP, GC, EDGE])
        down_edge1 = sb("down_edge1", [RP, EDGE])
        block_mask = sb("block_mask", [RP, GC, REM])
        bias_all = sb("bias_all", [128, C])
        bias_rem = sb("bias_rem", [RP, GROUPS])
        router = sb("router", [128, E1])
        router_b_all = sb("router_b_all", [128, E1])
        desc8 = sb("desc8", [128, E1])
        ebias = sb("ebias", [ROWS * E1, ROWS, 128])
        pooledT = sb("pooledT", [128, B, E0])
        moeT = sb("moeT", [128, E0, B])
        rsum_all = sb("rsum_all", [E0, B])

        s_fill = sem("s_fill")
        s_load = sem("s_load")
        s_dve0 = sem("s_dve0")
        s_pe0 = sem("s_pe0")

        passed = sem("passed")

        def credit(eng, *names):
            for s in names:
                eng.sem_inc(s, CREDIT)

        with ExitStack() as tmp:
            def tb(name, shape, dt=F32):
                return tmp.enter_context(nc.sbuf_tensor(name, shape, dt))

            w1x = tb("w1x", [128, 128])
            gw = tb("gw", [E0, 128])
            gwT = tb("gwT", [128, E0])
            w2n = tb("w2n", [128, TAPS, RED])
            b2n = tb("b2n", [128, TAPS, 1])
            part16 = tb("part16", [128, TAPS, RED + 1], BF16)
            rest = tb("rest", [128, TAPS, RED + 1])
            rest2 = tb("rest2", [128, TAPS, RED + 1])
            stack_rows = tb("stack_rows", [128, TAPS, 128])
            fu = tb("fu", [128, FT])
            fd = tb("fd", [128, FT])
            cb = tb("cb", [128, C])
            up_tap = tb("up_tap", [128, FT, UPN])
            down_tap = tb("down_tap", [128, 2, FT, 128])
            edge_tap = tb("edge_tap", [RP, FT, GC, EDGE])
            edge_sum = tb("edge_sum", [RP, GC, EDGE])
            brem = tb("brem", [RP, GROUPS, GC])
            ones_t = tb("ones_t", [128, 128])
            zeros_t = tb("zeros_t", [128, 128])
            ones_b = tb("ones_b", [6, 128], BF16)
            sel_b = tb("sel_b", [6, 128], BF16)
            ones_m = tb("ones_m", [RP, GC, REM])
            ones_m2 = tb("ones_m2", [RP, GC, REM])
            slots_i = tb("slots_i", [E0, 16], mybir.dt.int32)
            desc_i = tb("desc_i", [128, E1], mybir.dt.int32)

            n_zero = 9
            small = [(gw, gate_w), (w2n, w2.rearrange("(c k) o -> c k o", k=TAPS)),
                     (b2n, b2.rearrange("(c k a) -> c k a", k=TAPS, a=1)),
                     (gate_bias, gate_b.rearrange("(e a) -> e a", a=1)),
                     (fu, up_filter.partition_broadcast(128)), (fd, down_filter.partition_broadcast(128)),
                     (cb, conv_bias.partition_broadcast(128)), (router, router_w),
                     (router_b_all, router_b.partition_broadcast(128))]
            groups = [0, 1, 2, 4, 5, 6, 7]
            n_loads = len(small) + 3 * len(groups) + ROWS
            filled = n_zero + 11 + 4 * FT
            dve_steps = []
            with nc.Block() as block:
                @block.gpsimd
                def _(pool):
                    g = nc.gpsimd
                    for t, v in ((w1x, 0.0), (gamma_rep, 0.0), (beta_rep, 1.0), (ebias, 0.0), (stack_rows, 0.0),
                                 (ones_t, 1.0), (zeros_t, 0.0), (ones_b, 1.0), (ones_m, 1.0)):
                        g.memset(t[:], v).then_inc(s_fill, 1)
                    pool.wait_ge(s_fill, n_zero)
                    g.memset(mean_col[:], 1.0 / C).then_inc(s_fill, 1)
                    g.memset(eps6[:], 1e-6).then_inc(s_fill, 1)
                    g.memset(eps5[:], 1e-5).then_inc(s_fill, 1)
                    g.memset(ones3[:], 1.0).then_inc(s_fill, 1)
                    g.affine_select(out=ident[:], in_=zeros_t[:], compare_op=ALU.not_equal, fill=1.0, base=0,
                                    pattern=[[-1, 128]], channel_multiplier=1).then_inc(s_fill, 1)
                    g.affine_select(out=sel_b[:, 0:64], in_=ones_b[:, 0:64], compare_op=ALU.is_ge, fill=0.0, base=2,
                                    pattern=[[0, 64]], channel_multiplier=-1).then_inc(s_fill, 1)
                    g.affine_select(out=sel_b[:, 64:128], in_=ones_b[:, 64:128], compare_op=ALU.is_ge, fill=0.0,
                                    base=-3, pattern=[[0, 64]], channel_multiplier=1).then_inc(s_fill, 1)
                    g.iota(slots_i[:], pattern=[[1, 16]], base=0, channel_multiplier=0).then_inc(s_fill, 1)
                    g.iota(desc_i[:], pattern=[[-1, E1]], base=E1, channel_multiplier=0).then_inc(s_fill, 1)
                    g.affine_select(out=ones_m2[:], in_=ones_m[:], compare_op=ALU.is_ge, fill=0.0, base=0,
                                    pattern=[[-REM, GC], [0, REM]], channel_multiplier=1).then_inc(s_fill, 1)
                    pool.wait_ge(s_fill, n_zero + 10)
                    g.affine_select(out=block_mask[:], in_=ones_m2[:], compare_op=ALU.is_ge, fill=0.0, base=REM - 1,
                                    pattern=[[REM, GC], [0, REM]], channel_multiplier=-1).then_inc(s_fill, 1)
                    pool.wait_ge(s_load, 16 * n_loads)
                    for t in range(FT):
                        g.affine_select(out=up_tap[:, t, :], in_=fu[:, t:t + 1].to_broadcast([128, UPN]),
                                        compare_op=ALU.is_equal, fill=0.0, base=-t, pattern=[[1, UPN]],
                                        channel_multiplier=-2).then_inc(s_fill, 1)
                        for m in range(2):
                            g.affine_select(out=down_tap[:, m, t, :], in_=fd[:, t:t + 1].to_broadcast([128, 128]),
                                            compare_op=ALU.is_equal, fill=0.0, base=128 * m - (FT - 1) + t,
                                            pattern=[[-2, 128]], channel_multiplier=1).then_inc(s_fill, 1)
                        first = 2 * H - (FT - 1) + t - 2 * (128 - EDGE)
                        g.affine_select(out=edge_tap[:, t, :, :],
                                        in_=fd[0:RP, t:t + 1].unsqueeze(2).to_broadcast([RP, GC, EDGE]),
                                        compare_op=ALU.is_equal, fill=0.0, base=first,
                                        pattern=[[-REM, GC], [-2, EDGE]], channel_multiplier=1).then_inc(s_fill, 1)

                @block.sync
                def _(sp):
                    for dst, src in small:
                        sp.dma_start(dst[:], src).then_inc(s_load, 16)
                    sp.wait_ge(s_fill, n_zero)
                    for q in groups:
                        at = slice(RED * q, RED * q + RED)
                        sp.dma_start(w1x[at, :], w1).then_inc(s_load, 16)
                        sp.dma_start(gamma_rep[at, :], in_gamma.rearrange("(e a) -> e a", a=1)).then_inc(s_load, 16)
                        sp.dma_start(beta_rep[at, :], in_beta.rearrange("(e a) -> e a", a=1)).then_inc(s_load, 16)
                    for q in range(ROWS):
                        sp.dma_start(ebias[q * E1:q * E1 + E1, q, :], expert_b).then_inc(s_load, 16)

                @block.vector
                def _(dve):
                    v = nc.vector
                    link = Chain(dve, s_dve0, 0)
                    dve.wait_ge(s_fill, filled)
                    dve.wait_ge(s_load, 16 * n_loads)
                    link(v.tensor_scalar(center[:], ident[:], -1.0 / C, None, ALU.add))
                    link(v.tensor_copy(slots16[:], slots_i[:]))
                    link(v.tensor_copy(desc8[:], desc_i[:]))
                    link(v.tensor_copy(sel6[:], sel_b[:]))
                    link(v.tensor_copy(rest[:, :, 0:RED], w2n[:]))
                    link(v.tensor_copy(rest[:, :, RED:RED + 1], b2n[:]))
                    for n, (cols, bcol) in enumerate((((0, 64, 96), 48), ((16, 80), 49), ((32,), 50))):
                        link(v.tensor_copy(part16[:], rest[:]))
                        for c0 in cols:
                            link(v.tensor_copy(stack_rows[:, :, c0:c0 + RED], part16[:, :, 0:RED]))
                        link(v.tensor_copy(stack_rows[:, :, bcol:bcol + 1], part16[:, :, RED:RED + 1]))
                        link(v.tensor_tensor(rest2[:], rest[:], part16[:], ALU.subtract))
                        link(v.tensor_copy(rest[:], rest2[:]))
                    link(v.tensor_scalar(up_mat[:], up_tap[:, 0, :], 1.0, None, ALU.mult))
                    for t in range(1, FT):
                        link(v.tensor_tensor(up_mat[:], up_mat[:], up_tap[:, t, :], ALU.add))
                    link(v.tensor_scalar(up_mat[:], up_mat[:], 2.0, None, ALU.mult))
                    link(v.tensor_copy(down_mat[:], down_tap[:, :, 0, :]))
                    for t in range(1, FT):
                        link(v.tensor_tensor(down_mat[:], down_mat[:], down_tap[:, :, t, :], ALU.add))
                    link(v.tensor_copy(edge_sum[:], edge_tap[:, 0]))
                    for t in range(1, FT):
                        link(v.tensor_tensor(edge_sum[:], edge_sum[:], edge_tap[:, t], ALU.add))
                    link(v.tensor_tensor(down_edge[:], edge_sum[:], block_mask[:, :, 0:EDGE], ALU.mult))
                    link(v.tensor_reduce(down_edge1[:], down_edge[:].rearrange("p c j -> p j c"), AX_X, ALU.add))
                    link(v.tensor_scalar(bias_all[:], cb[:], GAIN, None, ALU.mult))
                    link(v.tensor_tensor(brem[:], bias_all[0:RP, :].rearrange("p (g c) -> p g c", c=GC),
                                         block_mask[:, :, 0:1].rearrange("p c a -> p a c")
                                         .to_broadcast([RP, GROUPS, GC]), ALU.mult))
                    link(v.tensor_reduce(bias_rem[:], brem[:], AX_X, ALU.add))
                    for k in range(TAPS):
                        dve.wait_ge(s_pe0, k + 1)
                        link(v.tensor_copy(wstack[:, k, :], bank[k % 2][:, 0:128]))
                    dve.wait_ge(s_pe0, TAPS + 1)
                    link(v.tensor_copy(w1rep[:], bank[TAPS % 2][:, 0:128]))
                    dve.wait_ge(s_pe0, TAPS + 2)
                    link(v.tensor_copy(gwT[:], bank[(TAPS + 1) % 2][:, 0:E0]))
                    dve.wait_ge(s_pe0, TAPS + 3)
                    link(v.tensor_copy(gateT[:], bank[TAPS % 2][:, 0:E0]))
                    dve_steps.append(link.n)

                @block.tensor
                def _(pe):
                    t = nc.tensor
                    before = dve_steps[0] - TAPS - 3
                    for k in range(TAPS):
                        pe.wait_ge(s_dve0, before + max(k - 1, 0))
                        t.transpose(bank[k % 2][:, 0:128], stack_rows[:, k, :], ident[:]).then_inc(s_pe0, 1)
                    pe.wait_ge(s_dve0, before + TAPS - 1)
                    t.transpose(bank[TAPS % 2][:, 0:128], w1x[:], ident[:]).then_inc(s_pe0, 1)
                    pe.wait_ge(s_dve0, before + TAPS)
                    t.transpose(bank[(TAPS + 1) % 2][:, 0:E0], gw[:], ident[0:E0, 0:E0]).then_inc(s_pe0, 1)
                    pe.wait_ge(s_dve0, before + TAPS + 2)
                    t.matmul(bank[TAPS % 2][:, 0:E0], center[:], gwT[:], start=True, stop=True).then_inc(s_pe0, 1)

        with ExitStack() as tmp:
            def tb(name, shape, dt=F32):
                return tmp.enter_context(nc.sbuf_tensor(name, shape, dt))

            def pair(name, shape, dt=F32):
                return [tb(f"{name}{u}", shape, dt) for u in range(2)]

            xn = tb("xn", [128, HP, HP])
            logits = tb("logits", [128, HALF + 8])
            picked = tb("picked", [128, HALF + 8], BF16)
            x_in = pair("x_in", [128, TILE])
            std = tb("std", [128, H])
            rstd = tb("rstd", [128, H])
            var_all = tb("var_all", [128, H])
            r_part = [tb(f"r_part{k}", [128, W], BF16) for k in range(3)]
            r_rest = tb("r_rest", [128, W])
            rA = pair("rA", [3, TILE], BF16)
            rB = pair("rB", [6, TILE], BF16)
            t_stats = tb("t_stats", [128, TILES * 6])
            t_mv = tb("t_mv", [128, 2])
            t_tmp = tb("t_tmp", [128, 2])
            t_scale = tb("t_scale", [128, 1])
            t_bias = tb("t_bias", [128, 1])
            stack = pair("stack", [128, TILE], BF16)
            t_full = pair("t_full", [128, TILE])
            t_high = pair("t_high", [128, TILE], BF16)
            t_rest = pair("t_rest", [128, TILE])
            square = t_rest
            prod_all = tb("prod_all", [128, TAPS, TILE])
            prod = [prod_all[:, k, :] for k in range(TAPS)]
            psum_in = [pair(f"part_sum{k}", [128, TILE]) for k in range(4)]
            x_res = pair("x_res", [128, TILE])
            x1 = pair("x1", [128, TILE])
            x1T = pair("x1T", [128, ROWS, C])
            sq_junk = tb("sq_junk", [128, ROWS, C], BF16)
            var4 = pair("var4", [128, ROWS])
            top_half = tb("top_half", [128, 8])
            idx_half = tb("idx_half", [128, 8], U32)
            idxf_half = tb("idxf_half", [128, 8])
            cand = tb("cand", [E0, 16])
            cand_idx = tb("cand_idx", [E0, 16])
            top = tb("top", [E0, 8])
            pos = tb("pos", [E0, 8], U32)
            posf = tb("posf", [E0, 8])
            cand_mark = tb("cand_mark", [E0, 16])
            kept = tb("kept", [E0, 16])
            kept2 = tb("kept2", [E0, 16])
            lists = tb("lists", [E0, 17])
            find = tb("find", [128, 9])
            token_eq = tb("token_eq", [E0, K0, 16])
            token_f = tb("token_f", [E0, K0])
            token = tb("token", [E0, K0], U32)
            zsum = tb("zsum", [128, 1])
            zsum2 = tb("zsum2", [E0, 1])
            zinv = tb("zinv", [E0, 1])
            rsum_b = tb("rsum_b", [E0, 1])
            top_exp = tb("top_exp", [E0, K0])
            rows = prod_all[0:E0, 0:2, :].rearrange("e a (k c) -> e (a k) c", c=C)
            rows_sq = prod_all[0:E0, 2:4, :].rearrange("e a (k c) -> e (a k) c", c=C)
            row_var = tb("row_var", [E0, K0])
            row_std = tb("row_std", [E0, K0])
            row_w = tb("row_w", [E0, K0])
            pooled = tb("pooled", [E0, C])

            centre_ps, rb_ps = bank[0:2], bank[0:2]
            t_ps, raw_ps = bank[2], bank[3]
            wgt_ps = [bank[0], bank[1], duo[0][:, 0]]
            acc_ps, xT_ps = duo[0][:, 1], duo[1][:, 0]
            var_ps = [bank[2 + u][:, 0:ROWS] for u in range(2)]
            turn_ps = duo[1][:, 1, 128:256]
            pool_ps = duo[1][:, 1, 256:256 + E0]

            def nsem(name):
                return tmp.enter_context(nc.semaphore(name))

            ld_x = [nsem(f"ld_x{u}") for u in range(2)]
            centred = nsem("centred")
            squared = nsem("squared")
            varied = nsem("varied")
            var_kept = nsem("var_kept")
            std_ready = nsem("std_ready")
            split_chain = nsem("split_chain")
            turned = nsem("turned")
            st_r = [nsem(f"st_r{k}") for k in range(3)]
            ld_rA = [nsem(f"ld_rA{u}") for u in range(2)]
            ld_rB = [[nsem(f"ld_rB{u}{h}") for h in range(2)] for u in range(2)]
            rb_ready = nsem("rb_ready")
            scaled = nsem("scaled")
            t_ready = nsem("t_ready")
            t_counted = nsem("t_counted")
            norm_chain = nsem("norm_chain")
            norm_std = nsem("norm_std")
            t2_ready = nsem("t2_ready")
            relu_chain = nsem("relu_chain")
            mid_ready = nsem("mid_ready")
            part_chain = nsem("part_chain")
            sum_chain = nsem("sum_chain")
            wgt_ready = nsem("wgt_ready")
            mul_done = nsem("mul_done")
            pair_chain = nsem("pair_chain")
            acc_ready = nsem("acc_ready")
            x1_ready = nsem("x1_ready")
            ld_res = [nsem(f"ld_res{u}") for u in range(2)]
            st_x1 = [nsem(f"st_x1{u}") for u in range(2)]
            st_xT = [nsem(f"st_xT{u}") for u in range(2)]
            xT_ready = nsem("xT_ready")
            raw_ready = nsem("raw_ready")
            raw_kept = nsem("raw_kept")
            xT_kept = nsem("xT_kept")
            var4_ready = nsem("var4_ready")
            var4_kept = nsem("var4_kept")
            std2_ready = nsem("std2_ready")
            turned2 = nsem("turned2")
            rb2_ready = nsem("rb2_ready")
            normed = nsem("normed")
            pick_chain = nsem("pick_chain")
            mv_cand = [nsem(f"mv_cand{k}") for k in range(2)]
            mv_list = [nsem(f"mv_list{k}") for k in range(2)]
            mv_sum = nsem("mv_sum")
            exp_all = nsem("exp_all")
            st_S = [nsem(f"st_S{k}") for k in range(2)]
            ld_rows = [nsem(f"ld_rows{k}") for k in range(K0)]
            pool_turned = nsem("pool_turned")
            pool_kept = nsem("pool_kept")
            border = nsem("border")

            SPLITS = 6
            NORMS = 5
            PICKS = 34
            half_tiles = TILES // 2

            def pick(b, n):
                return b * PICKS + (n + 1)

            def tile_of(ap, b, j):
                return ap[bass.ds(b, 1), :, bass.ds(j * ROWS, ROWS), :].rearrange("a c h w -> (a c) h w")

            def inner(j):
                return xn[:, bass.ds(j * ROWS + PAD, ROWS), PAD:PAD + W]

            def grid(ap):
                return ap.rearrange("p (h w) -> p h w", h=ROWS)

            with nc.Block() as block:
                @block.sync
                def _(sp):
                    for s in (*st_x1, *st_xT, *st_S):
                        sp.sem_inc(s, 16)

                    def store_r(base, views):
                        for k in range(3):
                            sp.wait_ge(split_chain, base + (3, 5, 6)[k])
                            sp.dma_start(views[k], r_part[k][:]).then_inc(st_r[k], 16)

                    with sp.Fori(0, B) as b:
                        with sp.Fori(0, half_tiles) as i:
                            for u in range(2):
                                n = b * TILES + i * 2 + u
                                sp.wait_ge(centred, done(n - 2))
                                sp.dma_start(grid(x_in[u][:]), tile_of(x, b, i * 2 + u)).then_inc(ld_x[u], 16)
                        store_r(b * 2 * SPLITS, [rA_dram[k].rearrange("(h w) -> h w", w=W) for k in range(3)])
                        for k in range(3):
                            sp.wait_ge(st_r[k], b * 32 + 16)
                        settle(sp, passed)
                        with sp.Fori(0, half_tiles) as i:
                            for u in range(2):
                                n = b * TILES + i * 2 + u
                                sp.wait_ge(rb_ready, done(n - 2))
                                sp.dma_start(rA[u][:], rA_dram[:, bass.ds((i * 2 + u) * TILE, TILE)])\
                                  .then_inc(ld_rA[u], 16)

                        sp.wait_ge(pick_chain, pick(b, 0))
                        settle(sp, passed)

                        def step(i, u, part):
                            j, p, half = item(i, u, 0)
                            if live(j, TILES):
                                sp.wait_ge(x1_ready, done(b * TILES + j - 2))
                                sp.dma_start(grid(x_res[p][:]), tile_of(x, b, j)).then_inc(ld_res[p], 16)
                            j, p, half = item(i, u, 3)
                            if live(j, TILES):
                                n = b * TILES + j
                                sp.wait_ge(x1_ready, done(n))
                                sp.dma_start(tile_of(x1_dram, b, j), grid(x1[p][:])).then_inc(st_x1[p], 16)
                                sp.wait_ge(xT_kept, done(n))
                                sp.dma_start(
                                    xT_dram[bass.ds(j * TILE, TILE), :].rearrange("(q p) c -> p q c", p=128),
                                    x1T[p][:]).then_inc(st_xT[p], 16)

                        walk(sp, passed, step, TILES, 3, parts=2)
                        store_r((b * 2 + 1) * SPLITS,
                                [rB_dram[k].rearrange("s t -> (s t)").rearrange("(h w) -> h w", w=W)
                                 for k in range(3)])
                        for k in range(3):
                            sp.wait_ge(st_r[k], b * 32 + 32)
                        settle(sp, passed)
                        with sp.Fori(0, half_tiles // 2) as i:
                            for u in range(2):
                                n = b * half_tiles + i * 2 + u
                                sp.wait_ge(rb2_ready, done(n - 2))
                                for h in range(2):
                                    sp.dma_start(rB[u][3 * h:3 * h + 3, :],
                                                 rB_dram[:, h, bass.ds((i * 2 + u) * TILE, TILE)])\
                                      .then_inc(ld_rB[u][h], 16)
                        sp.wait_ge(pick_chain, pick(b, 3))
                        sp.dma_start(cand[:, 8:16], top_half[64:128, :]).then_inc(mv_cand[0], 16)
                        sp.dma_start(cand_idx[:, 8:16], idxf_half[64:128, :]).then_inc(mv_cand[1], 16)
                        sp.wait_ge(pick_chain, pick(b, 15))
                        sp.dma_start(find[64:128, 0:8], lists[:, 8:16]).then_inc(mv_list[0], 16)
                        sp.dma_start(find[64:128, 8:9], lists[:, 16:17]).then_inc(mv_list[1], 16)
                        sp.wait_ge(exp_all, b * 3 + 1)
                        sp.dma_start(zsum2[:], zsum[64:128, :]).then_inc(mv_sum, 16)
                        sp.wait_ge(pick_chain, pick(b, 26))
                        for h in range(2):
                            sp.dma_start(
                                S_dram[bass.ds(b, 1), :, h * HALF:(h + 1) * HALF].rearrange("a e t -> (a e) t"),
                                logits[64 * h:64 * h + 64, 0:HALF]).then_inc(st_S[h], 16)
                    for s, n in ((st_x1, B * half_tiles), (st_xT, B * half_tiles), (st_S, B)):
                        for q in s:
                            sp.wait_ge(q, rounds(n))
                    for q in st_r:
                        sp.wait_ge(q, 32 * B)

                @block.tensor
                def _(pe):
                    t = nc.tensor
                    credit(pe, centred, varied, rb_ready, t_ready, t2_ready, wgt_ready, acc_ready, xT_ready,
                           raw_ready, rb2_ready)
                    with pe.Fori(0, B) as b:
                        def centre(i, u, part):
                            j, p, half = item(i, u, 0)
                            if live(j, TILES):
                                pe.wait_ge(ld_x[p], (b * half_tiles + half + 1) * 16)
                                pe.wait_ge(squared, done(b * TILES + j - 2))
                                t.matmul(centre_ps[p][:], center[:], x_in[p][:], start=True, stop=True)\
                                 .then_inc(centred, 1)
                            j, p, half = item(i, u, 1)
                            if live(j, TILES):
                                pe.wait_ge(squared, done(b * TILES + j))
                                pe.wait_ge(var_kept, done(b * TILES + j - 2))
                                for q in range(ROWS):
                                    mm = t.matmul(var_ps[p][:, q:q + 1], square[p][:, q * 128:q * 128 + 128],
                                                  mean_col[:], start=True, stop=True)
                                mm.then_inc(varied, 1)

                        walk(pe, passed, centre, TILES, 1)
                        pe.wait_ge(split_chain, b * 2 * SPLITS + 1)
                        t.transpose(turn_ps, rstd[:], ident[:]).then_inc(turned, 1)
                        settle(pe, passed)

                        def reduce(i, u, part):
                            j, p, half = item(i, u, 0)
                            if live(j, TILES):
                                pe.wait_ge(ld_rA[p], (b * half_tiles + half + 1) * 16)
                                pe.wait_ge(scaled, done(b * TILES + j - 2))
                                t.matmul(rb_ps[p][:], ones3[:], rA[p][:], start=True, stop=True)\
                                 .then_inc(rb_ready, 1)
                            j, p, half = item(i, u, 1)
                            if live(j, TILES):
                                pe.wait_ge(scaled, done(b * TILES + j))
                                pe.wait_ge(t_counted, done(b * TILES + j - 2))
                                t.matmul(bank[2 + p][:], w1rep[:], inner(j), start=True, stop=True)\
                                 .then_inc(t_ready, 1)

                        walk(pe, passed, reduce, TILES, 1)
                        pe.wait_ge(t_counted, done(b * TILES + TILES - 1))

                        def step(i, u, part):
                            j, p, half = item(i, u, 0)
                            if live(j, TILES):
                                n = b * TILES + j
                                pe.wait_ge(relu_chain, n * 3 - 3 + 3 + CREDIT)
                                t.matmul(t_ps[:], w1rep[:], inner(j), start=True, stop=True).then_inc(t2_ready, 1)
                            j1, p1, half1 = item(i, u, 1)
                            j2, p2, half2 = item(i, u, 2)
                            j3, p3, half3 = item(i, u, 3)
                            if live(j1, TILES):
                                pe.wait_ge(part_chain, (b * TILES + j1) * 2 + 2 + CREDIT * 2)
                            for k in range(TAPS):
                                if live(j1, TILES):
                                    n = b * TILES + j1
                                    pe.wait_ge(mul_done, done(n * TAPS + k - 3))
                                    t.matmul(wgt_ps[k % 3][:], wstack[:, k, :], stack[p1][:], start=True, stop=True)\
                                     .then_inc(wgt_ready, 1)
                                if 3 <= k < 7 and live(j2, TILES):
                                    n = b * TILES + j2
                                    if k == 3:
                                        pe.wait_ge(sum_chain, n * 3 + 3 + CREDIT * 3)
                                        pe.wait_ge(pair_chain, n * 2 + 2 + CREDIT * 2)
                                        pe.wait_ge(x1_ready, done(n - 1))
                                    mm = t.matmul(acc_ps, ident[:], psum_in[k - 3][p2][:], start=(k == 3), stop=(k == 6))
                                    if k == 6:
                                        mm.then_inc(acc_ready, 1)
                                if k == 1 and live(j3, TILES):
                                    n = b * TILES + j3
                                    pe.wait_ge(x1_ready, done(n))
                                    pe.wait_ge(raw_kept, done(n - 1))
                                    h = j3 // half_tiles if isinstance(j3, int) else part
                                    t.matmul(raw_ps[64 * h:64 * h + 64, :], gateT[:], x1[p3][:], start=True, stop=True)\
                                     .then_inc(raw_ready, 1)
                                if k == 2 and live(j3, TILES):
                                    pe.wait_ge(var4_ready, done(b * TILES + j3 - 1))
                                    for q in range(ROWS):
                                        mm = t.matmul(xT_ps[:, q * 128:q * 128 + 128], x1[p3][:, q * 128:q * 128 + 128],
                                                      center[:], start=True, stop=True)
                                    mm.then_inc(xT_ready, 1)

                        walk(pe, passed, step, TILES, 3, parts=2)
                        pe.wait_ge(split_chain, (b * 2 + 1) * SPLITS + 1)
                        t.transpose(turn_ps, rstd[:], ident[:]).then_inc(turned2, 1)
                        settle(pe, passed)
                        with pe.Fori(0, half_tiles // 2) as i:
                            for u in range(2):
                                n = b * half_tiles + i * 2 + u
                                for h in range(2):
                                    pe.wait_ge(ld_rB[u][h], (b * (half_tiles // 2) + i + 1) * 16)
                                pe.wait_ge(normed, done(n - 2))
                                t.matmul(rb_ps[u][:], sel6[:], rB[u][:], start=True, stop=True)\
                                 .then_inc(rb2_ready, 1)
                        pe.wait_ge(pick_chain, pick(b, PICKS))
                        settle(pe, passed)
                        t.transpose(pool_ps, pooled[:], ident[0:E0, 0:E0]).then_inc(pool_turned, 1)

                @block.scalar
                def _(act):
                    a = nc.scalar
                    credit(act, squared, raw_kept, xT_kept, var4_ready, mid_ready)
                    act.sem_inc(relu_chain, CREDIT)
                    with act.Fori(0, B) as b:
                        act.wait_ge(mul_done, done(b * TILES * TAPS - 1))
                        act.wait_ge(border, 2)
                        settle(act, passed)
                        with act.Fori(0, half_tiles) as i:
                            for u in range(2):
                                n = b * TILES + i * 2 + u
                                act.wait_ge(centred, done(n))
                                a.activation(inner(i * 2 + u), grid(centre_ps[u][:]), ACT.Copy)
                                act.wait_ge(varied, done(n - 2))
                                a.activation(square[u][:], centre_ps[u][:], ACT.Square).then_inc(squared, 1)
                        act.wait_ge(var_kept, done(b * TILES + TILES - 1))
                        a.activation(std[:], var_all[:], ACT.Sqrt, bias=eps6[:]).then_inc(std_ready, 1)
                        act.wait_ge(norm_chain, b * NORMS + 1)
                        a.activation(t_tmp[:, 0:1], t_mv[:, 1:2], ACT.Sqrt, bias=eps5[:]).then_inc(norm_std, 1)
                        act.wait_ge(norm_chain, b * NORMS + NORMS)
                        act.wait_ge(st_S[0], rounds(b))
                        act.wait_ge(st_S[1], rounds(b))

                        def step(i, u, part):
                            j, p, half = item(i, u, 0)
                            if live(j, TILES):
                                n = b * TILES + j
                                r0 = n * 3 + CREDIT
                                act.wait_ge(t2_ready, done(n))
                                act.wait_ge(wgt_ready, done(n * TAPS - TAPS - 1))
                                a.activation(stack[p][0:64, :], t_ps[0:64, :], ACT.Relu, scale=t_scale[0:64, :],
                                             bias=t_bias[0:64, :]).then_inc(relu_chain, 1)
                                a.activation(t_full[p][64:128, :], t_ps[64:128, :], ACT.Relu,
                                             scale=t_scale[64:128, :], bias=t_bias[64:128, :])\
                                 .then_inc(relu_chain, 1)
                                act.wait_ge(relu_chain, r0 + 2)
                                a.activation(t_high[p][64:128, :], t_full[p][64:128, :], ACT.Copy)\
                                 .then_inc(relu_chain, 1)
                                act.wait_ge(part_chain, n * 2 + 1 + CREDIT * 2)
                                a.activation(stack[p][64:128, :], t_rest[p][64:128, :], ACT.Copy)\
                                 .then_inc(mid_ready, 1)
                            j3, p3, half3 = item(i, u, 3)
                            if live(j3, TILES):
                                n = b * TILES + j3
                                h = j3 // half_tiles if isinstance(j3, int) else part
                                act.wait_ge(raw_ready, done(n))
                                a.activation(
                                    logits[64 * h:64 * h + 64, bass.ds((j3 - h * half_tiles) * TILE, TILE)],
                                    raw_ps[64 * h:64 * h + 64, :], ACT.Copy).then_inc(raw_kept, 1)
                                act.wait_ge(xT_ready, done(n))
                                act.wait_ge(st_xT[p3], rounds(b * half_tiles + half3))
                                a.activation(x1T[p3][:], xT_ps.rearrange("p (q c) -> p q c", q=ROWS), ACT.Copy)\
                                 .then_inc(xT_kept, 1)
                                act.wait_ge(var4_kept, done(n - 2))
                                for q in range(ROWS):
                                    ins = a.activation(sq_junk[:, q, :], xT_ps[:, q * 128:q * 128 + 128], ACT.Square,
                                                       accum_out=var4[p3][:, q:q + 1])
                                ins.then_inc(var4_ready, 1)

                        walk(act, passed, step, TILES, 3, parts=2)
                        act.wait_ge(var4_kept, done(b * TILES + TILES - 1))
                        a.activation(std[:], var_all[:], ACT.Sqrt, bias=eps5[:], scale=1.0 / C)\
                         .then_inc(std2_ready, 1)
                        act.wait_ge(pick_chain, pick(b, 18))
                        a.activation(logits[:, 0:HALF], logits[:, 0:HALF], ACT.Exp, bias=find[:, 8:9],
                                     accum_out=zsum[:]).then_inc(exp_all, 1)
                        a.activation(top_exp[:], top[:], ACT.Exp, bias=find[0:E0, 8:9]).then_inc(exp_all, 1)
                        act.wait_ge(pick_chain, pick(b, 28))
                        a.activation(row_std[:], row_var[:], ACT.Sqrt, bias=eps5[0:E0, :], scale=1.0 / C)\
                         .then_inc(exp_all, 1)

                @block.gpsimd
                def _(pool):
                    g = nc.gpsimd
                    pool.sem_inc(part_chain, CREDIT * 2)
                    pool.sem_inc(sum_chain, CREDIT * 3)
                    with pool.Fori(0, B) as b:
                        def step(i, u, part):
                            j, p, half = item(i, u, 0)
                            if live(j, TILES):
                                n = b * TILES + j
                                pool.wait_ge(relu_chain, n * 3 + 3 + CREDIT)
                                g.tensor_tensor(t_rest[p][64:128, :], t_full[p][64:128, :], t_high[p][64:128, :],
                                                ALU.subtract).then_inc(part_chain, 1)
                                pool.wait_ge(mid_ready, done(n))
                                g.tensor_tensor(stack[p][96:128, :], t_rest[p][96:128, :], stack[p][96:128, :],
                                                ALU.subtract).then_inc(part_chain, 1)
                                pool.wait_ge(part_chain, n * 2 + 2 + CREDIT * 2)
                            j, p, half = item(i, u, 1)
                            if live(j, TILES):
                                n = b * TILES + j
                                pool.wait_ge(acc_ready, done(n - 2))
                                for k in range(3):
                                    pool.wait_ge(mul_done, done(n * TAPS + 2 * k + 1))
                                    g.tensor_tensor(psum_in[k][p][:], prod[2 * k], prod[2 * k + 1], ALU.add)\
                                     .then_inc(sum_chain, 1)
                                pool.wait_ge(sum_chain, n * 3 + 3 + CREDIT * 3)

                        walk(pool, passed, step, TILES, 1)
                        for u in range(2):
                            pool.wait_ge(st_xT[u], rounds((b + 1) * half_tiles))
                        pool.wait_ge(pick_chain, pick(b, 23))
                        settle(pool, passed)
                        for k in range(K0):
                            g.indirect_dma_start(rows[:, k, :], None, xT_dram[:, :],
                                                 bass.IndirectOffsetOnAxis(ap=token[:, k:k + 1], axis=0))\
                             .then_inc(ld_rows[k], 16)

                @block.vector
                def _(dve):
                    v = nc.vector
                    credit(dve, var_kept, scaled, t_counted, mul_done, x1_ready, var4_kept, normed)
                    dve.sem_inc(pair_chain, CREDIT * 2)
                    dve.sem_inc(pick_chain, 1)
                    v.memset(xn[:], 0.0).then_inc(border, 1)
                    v.memset(logits[:, HALF:HALF + 8], NEG).then_inc(border, 1)

                    def split_r(link, turned_sem, b):
                        link(v.reciprocal(rstd[:], std[:]))
                        dve.wait_ge(turned_sem, b + 1)
                        link(v.tensor_copy(r_rest[:], turn_ps))
                        link(v.tensor_copy(r_part[0][:], r_rest[:]))
                        link(v.tensor_tensor(r_rest[:], r_rest[:], r_part[0][:], ALU.subtract))
                        link(v.tensor_copy(r_part[1][:], r_rest[:]))
                        link(v.tensor_tensor(r_part[2][:], r_rest[:], r_part[1][:], ALU.subtract))
                        assert link.n == SPLITS

                    with dve.Fori(0, B) as b:
                        with dve.Fori(0, half_tiles) as i:
                            for u in range(2):
                                dve.wait_ge(varied, done(b * TILES + i * 2 + u))
                                v.tensor_copy(var_all[:, bass.ds((i * 2 + u) * ROWS, ROWS)], var_ps[u])\
                                 .then_inc(var_kept, 1)
                        dve.wait_ge(std_ready, b + 1)
                        split_r(Chain(dve, split_chain, b * 2 * SPLITS), turned, b)
                        settle(dve, passed)

                        def reduce(i, u, part):
                            j, p, half = item(i, u, 0)
                            if live(j, TILES):
                                dve.wait_ge(rb_ready, done(b * TILES + j))
                                v.tensor_tensor(inner(j), inner(j), grid(rb_ps[p][:]), ALU.mult).then_inc(scaled, 1)
                            j, p, half = item(i, u, 1)
                            if live(j, TILES):
                                dve.wait_ge(t_ready, done(b * TILES + j))
                                v.bn_stats(t_stats[:, bass.ds(j * 6, 6)], bank[2 + p][:]).then_inc(t_counted, 1)

                        walk(dve, passed, reduce, TILES, 1)
                        dve.wait_ge(t_counted, done(b * TILES + TILES - 1))
                        dve.wait_ge(border, 2)
                        link = Chain(dve, norm_chain, b * NORMS)
                        settle(dve, passed)
                        link(v.bn_aggr(t_mv[:], t_stats[:]))
                        dve.wait_ge(norm_std, b + 1)
                        link(v.reciprocal(t_tmp[:, 1:2], t_tmp[:, 0:1]))
                        link(v.tensor_tensor(t_scale[:], t_tmp[:, 1:2], gamma_rep[:], ALU.mult))
                        link(v.tensor_tensor(t_tmp[:, 1:2], t_mv[:, 0:1], t_scale[:], ALU.mult))
                        link(v.tensor_tensor(t_bias[:], beta_rep[:], t_tmp[:, 1:2], ALU.subtract))
                        assert link.n == NORMS

                        def step(i, u, part):
                            j, p, half = item(i, u, 1)
                            if live(j, TILES):
                                n = b * TILES + j
                                for k in range(TAPS):
                                    dve.wait_ge(wgt_ready, done(n * TAPS + k))
                                    if k < 6:
                                        dve.wait_ge(sum_chain, n * 3 - 2 + k // 2 + CREDIT * 3)
                                    elif k == 6:
                                        dve.wait_ge(pair_chain, n * 2 + CREDIT * 2)
                                    v.tensor_tensor(
                                        grid(prod[k]), grid(wgt_ps[k % 3][:]),
                                        xn[:, bass.ds(j * ROWS + 2 * (k // 3), ROWS), 2 * (k % 3):2 * (k % 3) + W],
                                        ALU.mult).then_inc(mul_done, 1)
                                dve.wait_ge(mul_done, done(n * TAPS + 7))
                                v.tensor_tensor(prod[6], prod[6], prod[7], ALU.add).then_inc(pair_chain, 1)
                                dve.wait_ge(pair_chain, n * 2 + 1 + CREDIT * 2)
                                dve.wait_ge(mul_done, done(n * TAPS + 8))
                                dve.wait_ge(acc_ready, done(n - 2))
                                v.tensor_tensor(psum_in[3][p][:], prod[6], prod[8], ALU.add)\
                                 .then_inc(pair_chain, 1)
                            j, p, half = item(i, u, 2)
                            if live(j, TILES):
                                n = b * TILES + j
                                dve.wait_ge(acc_ready, done(n))
                                dve.wait_ge(ld_res[p], (b * half_tiles + half + 1) * 16)
                                dve.wait_ge(st_x1[p], rounds(b * half_tiles + half))
                                dve.wait_ge(xT_ready, done(n - 2))
                                v.tensor_tensor(x1[p][:], acc_ps, x_res[p][:], ALU.add).then_inc(x1_ready, 1)
                            j, p, half = item(i, u, 3)
                            if live(j, TILES):
                                n = b * TILES + j
                                dve.wait_ge(var4_ready, done(n))
                                v.tensor_copy(var_all[:, bass.ds(j * ROWS, ROWS)], var4[p][:]).then_inc(var4_kept, 1)

                        walk(dve, passed, step, TILES, 3, parts=2)
                        dve.wait_ge(std2_ready, b + 1)
                        split_r(Chain(dve, split_chain, (b * 2 + 1) * SPLITS), turned2, b)
                        dve.wait_ge(raw_kept, done(b * TILES + TILES - 1))
                        settle(dve, passed)
                        with dve.Fori(0, half_tiles // 2) as i:
                            for u in range(2):
                                at = bass.ds((i * 2 + u) * TILE, TILE)
                                dve.wait_ge(rb2_ready, done(b * half_tiles + i * 2 + u))
                                v.tensor_tensor(logits[:, at], logits[:, at], rb_ps[u][:], ALU.mult)\
                                 .then_inc(normed, 1)
                        dve.wait_ge(normed, done(b * half_tiles + half_tiles - 1))
                        link = Chain(dve, pick_chain, pick(b, 0))
                        dve.wait_ge(border, 2)
                        settle(dve, passed)
                        link(v.max(top_half[:], logits[:]))
                        settle(dve, passed)
                        link(v.max_index(idx_half[:], top_half[:], logits[:]))
                        link(v.tensor_copy(idxf_half[:], idx_half[:]))
                        link(v.tensor_copy(cand[:, 0:8], top_half[0:64, :]))
                        link(v.tensor_copy(cand_idx[:, 0:8], idxf_half[0:64, :]))
                        dve.wait_ge(mv_cand[0], b * 16 + 16)
                        dve.wait_ge(mv_cand[1], b * 16 + 16)
                        link(v.tensor_scalar(cand_idx[:, 8:16], cand_idx[:, 8:16], float(HALF), None, ALU.add))
                        settle(dve, passed)
                        link(v.max(top[:], cand[:]))
                        settle(dve, passed)
                        link(v.max_index(pos[:], top[:], cand[:]))
                        settle(dve, passed)
                        link(v.match_replace(cand_mark[:], top[:], cand[:], BIG))
                        link(v.tensor_scalar(kept[:], cand_mark[:], BIG, None, ALU.is_equal))
                        link(v.tensor_tensor(kept2[:], kept[:], cand[:], ALU.mult))
                        link(v.tensor_scalar(kept[:], kept[:], -1.0, -NEG, ALU.add, ALU.mult))
                        link(v.tensor_tensor(lists[:, 0:16], kept2[:], kept[:], ALU.add))
                        link(v.tensor_tensor(zinv[:], top[:, 0:1], gate_bias[:], ALU.add))
                        link(v.tensor_tensor(lists[:, 16:17], gate_bias[:], zinv[:], ALU.subtract))
                        link(v.tensor_copy(find[0:E0, 0:8], lists[:, 0:8]))
                        link(v.tensor_copy(find[0:E0, 8:9], lists[:, 16:17]))
                        dve.wait_ge(mv_list[0], b * 16 + 16)
                        dve.wait_ge(mv_list[1], b * 16 + 16)
                        settle(dve, passed)
                        link(v.match_replace(picked[:], find[:, 0:8], logits[:], BIG))
                        link(v.tensor_copy(posf[:], pos[:]))
                        link(v.tensor_tensor(token_eq[:], slots16[:].unsqueeze(1).to_broadcast([E0, K0, 16]),
                                             posf[:].unsqueeze(2).to_broadcast([E0, K0, 16]), ALU.is_equal))
                        link(v.tensor_tensor(token_eq[:], token_eq[:],
                                             cand_idx[:].unsqueeze(1).to_broadcast([E0, K0, 16]), ALU.mult))
                        link(v.tensor_reduce(token_f[:], token_eq[:], AX_X, ALU.add))
                        link(v.tensor_copy(token[:], token_f[:]))
                        dve.wait_ge(mv_sum, b * 16 + 16)
                        dve.wait_ge(exp_all, b * 3 + 2)
                        link(v.tensor_tensor(zinv[:], zsum[0:E0, :], zsum2[:], ALU.add))
                        link(v.reciprocal(rsum_b[:], zinv[:]))
                        link(v.scalar_tensor_tensor(out=logits[:, 0:HALF], in0=picked[:, 0:HALF], scalar=BIG,
                                                    in1=logits[:, 0:HALF], op0=ALU.is_equal, op1=ALU.mult))
                        for k in range(K0 - 1):
                            dve.wait_ge(ld_rows[k], b * 16 + 16)
                        dve.wait_ge(ld_rows[K0 - 1], b * 16 + 16)
                        link(v.tensor_tensor(rows_sq, rows, rows, ALU.mult))
                        link(v.tensor_reduce(row_var[:], rows_sq, AX_X, ALU.add))
                        dve.wait_ge(exp_all, b * 3 + 3)
                        link(v.reciprocal(row_w[:], row_std[:]))
                        link(v.tensor_tensor(row_w[:], row_w[:], top_exp[:], ALU.mult))
                        link(v.tensor_scalar(row_w[:], row_w[:], rsum_b[:], None, ALU.mult))
                        link(v.tensor_copy(rsum_all[:, bass.ds(b, 1)], rsum_b[:]))
                        link(v.tensor_tensor(rows, rows, row_w[:].unsqueeze(2).to_broadcast([E0, K0, C]),
                                             ALU.mult))
                        link(v.tensor_reduce(pooled[:], rows.rearrange("e k c -> e c k"), AX_X, ALU.add))
                        assert link.n == PICKS
                        dve.wait_ge(pool_turned, b + 1)
                        v.tensor_copy(pooledT[:, bass.ds(b, 1), :], pool_ps.unsqueeze(1)).then_inc(pool_kept, 1)
                        dve.wait_ge(pool_kept, b + 1)
        with ExitStack() as tmp:
            def tb(name, shape, dt=F32):
                return tmp.enter_context(nc.sbuf_tensor(name, shape, dt))

            def pair(name, shape, dt=F32):
                return [tb(f"{name}{u}", shape, dt) for u in range(2)]

            def nsem(name):
                return tmp.enter_context(nc.semaphore(name))

            HC = HID // 128
            first_w = [tb(f"first_w{u}", [128, HID]) for u in range(4)]
            second_w = [tb(f"second_w{u}", [128, HC, C]) for u in range(4)]
            first_b = tb("first_b", [E0, HID])
            second_b = tb("second_b", [E0, C])
            first_bT = tb("first_bT", [128, E0, HC])
            second_bT = tb("second_bT", [128, E0])
            hid = pair("hid", [128, HC, B])
            act_hid = pair("act_hid", [128, HC, B])
            ld_b = nsem("ld_b")
            ld_w = [[nsem(f"ld_w{u}{k}") for k in range(2)] for u in range(4)]
            bias_turned = nsem("bias_turned")
            bias_kept = nsem("bias_kept")
            hid_ready = nsem("hid_ready")
            hid_biased = nsem("hid_biased")
            hid_act = nsem("hid_act")
            moe_ready = nsem("moe_ready")
            moe_kept = nsem("moe_kept")
            hid_ps = [bank[u][:, 0:HC * B].rearrange("p (c b) -> p c b", b=B) for u in range(2)]
            moe_ps = [bank[2 + u][:, 0:B] for u in range(2)]

            with nc.Block() as block:
                @block.sync
                def _(sp):
                    sp.dma_start(first_b[:], ew1[:, C, :]).then_inc(ld_b, 16)
                    sp.dma_start(second_b[:], ew2[:, HID, :]).then_inc(ld_b, 16)
                    with sp.Fori(0, E0 // 4) as i:
                        for u in range(4):
                            sp.wait_ge(moe_ready, done(i * 4 + u - 4))
                            sp.dma_start(first_w[u][:], ew1[bass.ds(i * 4 + u, 1), 0:C, :]
                                         .rearrange("a d h -> (a d) h")).then_inc(ld_w[u][0], 16)
                            sp.dma_start(second_w[u][:], ew2[bass.ds(i * 4 + u, 1), 0:HID, :]
                                         .rearrange("a (p c) o -> (a p) c o", c=HC)).then_inc(ld_w[u][1], 16)

                @block.tensor
                def _(pe):
                    t = nc.tensor
                    credit(pe, hid_ready, moe_ready)
                    pe.wait_ge(ld_b, 32)
                    for c in range(HC):
                        if c >= 2:
                            pe.wait_ge(bias_kept, c - 1)
                        t.transpose(bank[c % 2][:, 0:E0], first_b[:, c:HID:HC], ident[0:E0, 0:E0])\
                         .then_inc(bias_turned, 1)
                    pe.wait_ge(bias_kept, HC - 1)
                    t.transpose(bank[0][:, 0:E0], second_b[:], ident[0:E0, 0:E0]).then_inc(bias_turned, 1)
                    pe.wait_ge(bias_kept, HC + 1)

                    def four(i):
                        for u in range(4):
                            for lag, n in ((0, i * 4 + u), (1, i * 4 + u - 1)):
                                if not live(n, E0):
                                    continue
                                w, p = (u - lag) % 4, (u - lag) % 2
                                if lag == 0:
                                    for k in range(2):
                                        pe.wait_ge(ld_w[w][k], (i + 1) * 16)
                                    pe.wait_ge(hid_biased, done(n - 2))
                                    for c in range(HC):
                                        mm = t.matmul(hid_ps[p][:, c, :], first_w[w][:, c:HID:HC],
                                                      pooledT[:, :, bass.ds(n, 1)].rearrange("p b a -> p (b a)"),
                                                      start=True, stop=True)
                                    mm.then_inc(hid_ready, 1)
                                else:
                                    pe.wait_ge(hid_act, done(n))
                                    pe.wait_ge(moe_kept, done(n - 2))
                                    for c in range(HC):
                                        mm = t.matmul(moe_ps[p], second_w[w][:, c, :], act_hid[p][:, c, :],
                                                      start=(c == 0), stop=(c == HC - 1))
                                    mm.then_inc(moe_ready, 1)

                    four(0)
                    with pe.Fori(1, E0 // 4) as i:
                        four(i)
                    pe.wait_ge(hid_act, done(E0 - 1))
                    pe.wait_ge(moe_kept, done(E0 - 3))
                    for c in range(HC):
                        mm = t.matmul(moe_ps[1], second_w[3][:, c, :], act_hid[1][:, c, :],
                                      start=(c == 0), stop=(c == HC - 1))
                    mm.then_inc(moe_ready, 1)

                @block.scalar
                def _(act):
                    credit(act, hid_act)
                    with act.Fori(0, E0 // 2) as i:
                        for u in range(2):
                            n = i * 2 + u
                            act.wait_ge(hid_biased, done(n))
                            act.wait_ge(moe_ready, done(n - 2))
                            nc.scalar.activation(act_hid[u][:], hid[u][:], ACT.Gelu).then_inc(hid_act, 1)

                @block.vector
                def _(dve):
                    v = nc.vector
                    credit(dve, hid_biased, moe_kept)
                    for c in range(HC):
                        dve.wait_ge(bias_turned, c + 1)
                        v.tensor_copy(first_bT[:, :, c:c + 1], bank[c % 2][:, 0:E0].unsqueeze(2)).then_inc(bias_kept, 1)
                    dve.wait_ge(bias_turned, HC + 1)
                    v.tensor_copy(second_bT[:], bank[0][:, 0:E0]).then_inc(bias_kept, 1)
                    dve.wait_ge(bias_kept, HC + 1)

                    def step(i, u, part):
                        j, p, half = item(i, u, 0)
                        if live(j, E0):
                            dve.wait_ge(hid_ready, done(j))
                            dve.wait_ge(hid_act, done(j - 2))
                            v.tensor_tensor(hid[p][:], hid_ps[p],
                                            first_bT[:, bass.ds(j, 1), :].rearrange("p a c -> p (a c)")
                                            .unsqueeze(2).to_broadcast([128, HC, B]), ALU.add)\
                             .then_inc(hid_biased, 1)
                        j, p, half = item(i, u, 1)
                        if live(j, E0):
                            dve.wait_ge(moe_ready, done(j))
                            v.tensor_tensor(moeT[:, bass.ds(j, 1), :].rearrange("p a b -> p (a b)"), moe_ps[p],
                                            second_bT[:, bass.ds(j, 1)].to_broadcast([128, B]), ALU.add)\
                             .then_inc(moe_kept, 1)

                    walk(dve, passed, step, E0, 1)
                    dve.wait_ge(moe_kept, done(E0 - 1))
        with ExitStack() as tmp:
            def tb(name, shape, dt=F32):
                return tmp.enter_context(nc.sbuf_tensor(name, shape, dt))

            def pair(name, shape, dt=F32):
                return [tb(f"{name}{u}", shape, dt) for u in range(2)]

            def nsem(name):
                return tmp.enter_context(nc.semaphore(name))

            experts = tb("experts", [128, E1, 128])
            img = tb("img", [128, H, C])
            moe_b = tb("moe_b", [128, E0])
            moe_w = tb("moe_w", [E0, C])
            rs_b = tb("rs_b", [E0, 1])
            x1_in = pair("x1_in", [128, TILE])
            S_in = pair("S_in", [E0, TILE])
            x2 = pair("x2", [128, TILE])
            stat4 = pair("stat4", [128, ROWS, 6])
            mv4 = pair("mv4", [128, ROWS, 2])
            mv_all = tb("mv_all", [128, H, 2])
            std_all = tb("std_all", [128, H])
            rstd_all = tb("rstd_all", [128, H])
            bias_g = pair("bias_g", [128, GC])
            brem_g = pair("brem_g", [RP, 1])
            grp = pair("grp", [128, GC, H])
            upc = pair("upc", [128, GC, UPN])
            act_in = pair("act_in", [128, GC, 2, UPN])
            upc_rem = pair("upc_rem", [128, RP])
            act_rem = pair("act_rem", [128, 2, RP])
            rem_in = pair("rem_in", [RP, UPN])
            rem_blk = pair("rem_blk", [RP, GC, REM])
            dnc = pair("dnc", [128, 2, GC, W])
            rem_dn = pair("rem_dn", [RP, W])
            tok = pair("tok", [128, OCTET, C])
            stat8 = tb("stat8", [128, OCTET, 6])
            mv8 = tb("mv8", [128, OCTET, 2])
            std8 = tb("std8", [128, OCTET])
            rstd8 = pair("rstd8", [128, OCTET])
            xh = pair("xh", [128, 2, TILE])
            lg = pair("lg", [128, OCTET, E1])
            mx = tb("mx", [128, OCTET])
            prb = pair("prb", [128, OCTET, E1])
            pr2 = tb("pr2", [128, OCTET, E1])
            sm = tb("sm", [128, OCTET])
            eq = tb("eq", [128, OCTET, E1])
            first = tb("first", [128, OCTET, E1])
            second = tb("second", [128, OCTET, E1])
            p1 = tb("p1", [128, OCTET])
            p2 = tb("p2", [128, OCTET])
            gate = pair("gate", [128, OCTET, E1])
            gate_std = pair("gate_std", [128, OCTET, E1])
            gateTs = pair("gateTs", [ROWS * E1, 2, 128])
            acc = [t[:].rearrange("p (q c) -> p q c", q=ROWS) for t in x2]
            ya = [t[:].rearrange("p q (a c) w -> p (q a) c w", a=2) for t in dnc]
            ys = pair("ys", [128, ROWS, C])
            res = pair("res", [128, TILE])

            blocks = TILES
            octets = TILES // 2
            ht = TILES // 2
            moe_got = nsem("moe_got")
            moe_turned = nsem("moe_turned")
            moe_scaled = nsem("moe_scaled")
            ld_experts = nsem("ld_experts")
            w_centred = nsem("w_centred")
            w_kept = nsem("w_kept")
            ld_x1 = [nsem(f"ld_x1{u}") for u in range(2)]
            ld_S = [nsem(f"ld_S{u}") for u in range(2)]
            add_ready = nsem("add_ready")
            x2_ready = nsem("x2_ready")
            img_turned = nsem("img_turned")
            img_kept = nsem("img_kept")
            stat_chain = nsem("stat_chain")
            mv_std = nsem("mv_std")
            mv_rstd = nsem("mv_rstd")
            grp_chain = nsem("grp_chain")
            bias_got = nsem("bias_got")
            up1_ready = nsem("up1_ready")
            up1_kept = nsem("up1_kept")
            up2_ready = nsem("up2_ready")
            up2_kept = nsem("up2_kept")
            leaky = nsem("leaky")
            rem_ready = nsem("rem_ready")
            down_ready = nsem("down_ready")
            down_kept = nsem("down_kept")
            conv_added = nsem("conv_added")
            mv_tok = [nsem(f"mv_tok{u}") for u in range(2)]
            tok_turned = nsem("tok_turned")
            xh_ready = nsem("xh_ready")
            stat8_chain = nsem("stat8_chain")
            std8_ready = nsem("std8_ready")
            lg_ready = nsem("lg_ready")
            route = nsem("route")
            exp_ready = nsem("exp_ready")
            gate_turned = nsem("gate_turned")
            gate_kept = nsem("gate_kept")
            exp_out = nsem("exp_out")
            act_part = nsem("act_part")
            dve_part = nsem("dve_part")
            y_chain = nsem("y_chain")
            acc_done = nsem("acc_done")
            out_ready = nsem("out_ready")
            out_kept = nsem("out_kept")
            st_out = [nsem(f"st_out{u}") for u in range(2)]

            ROUTES = 25
            ROUTE0 = 2 * CREDIT
            add_ps = bank[0:2]
            turn_ps = bank[2:4]
            up1_ps = bank[0:2]
            up2_ps = duo
            down_ps = bank[2:4]
            tok_ps = bank[0:2]
            lg_ps = bank[2][:, 0:OCTET * E1].rearrange("p (q e) -> p q e", e=E1)
            gT_ps = bank[2][0:ROWS * E1, 128:384].rearrange("p (k t) -> p k t", k=2)
            out_ps = bank[3]
            exp_ps = duo

            def rows_of(j):
                return bass.ds(j * ROWS, ROWS)

            def chan(ap, c0, n):
                return ap[:, :, bass.ds(c0, n)].rearrange("p h c -> p c h")

            def groups_of(eng, up, down):
                up(0, 0)
                up(1, 1)
                down(0, 0)
                settle(eng, passed)
                with eng.Fori(1, GROUPS // 2) as i:
                    up(i * 2, 0)
                    down(i * 2 - 1, 1)
                    up(i * 2 + 1, 1)
                    down(i * 2, 0)
                down(GROUPS - 1, 1)

            with nc.Block() as block:
                @block.sync
                def _(sp):
                    for s in st_out:
                        sp.sem_inc(s, 16)
                    sp.dma_start(experts[:], expert_w.rearrange("e d c -> d e c")).then_inc(ld_experts, 16)
                    with sp.Fori(0, B) as b:
                        with sp.Fori(0, ht) as i:
                            for u in range(2):
                                j = i * 2 + u
                                n = b * TILES + j
                                sp.wait_ge(x2_ready, done(n - 2))
                                sp.dma_start(x1_in[u][:].rearrange("p (h w) -> p h w", w=W),
                                             x1_dram[bass.ds(b, 1), :, rows_of(j), :]
                                             .rearrange("a c h w -> (a c) h w")).then_inc(ld_x1[u], 16)
                                sp.wait_ge(add_ready, done(n - 2))
                                sp.dma_start(S_in[u][:],
                                             S_dram[bass.ds(b, 1), :, bass.ds(j * TILE, TILE)]
                                             .rearrange("a e t -> (a e) t")).then_inc(ld_S[u], 16)
                        settle(sp, passed)
                        sp.wait_ge(conv_added, done(b * 2 * GROUPS + 2 * GROUPS - 1))

                        def step(i, u, part):
                            j, p, half = item(i, u, 0)
                            if live(j, octets):
                                sp.wait_ge(tok_turned, done((b * octets + j) * 2 - 3))
                                sp.dma_start(tok[p][:], img[:, bass.ds(j * OCTET, OCTET), :]).then_inc(mv_tok[p], 16)
                            for lag, k in ((3, 1), (2, 0)):
                                j, p, half = item(i, u, lag)
                                if live(j, octets):
                                    sp.wait_ge(out_kept, done((b * octets + j) * 2 + k))
                                    sp.dma_start(
                                        out[bass.ds(b, 1), :, bass.ds(j * OCTET + k * ROWS, ROWS), :]
                                        .rearrange("a c h w -> (a c) h w"),
                                        res[k][:].rearrange("p (h w) -> p h w", w=W)).then_inc(st_out[k], 16)

                        walk(sp, passed, step, octets, 3)
                    for s in st_out:
                        sp.wait_ge(s, rounds(B * ht))

                @block.tensor
                def _(pe):
                    t = nc.tensor
                    credit(pe, add_ready, img_turned, up1_ready, up2_ready, down_ready, tok_turned, lg_ready,
                           gate_turned, exp_out, out_ready)
                    pe.wait_ge(ld_experts, 16)
                    for h in range(2):
                        t.matmul(bank[h][:], center[:],
                                 experts[:, 4 * h:4 * h + 4, :].rearrange("d e c -> d (e c)"),
                                 start=True, stop=True).then_inc(w_centred, 1)
                    t.matmul(bank[2][:, 0:E1], center[:], router[:], start=True, stop=True).then_inc(w_centred, 1)
                    pe.wait_ge(w_kept, 3)
                    with pe.Fori(0, B) as b:
                        pe.wait_ge(moe_got, b * 2 + 2)
                        settle(pe, passed)
                        t.transpose(turn_ps[0][0:E0, 0:128], moe_b[:], ident[:]).then_inc(moe_turned, 1)
                        pe.wait_ge(moe_scaled, b + 1)
                        settle(pe, passed)

                        def add(i, u, part):
                            j, p, half = item(i, u, 0)
                            if live(j, TILES):
                                pe.wait_ge(ld_S[p], (b * ht + half + 1) * 16)
                                pe.wait_ge(x2_ready, done(b * TILES + j - 2))
                                t.matmul(add_ps[p][:], moe_w[:], S_in[p][:], start=True, stop=True)\
                                 .then_inc(add_ready, 1)
                            j, p, half = item(i, u, 1)
                            if live(j, TILES):
                                pe.wait_ge(x2_ready, done(b * TILES + j))
                                pe.wait_ge(img_kept, done(b * TILES + j - 2))
                                for q in range(ROWS):
                                    mm = t.transpose(turn_ps[p][:, q * 128:q * 128 + 128],
                                                     x2[p][:, q * 128:q * 128 + 128], ident[:])
                                mm.then_inc(img_turned, 1)

                        walk(pe, passed, add, TILES, 1)

                        def up(g, p):
                            G = b * GROUPS + g
                            pe.wait_ge(grp_chain, G * 2 + 2 + CREDIT * 2)
                            for c in range(GC + 1):
                                if c < GC:
                                    n = G * GC + c
                                    pe.wait_ge(up1_kept, done(n - 2))
                                    t.matmul(up1_ps[c % 2][:, 0:UPN], grp[p][:, c, :], up_mat[:],
                                             start=True, stop=True).then_inc(up1_ready, 1)
                                if c >= 1:
                                    second_up(G, p, c - 1)
                            second_up(G, p, GC)

                        def second_up(G, p, c):
                            n = G * (GC + 1) + c
                            bankp = (p + c) % 2
                            pe.wait_ge(up2_kept, done(n - 2))
                            if c < GC:
                                pe.wait_ge(up1_kept, done(G * GC + c))
                                for m in range(2):
                                    mm = t.matmul(up2_ps[bankp][:, m, 0:UPN], upc[p][:, c, m * 128:m * 128 + 128],
                                                  up_mat[:], start=True, stop=True)
                            else:
                                pe.wait_ge(rem_ready, G * 3 + 1 + CREDIT * 3)
                                mm = t.matmul(up2_ps[bankp][0:RP, 0, 0:UPN], upc_rem[p][:], up_mat[:],
                                              start=True, stop=True)
                            mm.then_inc(up2_ready, 1)

                        def down(g, p):
                            G = b * GROUPS + g
                            pe.wait_ge(leaky, done(G * (GC + 1) + GC))
                            for k in range(4):
                                m, h = k // 2, k % 2
                                n = G * 7 + k
                                ps = down_ps[(p + k) % 2]
                                drain(G, k)
                                for c in range(4):
                                    ch = 4 * h + c
                                    for q in range(2):
                                        t.matmul(ps[:, c * 128:c * 128 + 128], act_in[p][:, ch, q, m * 128:m * 128 + 128],
                                                 down_mat[:, q, :], start=(c == 0 and q == 0), stop=False,
                                                 skip_group_check=True)
                                mm = t.matmul(ps[:].rearrange("p (c w) -> p c w", w=W)[:, :, W - EDGE:W],
                                              rem_in[p][:, m * 128:m * 128 + 128], down_edge[:, 4 * h:4 * h + 4, :],
                                              start=False, stop=True, skip_group_check=True)
                                mm.then_inc(down_ready, 1)
                            pe.wait_ge(rem_ready, G * 3 + 3 + CREDIT * 3)
                            drain(G, 4)
                            ps = down_ps[p]
                            for q in range(2):
                                t.matmul(ps[0:RP, 0:W], act_rem[p][:, q, :], down_mat[:, q, :],
                                         start=(q == 0), stop=False, skip_group_check=True)
                            t.matmul(ps[0:RP, W - EDGE:W], rem_blk[p][:].rearrange("p c r -> p (c r)"), down_edge1[:],
                                     start=False, stop=True, skip_group_check=True).then_inc(down_ready, 1)
                            pe.wait_ge(down_kept, done(G * 5 + 4))
                            for h in range(2):
                                drain(G, 5 + h)
                                ps = down_ps[(p + 5 + h) % 2]
                                for c in range(4):
                                    for q in range(2):
                                        t.matmul(ps[:, c * 128:c * 128 + 128], dnc[p][:, q, 4 * h + c, :],
                                                 down_mat[:, q, :], start=(c == 0 and q == 0), stop=False,
                                                 skip_group_check=True)
                                t.matmul(ps[:].rearrange("p (c w) -> p c w", w=W)[:, :, W - EDGE:W],
                                         rem_dn[p][:], down_edge[:, 4 * h:4 * h + 4, :], start=False, stop=True,
                                         skip_group_check=True).then_inc(down_ready, 1)

                        def drain(G, k):
                            if k < 2:
                                pe.wait_ge(conv_added, done(G * 2 - 2 + k))
                            else:
                                pe.wait_ge(down_kept, done(G * 5 + k - 2))

                        groups_of(pe, up, down)


                        def step(i, u, part):
                            j, p, half = item(i, u, 0)
                            j1, p1_, half1 = item(i, u, 1)
                            j2, p2_, half2 = item(i, u, 2)
                            n, n1, n2 = (b * octets + k for k in (j, j1, j2))
                            if live(j, octets):
                                pe.wait_ge(mv_tok[p], (b * (octets // 2) + half + 1) * 16)
                                for k in range(2):
                                    pe.wait_ge(xh_ready, done(n * 2 + k - 2))
                                    for q in range(ROWS):
                                        mm = t.transpose(tok_ps[k][:, q * 128:q * 128 + 128],
                                                         tok[p][:, k * ROWS + q, :], ident[:])
                                    mm.then_inc(tok_turned, 1)
                            if live(j1, octets):
                                expert_row(n1, p1_, 0)
                                pe.wait_ge(route, n1 * ROUTES + ROUTES + ROUTE0)
                                for k in range(2):
                                    mm = t.transpose(gT_ps[:, k, :], gate[p1_][:, k * ROWS:k * ROWS + ROWS, :]
                                                     .rearrange("p q e -> p (q e)"), ident[:])
                                mm.then_inc(gate_turned, 1)
                                expert_row(n1, p1_, 1)
                            if live(j, octets):
                                pe.wait_ge(xh_ready, done(n * 2 + 1))
                                pe.wait_ge(gate_kept, done(n - 1))
                                for q in range(OCTET):
                                    mm = t.matmul(lg_ps[:, q, :],
                                                  xh[p][:, q // ROWS, q % ROWS * 128:q % ROWS * 128 + 128],
                                                  router[:], start=True, stop=True)
                                mm.then_inc(lg_ready, 1)
                            if live(j1, octets):
                                expert_row(n1, p1_, 2)
                                expert_row(n1, p1_, 3)
                            if live(j2, octets):
                                output(n2, p2_, 1)
                            if live(j1, octets):
                                for q in range(4, OCTET):
                                    expert_row(n1, p1_, q)
                                output(n1, p1_, 0)

                        def output(n, p, k):
                            pe.wait_ge(acc_done, done(n * 2 + k))
                            pe.wait_ge(gate_kept, done(n))
                            pe.wait_ge(out_kept, done(n * 2 + k - 1))
                            for q in range(ROWS):
                                at = slice(q * 128, q * 128 + 128)
                                t.matmul(out_ps[:, at], acc[k][:, q, :], ident[:], start=True, stop=False)
                                mm = t.matmul(out_ps[:, at], ebias[:, q, :], gateTs[p][:, k, :],
                                              start=False, stop=True)
                            mm.then_inc(out_ready, 1)

                        def expert_row(n, p, q):
                            r = n * OCTET + q
                            for h in range(2):
                                if h:
                                    pe.wait_ge(act_part, done(r - 2))
                                else:
                                    pe.wait_ge(dve_part, (r - 1 + CREDIT) * DVE_EXPERTS)
                                mm = t.matmul(exp_ps[q % 2][:, h, :],
                                              xh[p][:, q // ROWS, q % ROWS * 128:q % ROWS * 128 + 128],
                                              experts[:, 4 * h:4 * h + 4, :].rearrange("d e c -> d (e c)"),
                                              start=True, stop=True)
                            mm.then_inc(exp_out, 1)

                        walk(pe, passed, step, octets, 2)

                @block.scalar
                def _(act):
                    a = nc.scalar
                    credit(act, img_kept, up1_kept, up2_kept, down_kept, xh_ready, act_part, gate_kept, out_kept)
                    with act.Fori(0, B) as b:
                        act.wait_ge(acc_done, done(b * blocks - 1))
                        settle(act, passed)
                        with act.Fori(0, ht) as i:
                            for u in range(2):
                                n = b * TILES + i * 2 + u
                                act.wait_ge(img_turned, done(n))
                                a.activation(img[:, rows_of(i * 2 + u), :],
                                             turn_ps[u][:].rearrange("p (q c) -> p q c", q=ROWS), ACT.Copy)\
                                 .then_inc(img_kept, 1)
                        act.wait_ge(stat_chain, (b + 1) * TILES * 3 + CREDIT)
                        a.activation(std_all[:], mv_all[:, :, 1], ACT.Sqrt, bias=eps6[:]).then_inc(mv_std, 1)

                        def up(g, p):
                            G = b * GROUPS + g
                            act.wait_ge(bias_got, G * 2 + 2 + CREDIT * 2)
                            act.wait_ge(up2_ready, done(G * (GC + 1) - GC - 2))
                            for c in range(GC + 1):
                                if c < GC:
                                    act.wait_ge(up1_ready, done(G * GC + c))
                                    a.activation(upc[p][:, c, :], up1_ps[c % 2][:, 0:UPN], ACT.Copy)\
                                     .then_inc(up1_kept, 1)
                                if c == 0:
                                    act.wait_ge(down_ready, done(G * 7 - 14 + 4))
                                if c >= 1:
                                    act.wait_ge(up2_ready, done(G * (GC + 1) + c - 1))
                                    a.activation(act_in[p][:, c - 1, :, :], up2_ps[(p + c - 1) % 2][:, :, 0:UPN],
                                                 ACT.Identity, scale=GAIN, bias=bias_g[p][:, c - 1:c])\
                                     .then_inc(up2_kept, 1)
                            act.wait_ge(up2_ready, done(G * (GC + 1) + GC))
                            a.activation(rem_in[p][:], up2_ps[p][0:RP, 0, 0:UPN], ACT.Identity, scale=GAIN,
                                         bias=brem_g[p][:]).then_inc(up2_kept, 1)

                        def down(g, p):
                            G = b * GROUPS + g
                            act.wait_ge(down_ready, done(G * 7 - 14 + 6))
                            for k in range(4):
                                m, h = k // 2, k % 2
                                act.wait_ge(down_ready, done(G * 7 + k))
                                a.activation(dnc[p][:, m, 4 * h:4 * h + 4, :],
                                             down_ps[(p + k) % 2][:].rearrange("p (c w) -> p c w", w=W), ACT.Copy)\
                                 .then_inc(down_kept, 1)
                            act.wait_ge(down_ready, done(G * 7 + 4))
                            a.activation(rem_dn[p][:], down_ps[p][0:RP, 0:W], ACT.Copy).then_inc(down_kept, 1)

                        groups_of(act, up, down)

                        def step(i, u, part):
                            j, p, half = item(i, u, 0)
                            j1, p1_, half1 = item(i, u, 1)
                            j2, p2_, half2 = item(i, u, 2)
                            n, n1, n2 = (b * octets + k for k in (j, j1, j2))
                            if live(j, octets):
                                act.wait_ge(exp_out, done((n - 1) * OCTET - 1))
                                for k in range(2):
                                    act.wait_ge(tok_turned, done(n * 2 + k))
                                    a.activation(xh[p][:, k, :], tok_ps[k][:], ACT.Copy).then_inc(xh_ready, 1)
                            if live(j1, octets):
                                act.wait_ge(route, n1 * ROUTES + ROUTES + ROUTE0)
                                weigh(n1, p1_, 0)
                                act.wait_ge(gate_turned, done(n1))
                                act.wait_ge(out_ready, done(n1 * 2 - 3))
                                a.activation(gateTs[p1_][:], gT_ps, ACT.Copy).then_inc(gate_kept, 1)
                                weigh(n1, p1_, 1)
                            if live(j, octets):
                                act.wait_ge(stat8_chain, n * 2 + 2)
                                act.wait_ge(route, n * ROUTES - ROUTES + 1 + ROUTE0)
                                a.activation(std8[:], mv8[:, :, 1], ACT.Sqrt, bias=eps5[:]).then_inc(std8_ready, 1)
                            if live(j1, octets):
                                weigh(n1, p1_, 2)
                                weigh(n1, p1_, 3)
                            if live(j, octets):
                                act.wait_ge(route, n * ROUTES + 5 + ROUTE0)
                                a.activation(prb[p][:], lg[p][:], ACT.Exp).then_inc(exp_ready, 1)
                            if live(j1, octets):
                                weigh(n1, p1_, 4)
                            if live(j2, octets):
                                keep(n2, j2, half2, 1)
                            if live(j1, octets):
                                for q in range(5, OCTET):
                                    weigh(n1, p1_, q)
                                keep(n1, j1, half1, 0)

                        def keep(n, j, half, k):
                            act.wait_ge(out_ready, done(n * 2 + k))
                            act.wait_ge(st_out[k], rounds(b * ht + j))
                            a.activation(res[k][:], out_ps[:], ACT.Copy).then_inc(out_kept, 1)

                        def weigh(n, p, q):
                            k = q // ROWS
                            if q % ROWS == 0:
                                act.wait_ge(y_chain, (n * 2 + k) * 2 - 2 + CREDIT * 2)
                            act.wait_ge(exp_out, done(n * OCTET + q))
                            for e in range(DVE_EXPERTS, E1):
                                ins = a.activation(ya[k][:, q % ROWS, e - DVE_EXPERTS, :],
                                                   exp_ps[q % 2][:, e // 4, (e % 4) * 128:(e % 4) * 128 + 128],
                                                   ACT.Copy, scale=gate_std[p][:, q, e:e + 1])
                            ins.then_inc(act_part, 1)

                        walk(act, passed, step, octets, 2)

                @block.gpsimd
                def _(pool):
                    g_ = nc.gpsimd
                    pool.sem_inc(grp_chain, CREDIT * 2)
                    pool.sem_inc(y_chain, CREDIT * 2)
                    with pool.Fori(0, B) as b:
                        pool.wait_ge(mv_rstd, b + 1)
                        settle(pool, passed)
                        with pool.Fori(0, GROUPS // 2) as i:
                            for p in range(2):
                                g = i * 2 + p
                                G = b * GROUPS + g
                                pool.wait_ge(up1_ready, done(G * GC - GC - 1))
                                pool.wait_ge(grp_chain, G * 2 + CREDIT * 2)
                                g_.tensor_tensor(grp[p][:], chan(img, g * GC, GC),
                                                 mv_all[:, :, 0].unsqueeze(1).to_broadcast([128, GC, H]),
                                                 ALU.subtract).then_inc(grp_chain, 1)
                                pool.wait_ge(grp_chain, G * 2 + 1 + CREDIT * 2)
                                g_.tensor_tensor(grp[p][:], grp[p][:],
                                                 rstd_all[:].unsqueeze(1).to_broadcast([128, GC, H]),
                                                 ALU.mult).then_inc(grp_chain, 1)
                        settle(pool, passed)
                        with pool.Fori(0, octets) as j:
                            for k in range(2):
                                n = b * blocks + j * 2 + k
                                pool.wait_ge(act_part, done(n * ROWS + ROWS - 1))
                                pool.wait_ge(acc_done, done(n - 2))
                                g_.tensor_tensor(ya[k][:, :, 0:2, :], ya[k][:, :, 0:2, :], ya[k][:, :, 2:4, :],
                                                 ALU.add).then_inc(y_chain, 1)
                                pool.wait_ge(y_chain, n * 2 + 1 + CREDIT * 2)
                                g_.tensor_tensor(ys[k][:], ya[k][:, :, 0, :], ya[k][:, :, 1, :], ALU.add)\
                                  .then_inc(y_chain, 1)

                @block.vector
                def _(dve):
                    v = nc.vector
                    credit(dve, x2_ready, stat_chain, leaky, conv_added, acc_done)
                    dve.sem_inc(route, ROUTE0)
                    dve.sem_inc(rem_ready, CREDIT * 3)
                    dve.sem_inc(bias_got, CREDIT * 2)
                    dve.sem_inc(dve_part, CREDIT * DVE_EXPERTS)

                    def keep_stats(n, j, u):
                        s0 = n * 3 + CREDIT
                        for q in range(ROWS):
                            ins = v.bn_stats(stat4[u][:, q, :], img[:, bass.ds(j * ROWS + q, 1), :]
                                             .rearrange("p a c -> p (a c)"))
                        ins.then_inc(stat_chain, 1)
                        dve.wait_ge(stat_chain, s0 + 1)
                        settle(dve, passed)
                        for q in range(ROWS):
                            ins = v.bn_aggr(mv4[u][:, q, :], stat4[u][:, q, :])
                        ins.then_inc(stat_chain, 1)
                        dve.wait_ge(stat_chain, s0 + 2)
                        v.tensor_copy(mv_all[:, rows_of(j), :], mv4[u][:]).then_inc(stat_chain, 1)

                    dve.wait_ge(w_centred, 3)
                    for h in range(2):
                        v.tensor_copy(experts[:, 4 * h:4 * h + 4, :],
                                      bank[h][:].rearrange("p (e c) -> p e c", c=C)).then_inc(w_kept, 1)
                    v.tensor_copy(router[:], bank[2][:, 0:E1]).then_inc(w_kept, 1)

                    with dve.Fori(0, B) as b:
                        v.tensor_copy(moe_b[:], moeT[:, :, bass.ds(b, 1)].rearrange("p e a -> p (e a)"))\
                         .then_inc(moe_got, 1)
                        v.tensor_copy(rs_b[:], rsum_all[:, bass.ds(b, 1)]).then_inc(moe_got, 1)
                        dve.wait_ge(moe_turned, b + 1)
                        dve.wait_ge(moe_got, b * 2 + 2)
                        v.tensor_scalar(moe_w[:], turn_ps[0][0:E0, 0:128], rs_b[:], None, ALU.mult)\
                         .then_inc(moe_scaled, 1)
                        dve.wait_ge(out_ready, done(b * blocks - 1))
                        settle(dve, passed)

                        def add(i, u, part):
                            j, p, half = item(i, u, 0)
                            if live(j, TILES):
                                dve.wait_ge(add_ready, done(b * TILES + j))
                                dve.wait_ge(ld_x1[p], (b * ht + half + 1) * 16)
                                dve.wait_ge(img_turned, done(b * TILES + j - 2))
                                v.tensor_tensor(x2[p][:], add_ps[p][:], x1_in[p][:], ALU.add).then_inc(x2_ready, 1)
                            j, p, half = item(i, u, 2)
                            if live(j, TILES):
                                dve.wait_ge(img_kept, done(b * TILES + j))
                                keep_stats(b * TILES + j, j, p)

                        walk(dve, passed, add, TILES, 2)
                        dve.wait_ge(mv_std, b + 1)
                        v.reciprocal(rstd_all[:], std_all[:]).then_inc(mv_rstd, 1)

                        def up(g, p):
                            G = b * GROUPS + g
                            dve.wait_ge(up2_kept, done(G * (GC + 1) - GC - 2))
                            v.tensor_copy(bias_g[p][:], bias_all[:, bass.ds(g * GC, GC)]).then_inc(bias_got, 1)
                            v.tensor_copy(brem_g[p][:], bias_rem[:, bass.ds(g, 1)]).then_inc(bias_got, 1)
                            for c in range(GC):
                                n = G * (GC + 1) + c
                                dve.wait_ge(up2_kept, done(n))
                                z = act_in[p][:, c, :, :]
                                v.scalar_tensor_tensor(out=z, in0=z, scalar=SLOPE, in1=z, op0=ALU.mult, op1=ALU.max)\
                                 .then_inc(leaky, 1)
                                if c == GC - 2:
                                    dve.wait_ge(up1_kept, done(G * GC + GC - 1))
                                    v.tensor_copy(upc_rem[p][:].rearrange("p (c r) -> p c r", r=REM),
                                                  upc[p][:, :, 2 * W:UPN]).then_inc(rem_ready, 1)
                            n = G * (GC + 1) + GC
                            dve.wait_ge(leaky, done(n - 1))
                            v.tensor_copy(act_rem[p][:].rearrange("p q (c r) -> p q c r", r=REM),
                                          act_in[p][:, :, :, 2 * H:UPN].rearrange("p c q r -> p q c r"))\
                             .then_inc(rem_ready, 1)
                            dve.wait_ge(up2_kept, done(n))
                            z = rem_in[p][:]
                            v.scalar_tensor_tensor(out=z, in0=z, scalar=SLOPE, in1=z, op0=ALU.mult, op1=ALU.max)\
                             .then_inc(leaky, 1)
                            dve.wait_ge(leaky, done(n))
                            v.tensor_tensor(rem_blk[p][:],
                                            rem_in[p][:, 2 * H:UPN].unsqueeze(1).to_broadcast([RP, GC, REM]),
                                            block_mask[:], ALU.mult).then_inc(rem_ready, 1)

                        def down(g, p):
                            G = b * GROUPS + g
                            for h in range(2):
                                dve.wait_ge(down_ready, done(G * 7 + 5 + h))
                                at = chan(img, g * GC + 4 * h, 4)
                                v.tensor_tensor(at, down_ps[(p + 5 + h) % 2][:].rearrange("p (c h) -> p c h", h=H),
                                                at, ALU.add).then_inc(conv_added, 1)

                        groups_of(dve, up, down)
                        dve.wait_ge(conv_added, done(b * 2 * GROUPS + 2 * GROUPS - 1))

                        def step(i, u, part):
                            j, p, half = item(i, u, 0)
                            j1, p1_, half1 = item(i, u, 1)
                            j2, p2_, half2 = item(i, u, 2)
                            n, n1, n2 = (b * octets + k for k in (j, j1, j2))
                            now, before = live(j, octets), live(j1, octets)
                            link = Braid(dve, route, n * ROUTES + ROUTE0)

                            def w(q, e):
                                if before:
                                    weigh(n1, j1, p1_, q, e)
                                link.ready()

                            for e in range(DVE_EXPERTS):
                                w(0, e)
                                if now:
                                    for q in range(2 * e, 2 * e + 2):
                                        ins = v.bn_stats(stat8[:, q, :], img[:, bass.ds(j * OCTET + q, 1), :]
                                                         .rearrange("p a c -> p (a c)"))
                            if now:
                                ins.then_inc(stat8_chain, 1)
                            w(1, 0)
                            if now:
                                dve.wait_ge(stat8_chain, n * 2 + 1)
                                dve.wait_ge(std8_ready, n)
                                settle(dve, passed)
                                for q in range(OCTET):
                                    ins = v.bn_aggr(mv8[:, q, :], stat8[:, q, :])
                                ins.then_inc(stat8_chain, 1)
                            for e in range(1, DVE_EXPERTS):
                                w(1, e)
                            if live(j2, octets):
                                sum_up(n2, 1)
                            w(2, 0)
                            if now:
                                dve.wait_ge(std8_ready, n + 1)
                                link(v.reciprocal(rstd8[p][:], std8[:]))
                            w(2, 1)
                            if now:
                                dve.wait_ge(lg_ready, done(n))
                                link(v.tensor_tensor(lg[p][:], lg_ps, spread(rstd8[p]), ALU.mult))
                            w(2, 2)
                            if now:
                                link(v.tensor_tensor(lg[p][:], lg[p][:], router_b_all[:].unsqueeze(1)
                                                     .to_broadcast([128, OCTET, E1]), ALU.add))
                            w(2, 3)
                            if now:
                                link(v.tensor_reduce(mx[:], lg[p][:], AX_X, ALU.max))
                            w(3, 0)
                            if now:
                                link(v.tensor_tensor(lg[p][:], lg[p][:], spread(mx), ALU.subtract))
                            w(3, 1)
                            w(3, 2)
                            w(3, 3)
                            P = prb[p][:]
                            if now:
                                dve.wait_ge(exp_ready, n + 1)
                                link(v.tensor_reduce(sm[:], P, AX_X, ALU.add))
                            w(4, 0)
                            if now:
                                link(v.reciprocal(p1[:], sm[:]))
                            w(4, 1)
                            if now:
                                link(v.tensor_tensor(P, P, spread(p1), ALU.mult))
                            w(4, 2)
                            if now:
                                link(v.tensor_reduce(p1[:], P, AX_X, ALU.max))
                            w(4, 3)
                            if now:
                                link(v.tensor_tensor(eq[:], P, spread(p1), ALU.is_equal))
                            w(5, 0)
                            if now:
                                link(v.tensor_tensor(eq[:], eq[:], desc(), ALU.mult))
                            w(5, 1)
                            if now:
                                link(v.tensor_reduce(mx[:], eq[:], AX_X, ALU.max))
                            w(5, 2)
                            if now:
                                link(v.tensor_tensor(first[:], eq[:], spread(mx), ALU.is_equal))
                            w(5, 3)
                            if now:
                                link(v.scalar_tensor_tensor(out=pr2[:], in0=first[:], scalar=-2.0, in1=P,
                                                            op0=ALU.mult, op1=ALU.add))
                            if before:
                                sum_up(n1, 0)
                            w(6, 0)
                            if now:
                                link(v.tensor_reduce(p2[:], pr2[:], AX_X, ALU.max))
                            w(6, 1)
                            if now:
                                link(v.tensor_tensor(eq[:], pr2[:], spread(p2), ALU.is_equal))
                            w(6, 2)
                            if now:
                                link(v.tensor_tensor(eq[:], eq[:], desc(), ALU.mult))
                            w(6, 3)
                            if now:
                                link(v.tensor_reduce(mx[:], eq[:], AX_X, ALU.max))
                            w(7, 0)
                            if now:
                                link(v.tensor_tensor(second[:], eq[:], spread(mx), ALU.is_equal))
                            w(7, 1)
                            if now:
                                link(v.tensor_tensor(sm[:], p1[:], p2[:], ALU.add))
                            w(7, 2)
                            if now:
                                link(v.reciprocal(p1[:], sm[:]))
                            w(7, 3)
                            if now:
                                link(v.tensor_tensor(first[:], first[:], second[:], ALU.add))
                                link.ready()
                                link(v.tensor_tensor(P, P, first[:], ALU.mult))
                                link.ready()
                                link(v.tensor_tensor(gate[p][:], P, spread(p1), ALU.mult))
                                link.ready()
                                dve.wait_ge(act_part, done(n * OCTET - OCTET - 1))
                                link(v.tensor_tensor(gate_std[p][:], gate[p][:], spread(rstd8[p]), ALU.mult))
                                link.ready()
                                assert link.n == ROUTES, link.n

                        def spread(t):
                            return t[:].unsqueeze(2).to_broadcast([128, OCTET, E1])

                        def desc():
                            return desc8[:].unsqueeze(1).to_broadcast([128, OCTET, E1])

                        def weigh(n, j, p, q, e):
                            r, k = n * OCTET + q, q // ROWS
                            if e:
                                dve.wait_ge(dve_part, (r + CREDIT) * DVE_EXPERTS + e)
                            else:
                                dve.wait_ge(exp_out, done(r))
                                if q % ROWS == 0:
                                    dve.wait_ge(out_ready, done(n * 2 + k - 2))
                            before = acc[k][:, q % ROWS, :] if e else \
                                img[:, bass.ds(j * OCTET + q, 1), :].rearrange("p a c -> p (a c)")
                            v.scalar_tensor_tensor(
                                out=acc[k][:, q % ROWS, :],
                                in0=exp_ps[q % 2][:, e // 4, (e % 4) * 128:(e % 4) * 128 + 128],
                                scalar=gate_std[p][:, q, e:e + 1], in1=before, op0=ALU.mult, op1=ALU.add)\
                             .then_inc(dve_part, 1)

                        def sum_up(n, k):
                            dve.wait_ge(y_chain, (n * 2 + k) * 2 + 2 + CREDIT * 2)
                            dve.wait_ge(dve_part, (n * OCTET + k * ROWS + ROWS + CREDIT) * DVE_EXPERTS)
                            v.tensor_tensor(acc[k], acc[k], ys[k][:], ALU.add).then_inc(acc_done, 1)

                        walk(dve, passed, step, octets, 2)


_INS = ["x", "L0_conv_w1", "L0_conv_in_gamma", "L0_conv_in_beta", "L0_conv_w2", "L0_conv_b2",
        "L0_ffn_gate_w", "L0_ffn_gate_b", "L0_ffn_weight1", "L0_ffn_weight2", "L1_conv_bias",
        "L1_conv_up_filter", "L1_conv_down_filter", "L1_ffn_router_w", "L1_ffn_router_b",
        "L1_ffn_expert_w", "L1_ffn_expert_b"]


def kernel(**inputs):
    import concourse.bacc as _bacc
    from concourse.bass_utils import run_bass_kernel_spmd as _run

    nc = _bacc.Bacc("TRN2", target_bir_lowering=False, num_devices=1)
    arrays, args = {}, []
    for name in _INS:
        a = np.ascontiguousarray(inputs[name])
        arrays[f"in_{name}"] = a
        args.append(nc.dram_tensor(f"in_{name}", a.shape, mybir.dt.from_np(a.dtype), kind="ExternalInput").ap())
    args.append(nc.dram_tensor("out_0", (B, C, H, W), F32, kind="ExternalOutput").ap())
    metaformer_kernel(nc, *args)
    return _run(nc, [arrays], core_ids=[0]).results[0]["out_0"]
```

```python
from contextlib import ExitStack

import numpy as np

import concourse.bass as bass
from concourse import mybir

F32 = mybir.dt.float32
BF16 = mybir.dt.bfloat16
U32 = mybir.dt.uint32
ALU = mybir.AluOpType
ACT = mybir.ActivationFunctionType
AX_X = mybir.AxisListType.X

B, C, H, W = 8, 128, 128, 128
TOKENS = H * W
ROWS = 4
TILE = ROWS * W
TILES = H // ROWS
RED = 16
TAPS = 9
PAD = 2
HP = H + 2 * PAD
E0, K0, HID = 64, 8, 512
HALF = TOKENS // 2
NEG, BIG = -3.0e38, 2.0 ** 127
FT = 12
UPN = 2 * H + 10
REM = UPN - 2 * H
GC = 8
GROUPS = C // GC
RP = GC * REM
EDGE = 5
SLOPE, GAIN = 0.2, float(np.sqrt(2.0).astype(np.float32))
E1 = 8
OCTET = 2 * ROWS
ACT_EXPERTS = 4
DVE_EXPERTS = E1 - ACT_EXPERTS

CREDIT = 16


def done(n):
    return n + (CREDIT + 1)


def rounds(n):
    return (n + 1) * 16


def item(i, u, lag):
    d = u - lag
    p = d % 2
    half = i + (d - p) // 2
    return half * 2 + p, p, half


def settle(eng, passed):
    eng.sem_inc(passed, 1)


def walk(eng, passed, step, count, lag, parts=1):
    head = (lag + 1) // 2
    size = count // 2 // parts
    for part in range(parts):
        for i in range(part * size, part * size + head):
            for u in range(2):
                step(i, u, part)
        settle(eng, passed)
        with eng.Fori(part * size + head, (part + 1) * size) as i:
            for u in range(2):
                step(i, u, part)
    for s in range(count, count + lag):
        step(s // 2, s % 2, parts)


def live(j, count):
    return not isinstance(j, int) or 0 <= j < count


class Chain:

    def __init__(self, eng, sem, base):
        self.eng, self.sem, self.base, self.n = eng, sem, base, 0

    def __call__(self, ins):
        self.n += 1
        ins.then_inc(self.sem, 1)
        self.eng.wait_ge(self.sem, self.base + self.n)


class Braid:

    def __init__(self, eng, sem, base):
        self.eng, self.sem, self.base, self.n, self.waited = eng, sem, base, 0, 0

    def __call__(self, ins):
        self.n += 1
        ins.then_inc(self.sem, 1)

    def ready(self):
        if self.n > self.waited:
            self.eng.wait_ge(self.sem, self.base + self.n)
            self.waited = self.n


def metaformer_kernel(nc, x, w1, in_gamma, in_beta, w2, b2, gate_w, gate_b, ew1, ew2,
                      conv_bias, up_filter, down_filter, router_w, router_b, expert_w, expert_b, out):
    x1_dram = nc.dram_tensor("x1_dram", (B, C, H, W), F32).ap()
    xT_dram = nc.dram_tensor("xT_dram", (TOKENS, C), F32).ap()
    var_dram = nc.dram_tensor("var_dram", (H, W), F32).ap()
    r_dram = nc.dram_tensor("r_dram", (3, 2, HALF), BF16).ap()
    S_dram = nc.dram_tensor("S_dram", (B, E0, TOKENS), F32).ap()

    with ExitStack() as ctx:
        def sb(name, shape, dt=F32):
            return ctx.enter_context(nc.sbuf_tensor(name, shape, dt))

        def sem(name):
            return ctx.enter_context(nc.semaphore(name))

        bank = [ctx.enter_context(nc.psum_tensor(f"bank{i}", [128, 512], F32)) for i in range(4)]
        duo = [ctx.enter_context(nc.psum_tensor(f"duo{i}", [128, 2, 512], F32)) for i in range(2)]

        ident = sb("ident", [128, 128])
        center = sb("center", [128, 128])
        mean_cols = sb("mean_cols", [128, 32])
        eps6 = sb("eps6", [128, 1])
        eps5 = sb("eps5", [128, 1])
        sel_half = sb("sel_half", [6, 2, 128], BF16)
        sel6 = sb("sel6", [6, 128], BF16)
        w1rep = sb("w1rep", [128, 128])
        gamma_rep = sb("gamma_rep", [128, 1])
        beta_rep = sb("beta_rep", [128, 1])
        wstack = sb("wstack", [128, TAPS, 128], BF16)
        gateT = sb("gateT", [128, E0])
        gate_bias = sb("gate_bias", [E0, 1])
        slots16 = sb("slots16", [E0, 16])
        up_mat = sb("up_mat", [128, UPN])
        down_mat = sb("down_mat", [128, 2, 128])
        down_edge = sb("down_edge", [RP, GC, EDGE])
        down_edge1 = sb("down_edge1", [RP, EDGE])
        block_mask = sb("block_mask", [RP, GC, REM])
        bias_all = sb("bias_all", [128, C])
        bias_rem = sb("bias_rem", [RP, GROUPS])
        router = sb("router", [128, E1])
        router_b_all = sb("router_b_all", [128, E1])
        desc8 = sb("desc8", [128, E1])
        ebias = sb("ebias", [ROWS * E1, ROWS, 128])
        pooledT = sb("pooledT", [128, B, E0])
        moeT = sb("moeT", [128, E0, B])
        rsum_all = sb("rsum_all", [E0, B])

        s_fill = sem("s_fill")
        s_load = sem("s_load")
        s_dve0 = sem("s_dve0")
        s_pe0 = sem("s_pe0")

        passed = sem("passed")

        def credit(eng, *names):
            for s in names:
                eng.sem_inc(s, CREDIT)

        with ExitStack() as tmp:
            def tb(name, shape, dt=F32):
                return tmp.enter_context(nc.sbuf_tensor(name, shape, dt))

            w1x = tb("w1x", [128, 128])
            gw = tb("gw", [E0, 128])
            gwT = tb("gwT", [128, E0])
            w2n = tb("w2n", [128, TAPS, RED])
            b2n = tb("b2n", [128, TAPS, 1])
            part16 = tb("part16", [128, TAPS, RED + 1], BF16)
            rest = tb("rest", [128, TAPS, RED + 1])
            rest2 = tb("rest2", [128, TAPS, RED + 1])
            stack_rows = tb("stack_rows", [128, TAPS, 128])
            fu = tb("fu", [128, FT])
            fd = tb("fd", [128, FT])
            cb = tb("cb", [128, C])
            up_tap = tb("up_tap", [128, FT, UPN])
            down_tap = tb("down_tap", [128, 2, FT, 128])
            edge_tap = tb("edge_tap", [RP, FT, GC, EDGE])
            edge_sum = tb("edge_sum", [RP, GC, EDGE])
            brem = tb("brem", [RP, GROUPS, GC])
            ones_t = tb("ones_t", [128, 128])
            zeros_t = tb("zeros_t", [128, 128])
            ones_b = tb("ones_b", [6, 128], BF16)
            sel_b = tb("sel_b", [6, 128], BF16)
            ones_m = tb("ones_m", [RP, GC, REM])
            ones_m2 = tb("ones_m2", [RP, GC, REM])
            slots_i = tb("slots_i", [E0, 16], mybir.dt.int32)
            desc_i = tb("desc_i", [128, E1], mybir.dt.int32)

            n_zero = 9
            small = [(gw, gate_w), (w2n, w2.rearrange("(c k) o -> c k o", k=TAPS)),
                     (b2n, b2.rearrange("(c k a) -> c k a", k=TAPS, a=1)),
                     (gate_bias, gate_b.rearrange("(e a) -> e a", a=1)),
                     (fu, up_filter.partition_broadcast(128)), (fd, down_filter.partition_broadcast(128)),
                     (cb, conv_bias.partition_broadcast(128)), (router, router_w),
                     (router_b_all, router_b.partition_broadcast(128))]
            groups = [0, 1, 2, 4, 5, 6, 7]
            n_loads = len(small) + 3 * len(groups) + ROWS
            filled = n_zero + 12 + 4 * FT
            dve_steps = []
            with nc.Block() as block:
                @block.gpsimd
                def _(pool):
                    g = nc.gpsimd
                    for t, v in ((w1x, 0.0), (gamma_rep, 0.0), (beta_rep, 1.0), (ebias, 0.0), (stack_rows, 0.0),
                                 (ones_t, 1.0), (zeros_t, 0.0), (ones_b, 1.0), (ones_m, 1.0)):
                        g.memset(t[:], v).then_inc(s_fill, 1)
                    pool.wait_ge(s_fill, n_zero)
                    g.memset(mean_cols[:], 1.0 / C).then_inc(s_fill, 1)
                    g.memset(eps6[:], 1e-6).then_inc(s_fill, 1)
                    g.memset(eps5[:], 1e-5).then_inc(s_fill, 1)
                    g.affine_select(out=sel_half[:, 0, :], in_=ones_b[:], compare_op=ALU.is_ge, fill=0.0, base=2,
                                    pattern=[[0, 128]], channel_multiplier=-1).then_inc(s_fill, 1)
                    g.affine_select(out=sel_half[:, 1, :], in_=ones_b[:], compare_op=ALU.is_ge, fill=0.0, base=-3,
                                    pattern=[[0, 128]], channel_multiplier=1).then_inc(s_fill, 1)
                    g.affine_select(out=ident[:], in_=zeros_t[:], compare_op=ALU.not_equal, fill=1.0, base=0,
                                    pattern=[[-1, 128]], channel_multiplier=1).then_inc(s_fill, 1)
                    g.affine_select(out=sel_b[:, 0:64], in_=ones_b[:, 0:64], compare_op=ALU.is_ge, fill=0.0, base=2,
                                    pattern=[[0, 64]], channel_multiplier=-1).then_inc(s_fill, 1)
                    g.affine_select(out=sel_b[:, 64:128], in_=ones_b[:, 64:128], compare_op=ALU.is_ge, fill=0.0,
                                    base=-3, pattern=[[0, 64]], channel_multiplier=1).then_inc(s_fill, 1)
                    g.iota(slots_i[:], pattern=[[1, 16]], base=0, channel_multiplier=0).then_inc(s_fill, 1)
                    g.iota(desc_i[:], pattern=[[-1, E1]], base=E1, channel_multiplier=0).then_inc(s_fill, 1)
                    g.affine_select(out=ones_m2[:], in_=ones_m[:], compare_op=ALU.is_ge, fill=0.0, base=0,
                                    pattern=[[-REM, GC], [0, REM]], channel_multiplier=1).then_inc(s_fill, 1)
                    pool.wait_ge(s_fill, n_zero + 11)
                    g.affine_select(out=block_mask[:], in_=ones_m2[:], compare_op=ALU.is_ge, fill=0.0, base=REM - 1,
                                    pattern=[[REM, GC], [0, REM]], channel_multiplier=-1).then_inc(s_fill, 1)
                    pool.wait_ge(s_load, 16 * n_loads)
                    for t in range(FT):
                        g.affine_select(out=up_tap[:, t, :], in_=fu[:, t:t + 1].to_broadcast([128, UPN]),
                                        compare_op=ALU.is_equal, fill=0.0, base=-t, pattern=[[1, UPN]],
                                        channel_multiplier=-2).then_inc(s_fill, 1)
                        for m in range(2):
                            g.affine_select(out=down_tap[:, m, t, :], in_=fd[:, t:t + 1].to_broadcast([128, 128]),
                                            compare_op=ALU.is_equal, fill=0.0, base=128 * m - (FT - 1) + t,
                                            pattern=[[-2, 128]], channel_multiplier=1).then_inc(s_fill, 1)
                        first = 2 * H - (FT - 1) + t - 2 * (128 - EDGE)
                        g.affine_select(out=edge_tap[:, t, :, :],
                                        in_=fd[0:RP, t:t + 1].unsqueeze(2).to_broadcast([RP, GC, EDGE]),
                                        compare_op=ALU.is_equal, fill=0.0, base=first,
                                        pattern=[[-REM, GC], [-2, EDGE]], channel_multiplier=1).then_inc(s_fill, 1)

                @block.sync
                def _(sp):
                    for dst, src in small:
                        sp.dma_start(dst[:], src).then_inc(s_load, 16)
                    sp.wait_ge(s_fill, n_zero)
                    for q in groups:
                        at = slice(RED * q, RED * q + RED)
                        sp.dma_start(w1x[at, :], w1).then_inc(s_load, 16)
                        sp.dma_start(gamma_rep[at, :], in_gamma.rearrange("(e a) -> e a", a=1)).then_inc(s_load, 16)
                        sp.dma_start(beta_rep[at, :], in_beta.rearrange("(e a) -> e a", a=1)).then_inc(s_load, 16)
                    for q in range(ROWS):
                        sp.dma_start(ebias[q * E1:q * E1 + E1, q, :], expert_b).then_inc(s_load, 16)

                @block.vector
                def _(dve):
                    v = nc.vector
                    link = Chain(dve, s_dve0, 0)
                    dve.wait_ge(s_fill, n_zero + 12)
                    dve.wait_ge(s_load, 16 * n_loads)
                    link(v.tensor_scalar(center[:], ident[:], -1.0 / C, None, ALU.add))
                    link(v.tensor_copy(slots16[:], slots_i[:]))
                    link(v.tensor_copy(desc8[:], desc_i[:]))
                    link(v.tensor_copy(sel6[:], sel_b[:]))
                    link(v.tensor_copy(rest[:, :, 0:RED], w2n[:]))
                    link(v.tensor_copy(rest[:, :, RED:RED + 1], b2n[:]))
                    for n, (cols, bcol) in enumerate((((0, 64, 96), 48), ((16, 80), 49), ((32,), 50))):
                        link(v.tensor_copy(part16[:], rest[:]))
                        for c0 in cols:
                            link(v.tensor_copy(stack_rows[:, :, c0:c0 + RED], part16[:, :, 0:RED]))
                        link(v.tensor_copy(stack_rows[:, :, bcol:bcol + 1], part16[:, :, RED:RED + 1]))
                        link(v.tensor_tensor(rest2[:], rest[:], part16[:], ALU.subtract))
                        link(v.tensor_copy(rest[:], rest2[:]))
                    dve.wait_ge(s_fill, filled)
                    link(v.tensor_scalar(up_mat[:], up_tap[:, 0, :], 1.0, None, ALU.mult))
                    for t in range(1, FT):
                        link(v.tensor_tensor(up_mat[:], up_mat[:], up_tap[:, t, :], ALU.add))
                    link(v.tensor_scalar(up_mat[:], up_mat[:], 2.0, None, ALU.mult))
                    link(v.tensor_copy(down_mat[:], down_tap[:, :, 0, :]))
                    for t in range(1, FT):
                        link(v.tensor_tensor(down_mat[:], down_mat[:], down_tap[:, :, t, :], ALU.add))
                    link(v.tensor_copy(edge_sum[:], edge_tap[:, 0]))
                    for t in range(1, FT):
                        link(v.tensor_tensor(edge_sum[:], edge_sum[:], edge_tap[:, t], ALU.add))
                    link(v.tensor_tensor(down_edge[:], edge_sum[:], block_mask[:, :, 0:EDGE], ALU.mult))
                    link(v.tensor_reduce(down_edge1[:], down_edge[:].rearrange("p c j -> p j c"), AX_X, ALU.add))
                    link(v.tensor_scalar(bias_all[:], cb[:], GAIN, None, ALU.mult))
                    link(v.tensor_tensor(brem[:], bias_all[0:RP, :].rearrange("p (g c) -> p g c", c=GC),
                                         block_mask[:, :, 0:1].rearrange("p c a -> p a c")
                                         .to_broadcast([RP, GROUPS, GC]), ALU.mult))
                    link(v.tensor_reduce(bias_rem[:], brem[:], AX_X, ALU.add))
                    for k in range(TAPS):
                        dve.wait_ge(s_pe0, k + 1)
                        link(v.tensor_copy(wstack[:, k, :], bank[k % 2][:, 0:128]))
                    dve.wait_ge(s_pe0, TAPS + 1)
                    link(v.tensor_copy(w1rep[:], bank[TAPS % 2][:, 0:128]))
                    dve.wait_ge(s_pe0, TAPS + 2)
                    link(v.tensor_copy(gwT[:], bank[(TAPS + 1) % 2][:, 0:E0]))
                    dve.wait_ge(s_pe0, TAPS + 3)
                    link(v.tensor_copy(gateT[:], bank[TAPS % 2][:, 0:E0]))
                    dve_steps.append(link.n)

                @block.tensor
                def _(pe):
                    t = nc.tensor
                    before = dve_steps[0] - TAPS - 3
                    for k in range(TAPS):
                        pe.wait_ge(s_dve0, before + max(k - 1, 0))
                        t.transpose(bank[k % 2][:, 0:128], stack_rows[:, k, :], ident[:]).then_inc(s_pe0, 1)
                    pe.wait_ge(s_dve0, before + TAPS - 1)
                    t.transpose(bank[TAPS % 2][:, 0:128], w1x[:], ident[:]).then_inc(s_pe0, 1)
                    pe.wait_ge(s_dve0, before + TAPS)
                    t.transpose(bank[(TAPS + 1) % 2][:, 0:E0], gw[:], ident[0:E0, 0:E0]).then_inc(s_pe0, 1)
                    pe.wait_ge(s_dve0, before + TAPS + 2)
                    t.matmul(bank[TAPS % 2][:, 0:E0], center[:], gwT[:], start=True, stop=True).then_inc(s_pe0, 1)

        with ExitStack() as tmp:
            def tb(name, shape, dt=F32):
                return tmp.enter_context(nc.sbuf_tensor(name, shape, dt))

            def pair(name, shape, dt=F32):
                return [tb(f"{name}{u}", shape, dt) for u in range(2)]

            xn = tb("xn", [128, HP, HP])
            logits = tb("logits", [128, HALF + 8])
            picked = tb("picked", [128, HALF + 8], BF16)
            x_in = pair("x_in", [128, TILE])
            std = tb("std", [128, H])
            rstd = tb("rstd", [128, H])
            var_all = tb("var_all", [128, H])
            r_part = [tb(f"r_part{k}", [128, W], BF16) for k in range(3)]
            r_rest = tb("r_rest", [128, W])
            r_all = picked[0:6, 0:HALF]
            t_stats = tb("t_stats", [128, TILES * 6])
            t_mv = tb("t_mv", [128, 2])
            t_tmp = tb("t_tmp", [128, 2])
            t_scale = tb("t_scale", [128, 1])
            t_bias = tb("t_bias", [128, 1])
            stack = pair("stack", [128, TILE], BF16)
            t_full = pair("t_full", [128, TILE])
            t_high = pair("t_high", [128, TILE], BF16)
            t_rest = pair("t_rest", [128, TILE])
            square = t_rest
            var_rows = pair("var_rows", [128, W])
            prod_all = tb("prod_all", [128, TAPS, TILE])
            prod = [prod_all[:, k, :] for k in range(TAPS)]
            psum_in = [pair(f"part_sum{k}", [128, TILE]) for k in range(4)]
            x_res = pair("x_res", [128, TILE])
            x_slot = x_in + x_res
            x1 = pair("x1", [128, TILE])
            x1T = pair("x1T", [128, ROWS, C])
            sq_junk = tb("sq_junk", [128, ROWS, C], BF16)
            var4 = pair("var4", [128, ROWS])
            top_half = tb("top_half", [128, 8])
            idx_half = tb("idx_half", [128, 8], U32)
            idxf_half = tb("idxf_half", [128, 8])
            cand = tb("cand", [E0, 16])
            cand_idx = tb("cand_idx", [E0, 16])
            top = tb("top", [E0, 8])
            pos = tb("pos", [E0, 8], U32)
            posf = tb("posf", [E0, 8])
            cand_mark = tb("cand_mark", [E0, 16])
            kept = tb("kept", [E0, 16])
            kept2 = tb("kept2", [E0, 16])
            lists = tb("lists", [E0, 17])
            find = tb("find", [128, 9])
            token_eq = tb("token_eq", [E0, K0, 16])
            token_f = tb("token_f", [E0, K0])
            token = tb("token", [E0, K0], U32)
            zsum = tb("zsum", [128, 1])
            zsum2 = tb("zsum2", [E0, 1])
            zinv = tb("zinv", [E0, 1])
            rsum_b = tb("rsum_b", [E0, 1])
            top_exp = tb("top_exp", [E0, K0])
            rows = prod_all[0:E0, 0:2, :].rearrange("e a (k c) -> e (a k) c", c=C)
            rows_sq = prod_all[0:E0, 2:4, :].rearrange("e a (k c) -> e (a k) c", c=C)
            row_var = tb("row_var", [E0, K0])
            row_std = tb("row_std", [E0, K0])
            row_w = tb("row_w", [E0, K0])
            pooled = tb("pooled", [E0, C])

            centre_ps, rb_ps = bank[0:2], bank[0:2]
            rb2_ps = [duo[0][:, u] for u in range(2)]
            t_ps, raw_ps = bank[2], bank[3]
            wgt_ps = [bank[0], bank[1], duo[0][:, 0]]
            acc_ps, xT_ps = duo[0][:, 1], duo[1][:, 0]
            var_ps = [bank[2 + u][:, 0:W] for u in range(2)]
            turn_ps = duo[1][:, 1, 128:256]
            pool_ps = duo[1][:, 1, 256:256 + E0]

            def nsem(name):
                return tmp.enter_context(nc.semaphore(name))

            ld_x = [nsem(f"ld_x{u}") for u in range(4)]
            centred = nsem("centred")
            squared = nsem("squared")
            varied = nsem("varied")
            var_kept = nsem("var_kept")
            st_var = [nsem(f"st_var{u}") for u in range(2)]
            ld_var = nsem("ld_var")
            std_ready = nsem("std_ready")
            split_chain = nsem("split_chain")
            st_r = [nsem(f"st_r{k}") for k in range(3)]
            ld_r = [nsem(f"ld_r{h}") for h in range(2)]
            rb_ready = nsem("rb_ready")
            scaled = nsem("scaled")
            t_ready = nsem("t_ready")
            t_counted = nsem("t_counted")
            norm_chain = nsem("norm_chain")
            norm_std = nsem("norm_std")
            t2_ready = nsem("t2_ready")
            relu_chain = nsem("relu_chain")
            mid_ready = nsem("mid_ready")
            part_chain = nsem("part_chain")
            sum_chain = nsem("sum_chain")
            wgt_ready = nsem("wgt_ready")
            mul_done = nsem("mul_done")
            pair_chain = nsem("pair_chain")
            acc_ready = nsem("acc_ready")
            x1_ready = nsem("x1_ready")
            ld_res = [nsem(f"ld_res{u}") for u in range(2)]
            st_x1 = [nsem(f"st_x1{u}") for u in range(2)]
            st_xT = [nsem(f"st_xT{u}") for u in range(2)]
            xT_ready = nsem("xT_ready")
            raw_ready = nsem("raw_ready")
            raw_kept = nsem("raw_kept")
            xT_kept = nsem("xT_kept")
            var4_ready = nsem("var4_ready")
            var4_kept = nsem("var4_kept")
            std2_ready = nsem("std2_ready")
            turned2 = nsem("turned2")
            rb2_ready = nsem("rb2_ready")
            normed = nsem("normed")
            pick_chain = nsem("pick_chain")
            mv_cand = [nsem(f"mv_cand{k}") for k in range(2)]
            mv_list = [nsem(f"mv_list{k}") for k in range(2)]
            mv_sum = nsem("mv_sum")
            exp_all = nsem("exp_all")
            st_S = [nsem(f"st_S{k}") for k in range(2)]
            ld_rows = [nsem(f"ld_rows{k}") for k in range(K0)]
            pool_turned = nsem("pool_turned")
            pool_kept = nsem("pool_kept")
            border = nsem("border")

            SPLITS = (5, 6)
            NORMS = 5
            PICKS = 34
            half_tiles = TILES // 2

            def pick(b, n):
                return b * PICKS + (n + 1)

            def splits(b, use):
                return b * sum(SPLITS) + use * SPLITS[0] + 1

            def tile_of(ap, b, j):
                return ap[bass.ds(b, 1), :, bass.ds(j * ROWS, ROWS), :].rearrange("a c h w -> (a c) h w")

            def inner(j):
                return xn[:, bass.ds(j * ROWS + PAD, ROWS), PAD:PAD + W]

            def grid(ap):
                return ap.rearrange("p (h w) -> p h w", h=ROWS)

            with nc.Block() as block:
                @block.sync
                def _(sp):
                    for s in (*st_x1, *st_xT, *st_S, *st_var):
                        sp.sem_inc(s, 16)

                    def pass_r(b, use, broadcast):
                        for k in range(3):
                            sp.wait_ge(split_chain, splits(b, use) + use + (2, 4, 5)[k])
                            sp.dma_start(r_dram[k].rearrange("s t -> (s t)").rearrange("(h w) -> h w", w=W),
                                         r_part[k][:]).then_inc(st_r[k], 16)
                        for k in range(3):
                            sp.wait_ge(st_r[k], b * 32 + (use + 1) * 16)
                        sp.wait_ge(rb_ready, done(broadcast - 1))
                        for h in range(2):
                            sp.dma_start(r_all[3 * h:3 * h + 3, :], r_dram[:, h, :]).then_inc(ld_r[h], 16)

                    def quad(b, i):
                        for u in range(4):
                            if not isinstance(i, int) or i * 4 < TILES:
                                sp.wait_ge(centred, done(b * TILES + i * 4 + u - 4))
                                settle(sp, passed)
                                sp.dma_start(grid(x_slot[u][:]), tile_of(x, b, i * 4 + u)).then_inc(ld_x[u], 16)
                            if not isinstance(i, int) or i:
                                j = (i - 1) * 4 + u
                                sp.wait_ge(var_kept, done(b * TILES + j))
                                settle(sp, passed)
                                sp.dma_start(var_dram[bass.ds(j * ROWS, ROWS), :],
                                             var_rows[u % 2][0:128:32, :]).then_inc(st_var[u % 2], 16)

                    def start_centring(b):
                        sp.wait_ge(x1_ready, done(b * TILES - 1))
                        settle(sp, passed)
                        quad(b, 0)

                    def end_centring(b):
                        with sp.Fori(1, TILES // 4) as i:
                            quad(b, i)
                        quad(b, TILES // 4)
                        for u in range(2):
                            sp.wait_ge(st_var[u], rounds((b + 1) * half_tiles))
                        sp.wait_ge(split_chain, splits(b, 0))
                        sp.dma_start(var_all[:], var_dram).then_inc(ld_var, 16)

                    def rest(b):
                        sp.wait_ge(pick_chain, pick(b, 0))
                        settle(sp, passed)

                        def step(i, u, part):
                            j, p, half = item(i, u, 0)
                            if live(j, TILES):
                                sp.wait_ge(x1_ready, done(b * TILES + j - 2))
                                sp.dma_start(grid(x_res[p][:]), tile_of(x, b, j)).then_inc(ld_res[p], 16)
                            j, p, half = item(i, u, 3)
                            if live(j, TILES):
                                n = b * TILES + j
                                sp.wait_ge(x1_ready, done(n))
                                sp.dma_start(tile_of(x1_dram, b, j), grid(x1[p][:])).then_inc(st_x1[p], 16)
                            j, p, half = item(i, u, 4)
                            if live(j, TILES):
                                sp.wait_ge(xT_kept, done(b * TILES + j))
                                sp.dma_start(
                                    xT_dram[bass.ds(j * TILE, TILE), :].rearrange("(q p) c -> p q c", p=128),
                                    x1T[p][:]).then_inc(st_xT[p], 16)

                        walk(sp, passed, step, TILES, 4, parts=2)

                    def store_S(b):
                        sp.wait_ge(pick_chain, pick(b, 26))
                        for h in range(2):
                            sp.dma_start(
                                S_dram[bass.ds(b, 1), :, h * HALF:(h + 1) * HALF].rearrange("a e t -> (a e) t"),
                                logits[64 * h:64 * h + 64, 0:HALF]).then_inc(st_S[h], 16)

                    start_centring(0)
                    end_centring(0)
                    pass_r(0, 0, 0)
                    with sp.Fori(0, B - 1) as b:
                        rest(b)
                        start_centring(b + 1)
                        pass_r(b, 1, (b + 1) * TILES)
                        end_centring(b + 1)
                        sp.wait_ge(pick_chain, pick(b, 26))
                        settle(sp, passed)
                        pass_r(b + 1, 0, (b + 1) * TILES)
                        store_S(b)
                    rest(B - 1)
                    pass_r(B - 1, 1, B * TILES)
                    store_S(B - 1)
                    for s, n in ((st_x1, B * half_tiles), (st_var, B * half_tiles), (st_xT, B * half_tiles), (st_S, B)):
                        for q in s:
                            sp.wait_ge(q, rounds(n))
                    for q in st_r:
                        sp.wait_ge(q, 32 * B)

                @block.tensor
                def _(pe):
                    t = nc.tensor
                    credit(pe, centred, varied, rb_ready, t_ready, t2_ready, wgt_ready, acc_ready, xT_ready,
                           raw_ready, rb2_ready)
                    def centre(b, i):
                        for u in range(4):
                            n = b * TILES + i * 4 + u
                            pe.wait_ge(ld_x[u], (b * (TILES // 4) + i + 1) * 16)
                            pe.wait_ge(squared, done(n - 2))
                            t.matmul(centre_ps[u % 2][:], center[:], x_slot[u][:], start=True, stop=True)\
                             .then_inc(centred, 1)
                            if u or not isinstance(i, int):
                                variances(n - 1, (u + 1) % 2)

                    def variances(n, p):
                        pe.wait_ge(squared, done(n))
                        pe.wait_ge(var_kept, done(n - 2))
                        for q in range(ROWS):
                            mm = t.matmul(var_ps[p][32 * q:32 * q + 32, :], mean_cols[:],
                                          square[p][:, q * 128:q * 128 + 128], start=True, stop=True)
                        mm.then_inc(varied, 1)

                    def start_centring(b):
                        pe.wait_ge(raw_kept, done(b * TILES - 1))
                        pe.wait_ge(mul_done, done(b * TILES * TAPS - 1))
                        centre(b, 0)
                        settle(pe, passed)

                    def end_centring(b):
                        with pe.Fori(1, TILES // 4) as i:
                            centre(b, i)
                        variances(b * TILES + TILES - 1, 1)

                    def rest(b):
                        for h in range(2):
                            pe.wait_ge(ld_r[h], b * 32 + 16)
                        settle(pe, passed)

                        def reduce(i, u, part):
                            j, p, half = item(i, u, 0)
                            if live(j, TILES):
                                h = j // half_tiles if isinstance(j, int) else part
                                at = bass.ds((j - h * half_tiles) * TILE, TILE)
                                pe.wait_ge(scaled, done(b * TILES + j - 2))
                                t.matmul(rb_ps[p][:], sel_half[:, h, :], r_all[:, at], start=True, stop=True)\
                                 .then_inc(rb_ready, 1)
                            j, p, half = item(i, u, 1)
                            if live(j, TILES):
                                pe.wait_ge(scaled, done(b * TILES + j))
                                pe.wait_ge(t_counted, done(b * TILES + j - 2))
                                t.matmul(bank[2 + p][:], w1rep[:], inner(j), start=True, stop=True)\
                                 .then_inc(t_ready, 1)

                        walk(pe, passed, reduce, TILES, 1, parts=2)
                        pe.wait_ge(t_counted, done(b * TILES + TILES - 1))

                        def step(i, u, part):
                            j, p, half = item(i, u, 0)
                            j1, p1, half1 = item(i, u, 1)
                            j2, p2, half2 = item(i, u, 2)
                            j4, p4, half4 = item(i, u, 4)
                            n, n1, n2, n4 = (b * TILES + k for k in (j, j1, j2, j4))

                            def taps(first, last):
                                for k in range(first, last):
                                    pe.wait_ge(mul_done, done(n1 * TAPS + k - 3))
                                    t.matmul(wgt_ps[k % 3][:], wstack[:, k, :], stack[p1][:], start=True, stop=True)\
                                     .then_inc(wgt_ready, 1)

                            def add(k, h):
                                at = slice(h * TILE // 2, (h + 1) * TILE // 2)
                                return t.matmul(acc_ps[:, at], ident[:], psum_in[k][p2][:, at],
                                                start=(k == 0), stop=(k == 3))

                            if live(j1, TILES):
                                pe.wait_ge(part_chain, n1 * 2 + 2 + CREDIT * 2)
                                taps(0, 3)
                            if live(j, TILES):
                                pe.wait_ge(relu_chain, n * 3 - 3 + 3 + CREDIT)
                                t.matmul(t_ps[:], w1rep[:], inner(j), start=True, stop=True).then_inc(t2_ready, 1)
                            if live(j4, TILES):
                                pe.wait_ge(x1_ready, done(n4))
                                pe.wait_ge(raw_kept, done(n4 - 1))
                                h = j4 // half_tiles if isinstance(j4, int) else part
                                t.matmul(raw_ps[64 * h:64 * h + 64, :], gateT[:], x1[p4][:], start=True, stop=True)\
                                 .then_inc(raw_ready, 1)
                                pe.wait_ge(var4_ready, done(n4 - 1))
                                for q in range(ROWS):
                                    mm = t.matmul(xT_ps[:, q * 128:q * 128 + 128], x1[p4][:, q * 128:q * 128 + 128],
                                                  center[:], start=True, stop=True)
                                mm.then_inc(xT_ready, 1)
                            for k in range(3, TAPS):
                                if live(j1, TILES):
                                    taps(k, k + 1)
                                if live(j2, TILES):
                                    if k == 3:
                                        pe.wait_ge(sum_chain, n2 * 3 + 3 + CREDIT * 3)
                                        pe.wait_ge(pair_chain, n2 * 2 + 2 + CREDIT * 2)
                                        pe.wait_ge(x1_ready, done(n2 - 1))
                                    for m in {3: (0,), 4: (1,), 5: (2,), 6: (3,), 7: (4, 5), 8: (6, 7)}[k]:
                                        mm = add(m % 4, m // 4)
                            if live(j2, TILES):
                                mm.then_inc(acc_ready, 1)

                        walk(pe, passed, step, TILES, 4, parts=2)
                        pe.wait_ge(split_chain, splits(b, 1) + 1)
                        t.transpose(turn_ps, rstd[:], ident[:]).then_inc(turned2, 1)

                    def norm_logits(b):
                        for h in range(2):
                            pe.wait_ge(ld_r[h], b * 32 + 32)
                        settle(pe, passed)
                        with pe.Fori(0, half_tiles // 2) as i:
                            for u in range(2):
                                n = b * half_tiles + i * 2 + u
                                pe.wait_ge(normed, done(n - 2))
                                t.matmul(rb2_ps[u], sel6[:], r_all[:, bass.ds((i * 2 + u) * TILE, TILE)],
                                         start=True, stop=True)\
                                 .then_inc(rb2_ready, 1)

                    def turn_pooled(b):
                        pe.wait_ge(pick_chain, pick(b, PICKS))
                        settle(pe, passed)
                        t.transpose(pool_ps, pooled[:], ident[0:E0, 0:E0]).then_inc(pool_turned, 1)

                    start_centring(0)
                    end_centring(0)
                    with pe.Fori(0, B - 1) as b:
                        rest(b)
                        start_centring(b + 1)
                        norm_logits(b)
                        end_centring(b + 1)
                        turn_pooled(b)
                    rest(B - 1)
                    norm_logits(B - 1)
                    turn_pooled(B - 1)

                @block.scalar
                def _(act):
                    a = nc.scalar
                    credit(act, squared, var_kept, raw_kept, xT_kept, var4_ready, mid_ready)
                    act.sem_inc(relu_chain, CREDIT)
                    def first(b, part):
                        def centre(i):
                            for u in range(2):
                                n = b * TILES + i * 2 + u
                                act.wait_ge(centred, done(n))
                                a.activation(inner(i * 2 + u), grid(centre_ps[u][:]), ACT.Copy)
                                act.wait_ge(varied, done(n - 2))
                                a.activation(square[u][:], centre_ps[u][:], ACT.Square).then_inc(squared, 1)
                                keep_var(i, u)

                        def keep_var(i, u):
                            j, p, half = item(i, u, 2)
                            if live(j, TILES):
                                act.wait_ge(varied, done(b * TILES + j))
                                act.wait_ge(st_var[p], rounds(b * half_tiles + half))
                                a.activation(var_rows[p][:], var_ps[p], ACT.Copy).then_inc(var_kept, 1)

                        if part == 0:
                            act.wait_ge(mul_done, done(b * TILES * TAPS - 1))
                            act.wait_ge(border, 2)
                            centre(0)
                        settle(act, passed)
                        with act.Fori(max(part * half_tiles // 2, 1), (part + 1) * half_tiles // 2) as i:
                            centre(i)
                        if part == 1:
                            for u in range(2):
                                keep_var(half_tiles, u)

                    def token_std(b):
                        act.wait_ge(ld_var, b * 16 + 16)
                        act.wait_ge(split_chain, splits(b, 0))
                        a.activation(std[:], var_all[:], ACT.Sqrt, bias=eps6[:]).then_inc(std_ready, 1)

                    def rest(b):
                        act.wait_ge(norm_chain, b * NORMS + 1)
                        a.activation(t_tmp[:, 0:1], t_mv[:, 1:2], ACT.Sqrt, bias=eps5[:]).then_inc(norm_std, 1)
                        act.wait_ge(norm_chain, b * NORMS + NORMS)
                        act.wait_ge(st_S[0], rounds(b))
                        act.wait_ge(st_S[1], rounds(b))

                        def step(i, u, part):
                            j, p, half = item(i, u, 0)
                            if live(j, TILES):
                                n = b * TILES + j
                                r0 = n * 3 + CREDIT
                                act.wait_ge(t2_ready, done(n))
                                act.wait_ge(wgt_ready, done(n * TAPS - TAPS - 1))
                                a.activation(stack[p][0:64, :], t_ps[0:64, :], ACT.Relu, scale=t_scale[0:64, :],
                                             bias=t_bias[0:64, :]).then_inc(relu_chain, 1)
                                a.activation(t_full[p][64:128, :], t_ps[64:128, :], ACT.Relu,
                                             scale=t_scale[64:128, :], bias=t_bias[64:128, :])\
                                 .then_inc(relu_chain, 1)
                                act.wait_ge(relu_chain, r0 + 2)
                                a.activation(t_high[p][64:128, :], t_full[p][64:128, :], ACT.Copy)\
                                 .then_inc(relu_chain, 1)
                            j4, p4, half4 = item(i, u, 4)
                            if live(j4, TILES):
                                h = j4 // half_tiles if isinstance(j4, int) else part
                                act.wait_ge(raw_ready, done(b * TILES + j4))
                                a.activation(
                                    logits[64 * h:64 * h + 64, bass.ds((j4 - h * half_tiles) * TILE, TILE)],
                                    raw_ps[64 * h:64 * h + 64, :], ACT.Copy).then_inc(raw_kept, 1)
                            if live(j, TILES):
                                act.wait_ge(part_chain, (b * TILES + j) * 2 + 1 + CREDIT * 2)
                                a.activation(stack[p][64:128, :], t_rest[p][64:128, :], ACT.Copy)\
                                 .then_inc(mid_ready, 1)
                            if live(j4, TILES):
                                n = b * TILES + j4
                                act.wait_ge(xT_ready, done(n))
                                act.wait_ge(st_xT[p4], rounds(b * half_tiles + half4))
                                a.activation(x1T[p4][:], xT_ps.rearrange("p (q c) -> p q c", q=ROWS), ACT.Copy)\
                                 .then_inc(xT_kept, 1)
                                act.wait_ge(var4_kept, done(n - 2))
                                for q in range(ROWS):
                                    ins = a.activation(sq_junk[:, q, :], xT_ps[:, q * 128:q * 128 + 128], ACT.Square,
                                                       accum_out=var4[p4][:, q:q + 1])
                                ins.then_inc(var4_ready, 1)

                        walk(act, passed, step, TILES, 4, parts=2)
                        act.wait_ge(var4_kept, done(b * TILES + TILES - 1))
                        a.activation(std[:], var_all[:], ACT.Sqrt, bias=eps5[:], scale=1.0 / C)\
                         .then_inc(std2_ready, 1)

                    def exponentials(b):
                        act.wait_ge(pick_chain, pick(b, 18))
                        a.activation(logits[:, 0:HALF], logits[:, 0:HALF], ACT.Exp, bias=find[:, 8:9],
                                     accum_out=zsum[:]).then_inc(exp_all, 1)
                        a.activation(top_exp[:], top[:], ACT.Exp, bias=find[0:E0, 8:9]).then_inc(exp_all, 1)

                    def row_stds(b):
                        act.wait_ge(pick_chain, pick(b, 28))
                        a.activation(row_std[:], row_var[:], ACT.Sqrt, bias=eps5[0:E0, :], scale=1.0 / C)\
                         .then_inc(exp_all, 1)

                    first(0, 0)
                    first(0, 1)
                    token_std(0)
                    with act.Fori(0, B - 1) as b:
                        rest(b)
                        first(b + 1, 0)
                        exponentials(b)
                        first(b + 1, 1)
                        row_stds(b)
                        token_std(b + 1)
                    rest(B - 1)
                    exponentials(B - 1)
                    row_stds(B - 1)

                @block.gpsimd
                def _(pool):
                    g = nc.gpsimd
                    pool.sem_inc(part_chain, CREDIT * 2)
                    pool.sem_inc(sum_chain, CREDIT * 3)
                    with pool.Fori(0, B) as b:
                        def step(i, u, part):
                            j, p, half = item(i, u, 0)
                            if live(j, TILES):
                                n = b * TILES + j
                                pool.wait_ge(relu_chain, n * 3 + 3 + CREDIT)
                                g.tensor_tensor(t_rest[p][64:128, :], t_full[p][64:128, :], t_high[p][64:128, :],
                                                ALU.subtract).then_inc(part_chain, 1)
                                pool.wait_ge(mid_ready, done(n))
                                g.tensor_tensor(stack[p][96:128, :], t_rest[p][96:128, :], stack[p][96:128, :],
                                                ALU.subtract).then_inc(part_chain, 1)
                                pool.wait_ge(part_chain, n * 2 + 2 + CREDIT * 2)
                            j, p, half = item(i, u, 1)
                            if live(j, TILES):
                                n = b * TILES + j
                                pool.wait_ge(acc_ready, done(n - 2))
                                for k in range(3):
                                    pool.wait_ge(mul_done, done(n * TAPS + 2 * k + 1))
                                    g.tensor_tensor(psum_in[k][p][:], prod[2 * k], prod[2 * k + 1], ALU.add)\
                                     .then_inc(sum_chain, 1)
                                pool.wait_ge(sum_chain, n * 3 + 3 + CREDIT * 3)

                        walk(pool, passed, step, TILES, 1)
                        pool.wait_ge(pick_chain, pick(b, 3))
                        settle(pool, passed)
                        g.dma_start(cand[:, 8:16], top_half[64:128, :]).then_inc(mv_cand[0], 16)
                        g.dma_start(cand_idx[:, 8:16], idxf_half[64:128, :]).then_inc(mv_cand[1], 16)
                        pool.wait_ge(pick_chain, pick(b, 15))
                        settle(pool, passed)
                        g.dma_start(find[64:128, 0:8], lists[:, 8:16]).then_inc(mv_list[0], 16)
                        g.dma_start(find[64:128, 8:9], lists[:, 16:17]).then_inc(mv_list[1], 16)
                        for u in range(2):
                            pool.wait_ge(st_xT[u], rounds((b + 1) * half_tiles))
                        pool.wait_ge(pick_chain, pick(b, 23))
                        settle(pool, passed)
                        for k in range(K0):
                            g.indirect_dma_start(rows[:, k, :], None, xT_dram[:, :],
                                                 bass.IndirectOffsetOnAxis(ap=token[:, k:k + 1], axis=0))\
                             .then_inc(ld_rows[k], 16)
                        pool.wait_ge(exp_all, b * 3 + 1)
                        settle(pool, passed)
                        g.dma_start(zsum2[:], zsum[64:128, :]).then_inc(mv_sum, 16)

                @block.vector
                def _(dve):
                    v = nc.vector
                    credit(dve, scaled, t_counted, mul_done, x1_ready, var4_kept, normed)
                    dve.sem_inc(pair_chain, CREDIT * 2)
                    dve.sem_inc(pick_chain, 1)
                    dve.sem_inc(split_chain, 1)
                    v.memset(xn[:], 0.0).then_inc(border, 1)
                    v.memset(logits[:, HALF:HALF + 8], NEG).then_inc(border, 1)

                    def split_r(b, use):
                        link = Chain(dve, split_chain, splits(b, use))
                        if use:
                            link(v.reciprocal(rstd[:], std[:]))
                            dve.wait_ge(turned2, b + 1)
                            link(v.tensor_copy(r_rest[:], turn_ps))
                        else:
                            link(v.reciprocal(r_rest[:], std[:]))
                        link(v.tensor_copy(r_part[0][:], r_rest[:]))
                        link(v.tensor_tensor(r_rest[:], r_rest[:], r_part[0][:], ALU.subtract))
                        link(v.tensor_copy(r_part[1][:], r_rest[:]))
                        link(v.tensor_tensor(r_part[2][:], r_rest[:], r_part[1][:], ALU.subtract))
                        assert link.n == SPLITS[use]

                    with dve.Fori(0, B) as b:
                        dve.wait_ge(std_ready, b + 1)
                        split_r(b, 0)
                        settle(dve, passed)

                        def reduce(i, u, part):
                            j, p, half = item(i, u, 0)
                            if live(j, TILES):
                                dve.wait_ge(rb_ready, done(b * TILES + j))
                                v.tensor_tensor(inner(j), inner(j), grid(rb_ps[p][:]), ALU.mult).then_inc(scaled, 1)
                            j, p, half = item(i, u, 1)
                            if live(j, TILES):
                                dve.wait_ge(t_ready, done(b * TILES + j))
                                v.bn_stats(t_stats[:, bass.ds(j * 6, 6)], bank[2 + p][:]).then_inc(t_counted, 1)

                        walk(dve, passed, reduce, TILES, 1, parts=2)
                        dve.wait_ge(t_counted, done(b * TILES + TILES - 1))
                        dve.wait_ge(border, 2)
                        link = Chain(dve, norm_chain, b * NORMS)
                        settle(dve, passed)
                        link(v.bn_aggr(t_mv[:], t_stats[:]))
                        dve.wait_ge(norm_std, b + 1)
                        link(v.reciprocal(t_tmp[:, 1:2], t_tmp[:, 0:1]))
                        link(v.tensor_tensor(t_scale[:], t_tmp[:, 1:2], gamma_rep[:], ALU.mult))
                        link(v.tensor_tensor(t_tmp[:, 1:2], t_mv[:, 0:1], t_scale[:], ALU.mult))
                        link(v.tensor_tensor(t_bias[:], beta_rep[:], t_tmp[:, 1:2], ALU.subtract))
                        assert link.n == NORMS

                        def step(i, u, part):
                            j, p, half = item(i, u, 1)
                            if live(j, TILES):
                                n = b * TILES + j
                                for k in range(TAPS):
                                    dve.wait_ge(wgt_ready, done(n * TAPS + k))
                                    if k < 6:
                                        dve.wait_ge(sum_chain, n * 3 - 2 + k // 2 + CREDIT * 3)
                                    elif k == 6:
                                        dve.wait_ge(pair_chain, n * 2 + CREDIT * 2)
                                    v.tensor_tensor(
                                        grid(prod[k]), grid(wgt_ps[k % 3][:]),
                                        xn[:, bass.ds(j * ROWS + 2 * (k // 3), ROWS), 2 * (k % 3):2 * (k % 3) + W],
                                        ALU.mult).then_inc(mul_done, 1)
                                dve.wait_ge(mul_done, done(n * TAPS + 7))
                                v.tensor_tensor(prod[6], prod[6], prod[7], ALU.add).then_inc(pair_chain, 1)
                                dve.wait_ge(pair_chain, n * 2 + 1 + CREDIT * 2)
                                dve.wait_ge(mul_done, done(n * TAPS + 8))
                                dve.wait_ge(acc_ready, done(n - 2))
                                v.tensor_tensor(psum_in[3][p][:], prod[6], prod[8], ALU.add)\
                                 .then_inc(pair_chain, 1)
                            j, p, half = item(i, u, 2)
                            if live(j, TILES):
                                n = b * TILES + j
                                dve.wait_ge(acc_ready, done(n))
                                dve.wait_ge(ld_res[p], (b * half_tiles + half + 1) * 16)
                                dve.wait_ge(st_x1[p], rounds(b * half_tiles + half))
                                dve.wait_ge(xT_ready, done(n - 2))
                                v.tensor_tensor(x1[p][:], acc_ps, x_res[p][:], ALU.add).then_inc(x1_ready, 1)
                            j, p, half = item(i, u, 4)
                            if live(j, TILES):
                                n = b * TILES + j
                                dve.wait_ge(var4_ready, done(n))
                                v.tensor_copy(var_all[:, bass.ds(j * ROWS, ROWS)], var4[p][:]).then_inc(var4_kept, 1)

                        walk(dve, passed, step, TILES, 4, parts=2)
                        dve.wait_ge(std2_ready, b + 1)
                        split_r(b, 1)
                        dve.wait_ge(raw_kept, done(b * TILES + TILES - 1))
                        settle(dve, passed)
                        with dve.Fori(0, half_tiles // 2) as i:
                            for u in range(2):
                                at = bass.ds((i * 2 + u) * TILE, TILE)
                                dve.wait_ge(rb2_ready, done(b * half_tiles + i * 2 + u))
                                v.tensor_tensor(logits[:, at], logits[:, at], rb2_ps[u], ALU.mult)\
                                 .then_inc(normed, 1)
                        dve.wait_ge(normed, done(b * half_tiles + half_tiles - 1))
                        link = Chain(dve, pick_chain, pick(b, 0))
                        dve.wait_ge(border, 2)
                        settle(dve, passed)
                        link(v.max(top_half[:], logits[:]))
                        settle(dve, passed)
                        link(v.max_index(idx_half[:], top_half[:], logits[:]))
                        link(v.tensor_copy(idxf_half[:], idx_half[:]))
                        link(v.tensor_copy(cand[:, 0:8], top_half[0:64, :]))
                        link(v.tensor_copy(cand_idx[:, 0:8], idxf_half[0:64, :]))
                        dve.wait_ge(mv_cand[0], b * 16 + 16)
                        dve.wait_ge(mv_cand[1], b * 16 + 16)
                        link(v.tensor_scalar(cand_idx[:, 8:16], cand_idx[:, 8:16], float(HALF), None, ALU.add))
                        settle(dve, passed)
                        link(v.max(top[:], cand[:]))
                        settle(dve, passed)
                        link(v.max_index(pos[:], top[:], cand[:]))
                        settle(dve, passed)
                        link(v.match_replace(cand_mark[:], top[:], cand[:], BIG))
                        link(v.tensor_scalar(kept[:], cand_mark[:], BIG, None, ALU.is_equal))
                        link(v.tensor_tensor(kept2[:], kept[:], cand[:], ALU.mult))
                        link(v.tensor_scalar(kept[:], kept[:], -1.0, -NEG, ALU.add, ALU.mult))
                        link(v.tensor_tensor(lists[:, 0:16], kept2[:], kept[:], ALU.add))
                        link(v.tensor_tensor(zinv[:], top[:, 0:1], gate_bias[:], ALU.add))
                        link(v.tensor_tensor(lists[:, 16:17], gate_bias[:], zinv[:], ALU.subtract))
                        link(v.tensor_copy(find[0:E0, 0:8], lists[:, 0:8]))
                        link(v.tensor_copy(find[0:E0, 8:9], lists[:, 16:17]))
                        dve.wait_ge(mv_list[0], b * 16 + 16)
                        dve.wait_ge(mv_list[1], b * 16 + 16)
                        settle(dve, passed)
                        link(v.match_replace(picked[:], find[:, 0:8], logits[:], BIG))
                        link(v.tensor_copy(posf[:], pos[:]))
                        link(v.tensor_tensor(token_eq[:], slots16[:].unsqueeze(1).to_broadcast([E0, K0, 16]),
                                             posf[:].unsqueeze(2).to_broadcast([E0, K0, 16]), ALU.is_equal))
                        link(v.tensor_tensor(token_eq[:], token_eq[:],
                                             cand_idx[:].unsqueeze(1).to_broadcast([E0, K0, 16]), ALU.mult))
                        link(v.tensor_reduce(token_f[:], token_eq[:], AX_X, ALU.add))
                        link(v.tensor_copy(token[:], token_f[:]))
                        dve.wait_ge(mv_sum, b * 16 + 16)
                        dve.wait_ge(exp_all, b * 3 + 2)
                        link(v.tensor_tensor(zinv[:], zsum[0:E0, :], zsum2[:], ALU.add))
                        link(v.reciprocal(rsum_b[:], zinv[:]))
                        link(v.scalar_tensor_tensor(out=logits[:, 0:HALF], in0=picked[:, 0:HALF], scalar=BIG,
                                                    in1=logits[:, 0:HALF], op0=ALU.is_equal, op1=ALU.mult))
                        for k in range(K0 - 1):
                            dve.wait_ge(ld_rows[k], b * 16 + 16)
                        dve.wait_ge(ld_rows[K0 - 1], b * 16 + 16)
                        link(v.tensor_tensor(rows_sq, rows, rows, ALU.mult))
                        link(v.tensor_reduce(row_var[:], rows_sq, AX_X, ALU.add))
                        dve.wait_ge(exp_all, b * 3 + 3)
                        link(v.reciprocal(row_w[:], row_std[:]))
                        link(v.tensor_tensor(row_w[:], row_w[:], top_exp[:], ALU.mult))
                        link(v.tensor_scalar(row_w[:], row_w[:], rsum_b[:], None, ALU.mult))
                        link(v.tensor_copy(rsum_all[:, bass.ds(b, 1)], rsum_b[:]))
                        link(v.tensor_tensor(rows, rows, row_w[:].unsqueeze(2).to_broadcast([E0, K0, C]),
                                             ALU.mult))
                        link(v.tensor_reduce(pooled[:], rows.rearrange("e k c -> e c k"), AX_X, ALU.add))
                        assert link.n == PICKS
                        dve.wait_ge(pool_turned, b + 1)
                        v.tensor_copy(pooledT[:, bass.ds(b, 1), :], pool_ps.unsqueeze(1)).then_inc(pool_kept, 1)
                        dve.wait_ge(pool_kept, b + 1)
        with ExitStack() as tmp:
            def tb(name, shape, dt=F32):
                return tmp.enter_context(nc.sbuf_tensor(name, shape, dt))

            def pair(name, shape, dt=F32):
                return [tb(f"{name}{u}", shape, dt) for u in range(2)]

            def nsem(name):
                return tmp.enter_context(nc.semaphore(name))

            HC = HID // 128
            first_w = [tb(f"first_w{u}", [128, HID]) for u in range(4)]
            second_w = [tb(f"second_w{u}", [128, HC, C]) for u in range(4)]
            first_b = tb("first_b", [E0, HID])
            second_b = tb("second_b", [E0, C])
            first_bT = tb("first_bT", [128, E0, HC])
            second_bT = tb("second_bT", [128, E0])
            hid = pair("hid", [128, HC, B])
            act_hid = pair("act_hid", [128, HC, B])
            ld_b = nsem("ld_b")
            ld_w = [[nsem(f"ld_w{u}{k}") for k in range(2)] for u in range(4)]
            bias_turned = nsem("bias_turned")
            bias_kept = nsem("bias_kept")
            hid_ready = nsem("hid_ready")
            hid_biased = nsem("hid_biased")
            hid_act = nsem("hid_act")
            moe_ready = nsem("moe_ready")
            moe_kept = nsem("moe_kept")
            hid_ps = [bank[u][:, 0:HC * B].rearrange("p (c b) -> p c b", b=B) for u in range(2)]
            moe_ps = [bank[2 + u][:, 0:B] for u in range(2)]

            with nc.Block() as block:
                @block.sync
                def _(sp):
                    sp.dma_start(first_b[:], ew1[:, C, :]).then_inc(ld_b, 16)
                    sp.dma_start(second_b[:], ew2[:, HID, :]).then_inc(ld_b, 16)
                    with sp.Fori(0, E0 // 4) as i:
                        for u in range(4):
                            sp.wait_ge(moe_ready, done(i * 4 + u - 4))
                            sp.dma_start(first_w[u][:], ew1[bass.ds(i * 4 + u, 1), 0:C, :]
                                         .rearrange("a d h -> (a d) h")).then_inc(ld_w[u][0], 16)
                            sp.dma_start(second_w[u][:], ew2[bass.ds(i * 4 + u, 1), 0:HID, :]
                                         .rearrange("a (p c) o -> (a p) c o", c=HC)).then_inc(ld_w[u][1], 16)

                @block.tensor
                def _(pe):
                    t = nc.tensor
                    credit(pe, hid_ready, moe_ready)
                    pe.wait_ge(ld_b, 32)
                    for c in range(HC):
                        if c >= 2:
                            pe.wait_ge(bias_kept, c - 1)
                        t.transpose(bank[c % 2][:, 0:E0], first_b[:, c:HID:HC], ident[0:E0, 0:E0])\
                         .then_inc(bias_turned, 1)
                    pe.wait_ge(bias_kept, HC - 1)
                    t.transpose(bank[0][:, 0:E0], second_b[:], ident[0:E0, 0:E0]).then_inc(bias_turned, 1)
                    pe.wait_ge(bias_kept, HC + 1)

                    def four(i):
                        for u in range(4):
                            for lag, n in ((0, i * 4 + u), (1, i * 4 + u - 1)):
                                if not live(n, E0):
                                    continue
                                w, p = (u - lag) % 4, (u - lag) % 2
                                if lag == 0:
                                    for k in range(2):
                                        pe.wait_ge(ld_w[w][k], (i + 1) * 16)
                                    pe.wait_ge(hid_biased, done(n - 2))
                                    for c in range(HC):
                                        mm = t.matmul(hid_ps[p][:, c, :], first_w[w][:, c:HID:HC],
                                                      pooledT[:, :, bass.ds(n, 1)].rearrange("p b a -> p (b a)"),
                                                      start=True, stop=True)
                                    mm.then_inc(hid_ready, 1)
                                else:
                                    pe.wait_ge(hid_act, done(n))
                                    pe.wait_ge(moe_kept, done(n - 2))
                                    for c in range(HC):
                                        mm = t.matmul(moe_ps[p], second_w[w][:, c, :], act_hid[p][:, c, :],
                                                      start=(c == 0), stop=(c == HC - 1))
                                    mm.then_inc(moe_ready, 1)

                    four(0)
                    with pe.Fori(1, E0 // 4) as i:
                        four(i)
                    pe.wait_ge(hid_act, done(E0 - 1))
                    pe.wait_ge(moe_kept, done(E0 - 3))
                    for c in range(HC):
                        mm = t.matmul(moe_ps[1], second_w[3][:, c, :], act_hid[1][:, c, :],
                                      start=(c == 0), stop=(c == HC - 1))
                    mm.then_inc(moe_ready, 1)

                @block.scalar
                def _(act):
                    credit(act, hid_act)
                    with act.Fori(0, E0 // 2) as i:
                        for u in range(2):
                            n = i * 2 + u
                            act.wait_ge(hid_biased, done(n))
                            act.wait_ge(moe_ready, done(n - 2))
                            nc.scalar.activation(act_hid[u][:], hid[u][:], ACT.Gelu).then_inc(hid_act, 1)

                @block.vector
                def _(dve):
                    v = nc.vector
                    credit(dve, hid_biased, moe_kept)
                    for c in range(HC):
                        dve.wait_ge(bias_turned, c + 1)
                        v.tensor_copy(first_bT[:, :, c:c + 1], bank[c % 2][:, 0:E0].unsqueeze(2)).then_inc(bias_kept, 1)
                    dve.wait_ge(bias_turned, HC + 1)
                    v.tensor_copy(second_bT[:], bank[0][:, 0:E0]).then_inc(bias_kept, 1)
                    dve.wait_ge(bias_kept, HC + 1)

                    def step(i, u, part):
                        j, p, half = item(i, u, 0)
                        if live(j, E0):
                            dve.wait_ge(hid_ready, done(j))
                            dve.wait_ge(hid_act, done(j - 2))
                            v.tensor_tensor(hid[p][:], hid_ps[p],
                                            first_bT[:, bass.ds(j, 1), :].rearrange("p a c -> p (a c)")
                                            .unsqueeze(2).to_broadcast([128, HC, B]), ALU.add)\
                             .then_inc(hid_biased, 1)
                        j, p, half = item(i, u, 1)
                        if live(j, E0):
                            dve.wait_ge(moe_ready, done(j))
                            v.tensor_tensor(moeT[:, bass.ds(j, 1), :].rearrange("p a b -> p (a b)"), moe_ps[p],
                                            second_bT[:, bass.ds(j, 1)].to_broadcast([128, B]), ALU.add)\
                             .then_inc(moe_kept, 1)

                    walk(dve, passed, step, E0, 1)
                    dve.wait_ge(moe_kept, done(E0 - 1))
        with ExitStack() as tmp:
            def tb(name, shape, dt=F32):
                return tmp.enter_context(nc.sbuf_tensor(name, shape, dt))

            def pair(name, shape, dt=F32):
                return [tb(f"{name}{u}", shape, dt) for u in range(2)]

            def nsem(name):
                return tmp.enter_context(nc.semaphore(name))

            experts = tb("experts", [128, E1, 128])
            img = tb("img", [128, H, C])
            moe_b = tb("moe_b", [128, 2, 2, E0])
            moe_w = pair("moe_w", [128, C])
            rs_pair = tb("rs_pair", [128, B])
            rs_b = tb("rs_b", [128, 1])
            S_in = pair("S_in", [128, TILE])
            x2 = pair("x2", [128, TILE])
            mean_all = tb("mean_all", [128, H])
            var_all = tb("var_all2", [128, H])
            spread_all = tb("spread_all", [128, H])
            std_all = tb("std_all", [128, H])
            rstd_all = tb("rstd_all", [128, H])
            bias_g = pair("bias_g", [128, GC])
            brem_g = pair("brem_g", [RP, 1])
            grp = pair("grp", [128, GC, H])
            upc = pair("upc", [128, GC, UPN])
            act_in = pair("act_in", [128, GC, 2, UPN])
            upc_rem = pair("upc_rem", [128, RP])
            act_rem = pair("act_rem", [128, 2, RP])
            rem_in = pair("rem_in", [RP, UPN])
            rem_blk = pair("rem_blk", [RP, GC, REM])
            dnc = pair("dnc", [128, 2, GC, W])
            rem_dn = pair("rem_dn", [RP, W])
            tok = pair("tok", [128, OCTET, C])
            x1_in = [t[:].rearrange("p q c -> p (q c)")[:, k * TILE:(k + 1) * TILE] for t in tok for k in range(2)]
            stat_all = tb("stat_all", [128, H, 6])
            stat8 = tb("stat8", [128, OCTET, 6])
            mv8 = tb("mv8", [128, OCTET, 2])
            std8 = tb("std8", [128, OCTET])
            rstd8 = pair("rstd8", [128, OCTET])
            xh = pair("xh", [128, 2, TILE])
            lg = pair("lg", [128, OCTET, E1])
            mx = tb("mx", [128, OCTET])
            prb = pair("prb", [128, OCTET, E1])
            pr2 = tb("pr2", [128, OCTET, E1])
            sm = tb("sm", [128, OCTET])
            eq = tb("eq", [128, OCTET, E1])
            first = tb("first", [128, OCTET, E1])
            second = tb("second", [128, OCTET, E1])
            p1 = tb("p1", [128, OCTET])
            p2 = tb("p2", [128, OCTET])
            gate = pair("gate", [128, OCTET, E1])
            gate_std = pair("gate_std", [128, OCTET, E1])
            gateTs = pair("gateTs", [ROWS * E1, 2, 128])
            acc = [t[:].rearrange("p (q c) -> p q c", q=ROWS) for t in x2]
            ya = [t[:].rearrange("p q (a c) w -> p (q a) c w", a=2) for t in dnc]
            ys = pair("ys", [128, ROWS, C])
            res = pair("res", [128, TILE])

            blocks = TILES
            octets = TILES // 2
            ht = TILES // 2
            moe_got = nsem("moe_got")
            moe_turned = nsem("moe_turned")
            moe_scaled = nsem("moe_scaled")
            ld_experts = nsem("ld_experts")
            w_centred = nsem("w_centred")
            w_kept = nsem("w_kept")
            ld_x1 = [nsem(f"ld_x1{u}") for u in range(4)]
            ld_S = [[nsem(f"ld_S{u}{h}") for h in range(2)] for u in range(2)]
            ld_rs = [nsem(f"ld_rs{h}") for h in range(2)]
            moe_blank = nsem("moe_blank")
            add_ready = nsem("add_ready")
            x2_ready = nsem("x2_ready")
            img_turned = nsem("img_turned")
            img_kept = nsem("img_kept")
            stat_got = nsem("stat_got")
            stat_chain = nsem("stat_chain")
            mv_std = nsem("mv_std")
            mv_rstd = nsem("mv_rstd")
            grp_chain = nsem("grp_chain")
            bias_got = nsem("bias_got")
            up1_ready = nsem("up1_ready")
            up1_kept = nsem("up1_kept")
            up2_ready = nsem("up2_ready")
            up2_kept = nsem("up2_kept")
            leaky = nsem("leaky")
            rem_ready = nsem("rem_ready")
            down_ready = nsem("down_ready")
            down_kept = nsem("down_kept")
            conv_added = nsem("conv_added")
            mv_tok = [nsem(f"mv_tok{u}") for u in range(2)]
            tok_turned = nsem("tok_turned")
            xh_ready = nsem("xh_ready")
            stat8_chain = nsem("stat8_chain")
            std8_ready = nsem("std8_ready")
            lg_ready = nsem("lg_ready")
            route = nsem("route")
            exp_ready = nsem("exp_ready")
            gate_turned = nsem("gate_turned")
            gate_kept = nsem("gate_kept")
            exp_out = nsem("exp_out")
            act_part = nsem("act_part")
            dve_part = nsem("dve_part")
            y_chain = nsem("y_chain")
            acc_done = nsem("acc_done")
            out_ready = nsem("out_ready")
            out_kept = nsem("out_kept")
            st_out = [nsem(f"st_out{u}") for u in range(2)]

            ROUTES = 25
            ROUTE0 = 2 * CREDIT
            add_ps = bank[0:2]
            turn_ps = bank[2:4]
            up1_ps = bank[0:2]
            up2_ps = duo
            down_ps = bank[2:4]
            tok_ps = bank[0:2]
            lg_ps = bank[2][:, 0:OCTET * E1].rearrange("p (q e) -> p q e", e=E1)
            gT_ps = bank[2][0:ROWS * E1, 128:384].rearrange("p (k t) -> p k t", k=2)
            out_ps = bank[3]
            exp_ps = duo

            def rows_of(j):
                return bass.ds(j * ROWS, ROWS)

            def chan(ap, c0, n):
                return ap[:, :, bass.ds(c0, n)].rearrange("p h c -> p c h")

            def groups_of(eng, up, down):
                up(0, 0)
                up(1, 1)
                down(0, 0)
                settle(eng, passed)
                with eng.Fori(1, GROUPS // 2) as i:
                    up(i * 2, 0)
                    down(i * 2 - 1, 1)
                    up(i * 2 + 1, 1)
                    down(i * 2, 0)
                down(GROUPS - 1, 1)

            with nc.Block() as block:
                @block.sync
                def _(sp):
                    for h in range(2):
                        sp.dma_start(rs_pair[64 * h:64 * h + 64, :], rsum_all[:]).then_inc(ld_rs[h], 16)
                    sp.dma_start(experts[:], expert_w.rearrange("e d c -> d e c")).then_inc(ld_experts, 16)
                    with sp.Fori(0, B) as b:
                        sp.wait_ge(tok_turned, done(b * blocks - 1))
                        settle(sp, passed)
                        with sp.Fori(0, ht // 2) as i:
                            for k in range(2):
                                n = b * TILES + i * 4 + 2 * k
                                sp.wait_ge(add_ready, done(n - 3))
                                for h in range(2):
                                    sp.dma_start(S_in[k][64 * h:64 * h + 64, :],
                                                 S_dram[bass.ds(b, 1), :, bass.ds((i * 4 + 2 * k + h) * TILE, TILE)]
                                                 .rearrange("a e t -> (a e) t")).then_inc(ld_S[k][h], 16)
                                for u in range(2):
                                    sp.wait_ge(x2_ready, done(n + u - 4))
                                    sp.dma_start(x1_in[2 * k + u].rearrange("p (h w) -> p h w", w=W),
                                                 x1_dram[bass.ds(b, 1), :, rows_of(i * 4 + 2 * k + u), :]
                                                 .rearrange("a c h w -> (a c) h w")).then_inc(ld_x1[2 * k + u], 16)
                        sp.wait_ge(conv_added, done(b * 2 * GROUPS + 2 * GROUPS - 1))

                        def step(i, u, part):
                            j, p, half = item(i, u, 0)
                            if live(j, octets):
                                sp.wait_ge(tok_turned, done((b * octets + j) * 2 - 3))
                                sp.dma_start(tok[p][:], img[:, bass.ds(j * OCTET, OCTET), :]).then_inc(mv_tok[p], 16)

                        walk(sp, passed, step, octets, 1)

                @block.tensor
                def _(pe):
                    t = nc.tensor
                    credit(pe, add_ready, img_turned, up1_ready, up2_ready, down_ready, tok_turned, lg_ready,
                           gate_turned, exp_out, out_ready)
                    pe.wait_ge(ld_experts, 16)
                    for h in range(2):
                        t.matmul(bank[h][:], center[:],
                                 experts[:, 4 * h:4 * h + 4, :].rearrange("d e c -> d (e c)"),
                                 start=True, stop=True).then_inc(w_centred, 1)
                    t.matmul(bank[2][:, 0:E1], center[:], router[:], start=True, stop=True).then_inc(w_centred, 1)
                    pe.wait_ge(w_kept, 3)
                    with pe.Fori(0, B) as b:
                        pe.wait_ge(moe_got, b * 3 + 3)
                        pe.wait_ge(moe_blank, 1)
                        settle(pe, passed)
                        for h in range(2):
                            mm = t.transpose(turn_ps[0][:, 128 * h:128 * h + 128],
                                             moe_b[:, h, :, :].rearrange("p k e -> p (k e)"), ident[:])
                        mm.then_inc(moe_turned, 1)
                        pe.wait_ge(moe_scaled, b * 2 + 2)
                        settle(pe, passed)

                        def tiles(i):
                            for u in range(4):
                                n = b * TILES + i * 4 + u
                                k, h = u // 2, u % 2
                                if h == 0:
                                    for g in range(2):
                                        pe.wait_ge(ld_S[k][g], (b * (ht // 2) + i + 1) * 16)
                                pe.wait_ge(x2_ready, done(n - 2))
                                t.matmul(add_ps[h][:], moe_w[h][:], S_in[k][:], start=True, stop=True)\
                                 .then_inc(add_ready, 1)
                                if u or not isinstance(i, int):
                                    turn(n - 1, 1 - h)

                        def turn(n, p):
                            pe.wait_ge(x2_ready, done(n))
                            pe.wait_ge(img_kept, done(n - 2))
                            for q in range(ROWS):
                                mm = t.transpose(turn_ps[p][:, q * 128:q * 128 + 128],
                                                 x2[p][:, q * 128:q * 128 + 128], ident[:])
                            mm.then_inc(img_turned, 1)

                        pe.wait_ge(out_kept, done(b * blocks - 1))
                        tiles(0)
                        settle(pe, passed)
                        with pe.Fori(1, ht // 2) as i:
                            tiles(i)
                        turn(b * TILES + TILES - 1, 1)

                        def up(g, p):
                            G = b * GROUPS + g
                            pe.wait_ge(grp_chain, G * 2 + 2 + CREDIT * 2)
                            for c in range(GC + 1):
                                if c < GC:
                                    n = G * GC + c
                                    pe.wait_ge(up1_kept, done(n - 2))
                                    t.matmul(up1_ps[c % 2][:, 0:UPN], grp[p][:, c, :], up_mat[:],
                                             start=True, stop=True).then_inc(up1_ready, 1)
                                if c >= 1:
                                    second_up(G, p, c - 1)
                            second_up(G, p, GC)

                        def second_up(G, p, c):
                            n = G * (GC + 1) + c
                            bankp = (p + c) % 2
                            pe.wait_ge(up2_kept, done(n - 2))
                            if c < GC:
                                pe.wait_ge(up1_kept, done(G * GC + c))
                                for m in range(2):
                                    mm = t.matmul(up2_ps[bankp][:, m, 0:UPN], upc[p][:, c, m * 128:m * 128 + 128],
                                                  up_mat[:], start=True, stop=True)
                            else:
                                pe.wait_ge(rem_ready, G * 3 + 1 + CREDIT * 3)
                                mm = t.matmul(up2_ps[bankp][0:RP, 0, 0:UPN], upc_rem[p][:], up_mat[:],
                                              start=True, stop=True)
                            mm.then_inc(up2_ready, 1)

                        def down(g, p):
                            G = b * GROUPS + g
                            pe.wait_ge(leaky, done(G * (GC + 1) + GC))
                            for k in (0, 1, 3, 4):
                                h, m = k // 3, k % 3 % 2
                                if k == 3:
                                    remainder(G, p)
                                ps = down_ps[(p + k) % 2]
                                drain(G, k)
                                for c in range(4):
                                    ch = 4 * h + c
                                    for q in range(2):
                                        t.matmul(ps[:, c * 128:c * 128 + 128],
                                                 act_in[p][:, ch, q, m * 128:m * 128 + 128],
                                                 down_mat[:, q, :], start=(c == 0 and q == 0), stop=False,
                                                 skip_group_check=True)
                                mm = t.matmul(ps[:].rearrange("p (c w) -> p c w", w=W)[:, :, W - EDGE:W],
                                              rem_in[p][:, m * 128:m * 128 + 128], down_edge[:, 4 * h:4 * h + 4, :],
                                              start=False, stop=True, skip_group_check=True)
                                mm.then_inc(down_ready, 1)
                            for h in range(2):
                                pe.wait_ge(down_kept, done(G * 5 + 2 + 2 * h))
                                drain(G, 5 + h)
                                ps = down_ps[(p + 5 + h) % 2]
                                for c in range(4):
                                    for q in range(2):
                                        t.matmul(ps[:, c * 128:c * 128 + 128], dnc[p][:, q, 4 * h + c, :],
                                                 down_mat[:, q, :], start=(c == 0 and q == 0), stop=False,
                                                 skip_group_check=True)
                                t.matmul(ps[:].rearrange("p (c w) -> p c w", w=W)[:, :, W - EDGE:W],
                                         rem_dn[p][:], down_edge[:, 4 * h:4 * h + 4, :], start=False, stop=True,
                                         skip_group_check=True).then_inc(down_ready, 1)

                        def remainder(G, p):
                            pe.wait_ge(rem_ready, G * 3 + 3 + CREDIT * 3)
                            drain(G, 2)
                            ps = down_ps[p]
                            for q in range(2):
                                t.matmul(ps[0:RP, 0:W], act_rem[p][:, q, :], down_mat[:, q, :],
                                         start=(q == 0), stop=False, skip_group_check=True)
                            t.matmul(ps[0:RP, W - EDGE:W], rem_blk[p][:].rearrange("p c r -> p (c r)"), down_edge1[:],
                                     start=False, stop=True, skip_group_check=True).then_inc(down_ready, 1)

                        def drain(G, k):
                            if k < 2:
                                pe.wait_ge(conv_added, done(G * 2 - 2 + k))
                            else:
                                pe.wait_ge(down_kept, done(G * 5 + k - 2))

                        groups_of(pe, up, down)


                        def step(i, u, part):
                            j, p, half = item(i, u, 0)
                            j1, p1_, half1 = item(i, u, 1)
                            j2, p2_, half2 = item(i, u, 2)
                            n, n1, n2 = (b * octets + k for k in (j, j1, j2))
                            if live(j, octets):
                                pe.wait_ge(mv_tok[p], (b * (octets // 2) + half + 1) * 16)
                                for k in range(2):
                                    pe.wait_ge(xh_ready, done(n * 2 + k - 2))
                                    for q in range(ROWS):
                                        mm = t.transpose(tok_ps[k][:, q * 128:q * 128 + 128],
                                                         tok[p][:, k * ROWS + q, :], ident[:])
                                    mm.then_inc(tok_turned, 1)
                            if live(j1, octets):
                                expert_row(n1, p1_, 0)
                                pe.wait_ge(route, n1 * ROUTES + ROUTES + ROUTE0)
                                for k in range(2):
                                    mm = t.transpose(gT_ps[:, k, :], gate[p1_][:, k * ROWS:k * ROWS + ROWS, :]
                                                     .rearrange("p q e -> p (q e)"), ident[:])
                                mm.then_inc(gate_turned, 1)
                                expert_row(n1, p1_, 1)
                            if live(j, octets):
                                pe.wait_ge(xh_ready, done(n * 2 + 1))
                                pe.wait_ge(gate_kept, done(n - 1))
                                for q in range(OCTET):
                                    mm = t.matmul(lg_ps[:, q, :],
                                                  xh[p][:, q // ROWS, q % ROWS * 128:q % ROWS * 128 + 128],
                                                  router[:], start=True, stop=True)
                                mm.then_inc(lg_ready, 1)
                            if live(j1, octets):
                                expert_row(n1, p1_, 2)
                                expert_row(n1, p1_, 3)
                            if live(j2, octets):
                                output(n2, p2_, 1)
                            if live(j1, octets):
                                for q in range(4, OCTET):
                                    expert_row(n1, p1_, q)
                                output(n1, p1_, 0)

                        def output(n, p, k):
                            pe.wait_ge(acc_done, done(n * 2 + k))
                            pe.wait_ge(gate_kept, done(n))
                            pe.wait_ge(out_kept, done(n * 2 + k - 1))
                            for q in range(ROWS):
                                at = slice(q * 128, q * 128 + 128)
                                t.matmul(out_ps[:, at], acc[k][:, q, :], ident[:], start=True, stop=False)
                                mm = t.matmul(out_ps[:, at], ebias[:, q, :], gateTs[p][:, k, :],
                                              start=False, stop=True)
                            mm.then_inc(out_ready, 1)

                        def expert_row(n, p, q):
                            r = n * OCTET + q
                            for h in range(2):
                                if h:
                                    pe.wait_ge(act_part, done(r - 2))
                                else:
                                    pe.wait_ge(dve_part, (r - 1 + CREDIT) * DVE_EXPERTS)
                                mm = t.matmul(exp_ps[q % 2][:, h, :],
                                              xh[p][:, q // ROWS, q % ROWS * 128:q % ROWS * 128 + 128],
                                              experts[:, 4 * h:4 * h + 4, :].rearrange("d e c -> d (e c)"),
                                              start=True, stop=True)
                            mm.then_inc(exp_out, 1)

                        walk(pe, passed, step, octets, 2)

                @block.scalar
                def _(act):
                    a = nc.scalar
                    for s in st_out:
                        act.sem_inc(s, 16)
                    credit(act, img_kept, up1_kept, up2_kept, down_kept, xh_ready, act_part, gate_kept, out_kept)
                    with act.Fori(0, B) as b:
                        act.wait_ge(acc_done, done(b * blocks - 1))
                        settle(act, passed)
                        with act.Fori(0, ht) as i:
                            for u in range(2):
                                n = b * TILES + i * 2 + u
                                act.wait_ge(img_turned, done(n))
                                a.activation(img[:, rows_of(i * 2 + u), :],
                                             turn_ps[u][:].rearrange("p (q c) -> p q c", q=ROWS), ACT.Copy)\
                                 .then_inc(img_kept, 1)
                        act.wait_ge(stat_chain, b * 6 + 4)
                        a.activation(std_all[:], var_all[:], ACT.Sqrt, bias=eps6[:]).then_inc(mv_std, 1)

                        def up(g, p):
                            G = b * GROUPS + g
                            act.wait_ge(up2_ready, done(G * (GC + 1) - GC - 2))
                            for c in range(GC + 1):
                                if c < GC:
                                    act.wait_ge(up1_ready, done(G * GC + c))
                                    a.activation(upc[p][:, c, :], up1_ps[c % 2][:, 0:UPN], ACT.Copy)\
                                     .then_inc(up1_kept, 1)
                                if c == 0:
                                    act.wait_ge(down_ready, done(G * 7 - 14 + 4))
                                if c == 1:
                                    act.wait_ge(bias_got, G * 2 + 2 + CREDIT * 2)
                                if c >= 1:
                                    act.wait_ge(up2_ready, done(G * (GC + 1) + c - 1))
                                    a.activation(act_in[p][:, c - 1, :, :], up2_ps[(p + c - 1) % 2][:, :, 0:UPN],
                                                 ACT.Identity, scale=GAIN, bias=bias_g[p][:, c - 1:c])\
                                     .then_inc(up2_kept, 1)
                            act.wait_ge(up2_ready, done(G * (GC + 1) + GC))
                            a.activation(rem_in[p][:], up2_ps[p][0:RP, 0, 0:UPN], ACT.Identity, scale=GAIN,
                                         bias=brem_g[p][:]).then_inc(up2_kept, 1)

                        def down(g, p):
                            G = b * GROUPS + g
                            act.wait_ge(down_ready, done(G * 7 - 14 + 6))
                            for k in range(5):
                                act.wait_ge(down_ready, done(G * 7 + k))
                                if k == 2:
                                    a.activation(rem_dn[p][:], down_ps[p][0:RP, 0:W], ACT.Copy).then_inc(down_kept, 1)
                                else:
                                    h, m = k // 3, k % 3 % 2
                                    a.activation(dnc[p][:, m, 4 * h:4 * h + 4, :],
                                                 down_ps[(p + k) % 2][:].rearrange("p (c w) -> p c w", w=W), ACT.Copy)\
                                     .then_inc(down_kept, 1)

                        groups_of(act, up, down)

                        def step(i, u, part):
                            j, p, half = item(i, u, 0)
                            j1, p1_, half1 = item(i, u, 1)
                            j2, p2_, half2 = item(i, u, 2)
                            n, n1, n2 = (b * octets + k for k in (j, j1, j2))
                            if live(j, octets):
                                act.wait_ge(exp_out, done((n - 1) * OCTET - 1))
                                for k in range(2):
                                    act.wait_ge(tok_turned, done(n * 2 + k))
                                    a.activation(xh[p][:, k, :], tok_ps[k][:], ACT.Copy).then_inc(xh_ready, 1)
                            if live(j1, octets):
                                act.wait_ge(route, n1 * ROUTES + ROUTES + ROUTE0)
                                weigh(n1, p1_, 0)
                                act.wait_ge(gate_turned, done(n1))
                                act.wait_ge(out_ready, done(n1 * 2 - 3))
                                a.activation(gateTs[p1_][:], gT_ps, ACT.Copy).then_inc(gate_kept, 1)
                                weigh(n1, p1_, 1)
                            if live(j, octets):
                                act.wait_ge(stat8_chain, n * 2 + 2)
                                act.wait_ge(route, n * ROUTES - ROUTES + 1 + ROUTE0)
                                a.activation(std8[:], mv8[:, :, 1], ACT.Sqrt, bias=eps5[:]).then_inc(std8_ready, 1)
                            if live(j1, octets):
                                weigh(n1, p1_, 2)
                                weigh(n1, p1_, 3)
                            if live(j, octets):
                                act.wait_ge(route, n * ROUTES + 5 + ROUTE0)
                                a.activation(prb[p][:], lg[p][:], ACT.Exp).then_inc(exp_ready, 1)
                            if live(j1, octets):
                                weigh(n1, p1_, 4)
                            if live(j2, octets):
                                keep(n2, j2, 1)
                            if live(j1, octets):
                                for q in range(5, OCTET):
                                    weigh(n1, p1_, q)
                                keep(n1, j1, 0)

                        def keep(n, j, k):
                            act.wait_ge(out_ready, done(n * 2 + k))
                            act.wait_ge(st_out[k], rounds(b * ht + j))
                            a.activation(res[k][:], out_ps[:], ACT.Copy).then_inc(out_kept, 1)
                            act.wait_ge(out_kept, done(n * 2 + k))
                            act.dma_start(out[bass.ds(b, 1), :, bass.ds(j * OCTET + k * ROWS, ROWS), :]
                                          .rearrange("a c h w -> (a c) h w"),
                                          res[k][:].rearrange("p (h w) -> p h w", w=W)).then_inc(st_out[k], 16)

                        def weigh(n, p, q):
                            k = q // ROWS
                            if q % ROWS == 0:
                                act.wait_ge(y_chain, (n * 2 + k) * 2 - 2 + CREDIT * 2)
                            act.wait_ge(exp_out, done(n * OCTET + q))
                            for e in range(DVE_EXPERTS, E1):
                                ins = a.activation(ya[k][:, q % ROWS, e - DVE_EXPERTS, :],
                                                   exp_ps[q % 2][:, e // 4, (e % 4) * 128:(e % 4) * 128 + 128],
                                                   ACT.Copy, scale=gate_std[p][:, q, e:e + 1])
                            ins.then_inc(act_part, 1)

                        walk(act, passed, step, octets, 2)
                    for s in st_out:
                        act.wait_ge(s, rounds(B * ht))

                @block.gpsimd
                def _(pool):
                    g_ = nc.gpsimd
                    pool.sem_inc(grp_chain, CREDIT * 2)
                    pool.sem_inc(y_chain, CREDIT * 2)
                    with pool.Fori(0, B) as b:
                        pool.wait_ge(mv_rstd, b + 1)
                        settle(pool, passed)
                        with pool.Fori(0, GROUPS // 2) as i:
                            for p in range(2):
                                g = i * 2 + p
                                G = b * GROUPS + g
                                pool.wait_ge(up1_ready, done(G * GC - GC - 1))
                                pool.wait_ge(grp_chain, G * 2 + CREDIT * 2)
                                g_.tensor_tensor(grp[p][:], chan(img, g * GC, GC),
                                                 mean_all[:].unsqueeze(1).to_broadcast([128, GC, H]),
                                                 ALU.subtract).then_inc(grp_chain, 1)
                                pool.wait_ge(grp_chain, G * 2 + 1 + CREDIT * 2)
                                g_.tensor_tensor(grp[p][:], grp[p][:],
                                                 rstd_all[:].unsqueeze(1).to_broadcast([128, GC, H]),
                                                 ALU.mult).then_inc(grp_chain, 1)
                        settle(pool, passed)
                        with pool.Fori(0, octets) as j:
                            for k in range(2):
                                n = b * blocks + j * 2 + k
                                pool.wait_ge(act_part, done(n * ROWS + ROWS - 1))
                                pool.wait_ge(acc_done, done(n - 2))
                                g_.tensor_tensor(ya[k][:, :, 0:2, :], ya[k][:, :, 0:2, :], ya[k][:, :, 2:4, :],
                                                 ALU.add).then_inc(y_chain, 1)
                                pool.wait_ge(y_chain, n * 2 + 1 + CREDIT * 2)
                                g_.tensor_tensor(ys[k][:], ya[k][:, :, 0, :], ya[k][:, :, 1, :], ALU.add)\
                                  .then_inc(y_chain, 1)

                @block.vector
                def _(dve):
                    v = nc.vector
                    credit(dve, x2_ready, stat_got, leaky, conv_added, acc_done)
                    dve.sem_inc(route, ROUTE0)
                    dve.sem_inc(rem_ready, CREDIT * 3)
                    dve.sem_inc(bias_got, CREDIT * 2)
                    dve.sem_inc(dve_part, CREDIT * DVE_EXPERTS)

                    def keep_stats(b, i, u):
                        j, p, half = item(i, u, 2)
                        if live(j, TILES):
                            dve.wait_ge(img_kept, done(b * TILES + j))
                            for q in range(ROWS):
                                ins = v.bn_stats(stat_all[:, bass.ds(j * ROWS + q, 1), :].rearrange("p a s -> p (a s)"),
                                                 img[:, bass.ds(j * ROWS + q, 1), :].rearrange("p a c -> p (a c)"))
                            ins.then_inc(stat_got, 1)

                    v.memset(moe_b[:], 0.0).then_inc(moe_blank, 1)
                    dve.wait_ge(moe_blank, 1)
                    for h in range(2):
                        dve.wait_ge(ld_rs[h], 16)
                    dve.wait_ge(w_centred, 3)
                    for h in range(2):
                        v.tensor_copy(experts[:, 4 * h:4 * h + 4, :],
                                      bank[h][:].rearrange("p (e c) -> p e c", c=C)).then_inc(w_kept, 1)
                    v.tensor_copy(router[:], bank[2][:, 0:E1]).then_inc(w_kept, 1)

                    with dve.Fori(0, B) as b:
                        for h in range(2):
                            v.tensor_copy(moe_b[:, h, h, :], moeT[:, :, bass.ds(b, 1)].rearrange("p e a -> p (e a)"))\
                             .then_inc(moe_got, 1)
                        v.tensor_copy(rs_b[:], rs_pair[:, bass.ds(b, 1)]).then_inc(moe_got, 1)
                        dve.wait_ge(moe_turned, b + 1)
                        dve.wait_ge(moe_got, b * 3 + 3)
                        for h in range(2):
                            v.tensor_scalar(moe_w[h][:], turn_ps[0][:, 128 * h:128 * h + 128], rs_b[:], None,
                                            ALU.mult).then_inc(moe_scaled, 1)
                        dve.wait_ge(out_ready, done(b * blocks - 1))
                        settle(dve, passed)

                        def tiles(i):
                            for u in range(4):
                                n = b * TILES + i * 4 + u
                                dve.wait_ge(add_ready, done(n))
                                dve.wait_ge(ld_x1[u], (b * (ht // 2) + i + 1) * 16)
                                dve.wait_ge(img_turned, done(n - 2))
                                v.tensor_tensor(x2[u % 2][:], add_ps[u % 2][:], x1_in[u], ALU.add).then_inc(x2_ready, 1)
                                keep_stats(b, i * 2 + u // 2, u % 2)

                        tiles(0)
                        settle(dve, passed)
                        with dve.Fori(1, ht // 2) as i:
                            tiles(i)
                        for u in range(2):
                            keep_stats(b, ht, u)
                        dve.wait_ge(stat_got, done(b * TILES + TILES - 1))
                        link = Chain(dve, stat_chain, b * 6)
                        link(v.tensor_tensor(spread_all[:], stat_all[:, :, 1], stat_all[:, :, 4], ALU.subtract))
                        link(v.scalar_tensor_tensor(out=spread_all[:], in0=spread_all[:], scalar=0.25,
                                                    in1=spread_all[:], op0=ALU.mult, op1=ALU.mult))
                        link(v.tensor_tensor(var_all[:], stat_all[:, :, 2], stat_all[:, :, 5], ALU.add))
                        link(v.scalar_tensor_tensor(out=var_all[:], in0=var_all[:], scalar=1.0 / C, in1=spread_all[:],
                                                    op0=ALU.mult, op1=ALU.add))
                        link(v.tensor_tensor(mean_all[:], stat_all[:, :, 1], stat_all[:, :, 4], ALU.add))
                        link(v.tensor_scalar(mean_all[:], mean_all[:], 0.5, None, ALU.mult))
                        dve.wait_ge(mv_std, b + 1)
                        v.reciprocal(rstd_all[:], std_all[:]).then_inc(mv_rstd, 1)

                        def up(g, p):
                            G = b * GROUPS + g
                            dve.wait_ge(up2_kept, done(G * (GC + 1) - GC - 2))
                            v.tensor_copy(bias_g[p][:], bias_all[:, bass.ds(g * GC, GC)]).then_inc(bias_got, 1)
                            v.tensor_copy(brem_g[p][:], bias_rem[:, bass.ds(g, 1)]).then_inc(bias_got, 1)
                            for c in range(GC):
                                n = G * (GC + 1) + c
                                dve.wait_ge(up2_kept, done(n))
                                z = act_in[p][:, c, :, :]
                                v.scalar_tensor_tensor(out=z, in0=z, scalar=SLOPE, in1=z, op0=ALU.mult, op1=ALU.max)\
                                 .then_inc(leaky, 1)
                                if c == GC - 3:
                                    dve.wait_ge(up1_kept, done(G * GC + GC - 1))
                                    v.tensor_copy(upc_rem[p][:].rearrange("p (c r) -> p c r", r=REM),
                                                  upc[p][:, :, 2 * W:UPN]).then_inc(rem_ready, 1)
                            n = G * (GC + 1) + GC
                            dve.wait_ge(leaky, done(n - 1))
                            v.tensor_copy(act_rem[p][:].rearrange("p q (c r) -> p q c r", r=REM),
                                          act_in[p][:, :, :, 2 * H:UPN].rearrange("p c q r -> p q c r"))\
                             .then_inc(rem_ready, 1)
                            dve.wait_ge(up2_kept, done(n))
                            z = rem_in[p][:]
                            v.scalar_tensor_tensor(out=z, in0=z, scalar=SLOPE, in1=z, op0=ALU.mult, op1=ALU.max)\
                             .then_inc(leaky, 1)
                            dve.wait_ge(leaky, done(n))
                            v.tensor_tensor(rem_blk[p][:],
                                            rem_in[p][:, 2 * H:UPN].unsqueeze(1).to_broadcast([RP, GC, REM]),
                                            block_mask[:], ALU.mult).then_inc(rem_ready, 1)

                        def down(g, p):
                            G = b * GROUPS + g
                            for h in range(2):
                                dve.wait_ge(down_ready, done(G * 7 + 5 + h))
                                at = chan(img, g * GC + 4 * h, 4)
                                v.tensor_tensor(at, down_ps[(p + 5 + h) % 2][:].rearrange("p (c h) -> p c h", h=H),
                                                at, ALU.add).then_inc(conv_added, 1)

                        groups_of(dve, up, down)
                        dve.wait_ge(conv_added, done(b * 2 * GROUPS + 2 * GROUPS - 1))

                        def step(i, u, part):
                            j, p, half = item(i, u, 0)
                            j1, p1_, half1 = item(i, u, 1)
                            j2, p2_, half2 = item(i, u, 2)
                            n, n1, n2 = (b * octets + k for k in (j, j1, j2))
                            now, before = live(j, octets), live(j1, octets)
                            link = Braid(dve, route, n * ROUTES + ROUTE0)

                            def w(q, e):
                                if before:
                                    weigh(n1, j1, p1_, q, e)
                                link.ready()

                            for e in range(DVE_EXPERTS):
                                w(0, e)
                                if now:
                                    for q in range(2 * e, 2 * e + 2):
                                        ins = v.bn_stats(stat8[:, q, :], img[:, bass.ds(j * OCTET + q, 1), :]
                                                         .rearrange("p a c -> p (a c)"))
                            if now:
                                ins.then_inc(stat8_chain, 1)
                            w(1, 0)
                            if now:
                                dve.wait_ge(stat8_chain, n * 2 + 1)
                                dve.wait_ge(std8_ready, n)
                                settle(dve, passed)
                                for q in range(OCTET):
                                    ins = v.bn_aggr(mv8[:, q, :], stat8[:, q, :])
                                ins.then_inc(stat8_chain, 1)
                            for e in range(1, DVE_EXPERTS):
                                w(1, e)
                            if live(j2, octets):
                                sum_up(n2, 1)
                            w(2, 0)
                            if now:
                                dve.wait_ge(std8_ready, n + 1)
                                link(v.reciprocal(rstd8[p][:], std8[:]))
                            w(2, 1)
                            if now:
                                dve.wait_ge(lg_ready, done(n))
                                link(v.tensor_tensor(lg[p][:], lg_ps, spread(rstd8[p]), ALU.mult))
                            w(2, 2)
                            if now:
                                link(v.tensor_tensor(lg[p][:], lg[p][:], router_b_all[:].unsqueeze(1)
                                                     .to_broadcast([128, OCTET, E1]), ALU.add))
                            w(2, 3)
                            if now:
                                link(v.tensor_reduce(mx[:], lg[p][:], AX_X, ALU.max))
                            w(3, 0)
                            if now:
                                link(v.tensor_tensor(lg[p][:], lg[p][:], spread(mx), ALU.subtract))
                            w(3, 1)
                            w(3, 2)
                            w(3, 3)
                            P = prb[p][:]
                            if now:
                                dve.wait_ge(exp_ready, n + 1)
                                link(v.tensor_reduce(sm[:], P, AX_X, ALU.add))
                            w(4, 0)
                            if now:
                                link(v.reciprocal(p1[:], sm[:]))
                            w(4, 1)
                            if now:
                                link(v.tensor_tensor(P, P, spread(p1), ALU.mult))
                            w(4, 2)
                            if now:
                                link(v.tensor_reduce(p1[:], P, AX_X, ALU.max))
                            w(4, 3)
                            if now:
                                link(v.tensor_tensor(eq[:], P, spread(p1), ALU.is_equal))
                            w(5, 0)
                            if now:
                                link(v.tensor_tensor(eq[:], eq[:], desc(), ALU.mult))
                            w(5, 1)
                            if now:
                                link(v.tensor_reduce(mx[:], eq[:], AX_X, ALU.max))
                            w(5, 2)
                            if now:
                                link(v.tensor_tensor(first[:], eq[:], spread(mx), ALU.is_equal))
                            w(5, 3)
                            if now:
                                link(v.scalar_tensor_tensor(out=pr2[:], in0=first[:], scalar=-2.0, in1=P,
                                                            op0=ALU.mult, op1=ALU.add))
                            if before:
                                sum_up(n1, 0)
                            w(6, 0)
                            if now:
                                link(v.tensor_reduce(p2[:], pr2[:], AX_X, ALU.max))
                            w(6, 1)
                            if now:
                                link(v.tensor_tensor(eq[:], pr2[:], spread(p2), ALU.is_equal))
                            w(6, 2)
                            if now:
                                link(v.tensor_tensor(eq[:], eq[:], desc(), ALU.mult))
                            w(6, 3)
                            if now:
                                link(v.tensor_reduce(mx[:], eq[:], AX_X, ALU.max))
                            w(7, 0)
                            if now:
                                link(v.tensor_tensor(second[:], eq[:], spread(mx), ALU.is_equal))
                            w(7, 1)
                            if now:
                                link(v.tensor_tensor(sm[:], p1[:], p2[:], ALU.add))
                            w(7, 2)
                            if now:
                                link(v.reciprocal(p1[:], sm[:]))
                            w(7, 3)
                            if now:
                                link(v.tensor_tensor(first[:], first[:], second[:], ALU.add))
                                link.ready()
                                link(v.tensor_tensor(P, P, first[:], ALU.mult))
                                link.ready()
                                link(v.tensor_tensor(gate[p][:], P, spread(p1), ALU.mult))
                                link.ready()
                                dve.wait_ge(act_part, done(n * OCTET - OCTET - 1))
                                link(v.tensor_tensor(gate_std[p][:], gate[p][:], spread(rstd8[p]), ALU.mult))
                                link.ready()
                                assert link.n == ROUTES, link.n

                        def spread(t):
                            return t[:].unsqueeze(2).to_broadcast([128, OCTET, E1])

                        def desc():
                            return desc8[:].unsqueeze(1).to_broadcast([128, OCTET, E1])

                        def weigh(n, j, p, q, e):
                            r, k = n * OCTET + q, q // ROWS
                            if e:
                                dve.wait_ge(dve_part, (r + CREDIT) * DVE_EXPERTS + e)
                            else:
                                dve.wait_ge(exp_out, done(r))
                                if q % ROWS == 0:
                                    dve.wait_ge(out_ready, done(n * 2 + k - 2))
                            before = acc[k][:, q % ROWS, :] if e else \
                                img[:, bass.ds(j * OCTET + q, 1), :].rearrange("p a c -> p (a c)")
                            v.scalar_tensor_tensor(
                                out=acc[k][:, q % ROWS, :],
                                in0=exp_ps[q % 2][:, e // 4, (e % 4) * 128:(e % 4) * 128 + 128],
                                scalar=gate_std[p][:, q, e:e + 1], in1=before, op0=ALU.mult, op1=ALU.add)\
                             .then_inc(dve_part, 1)

                        def sum_up(n, k):
                            dve.wait_ge(y_chain, (n * 2 + k) * 2 + 2 + CREDIT * 2)
                            dve.wait_ge(dve_part, (n * OCTET + k * ROWS + ROWS + CREDIT) * DVE_EXPERTS)
                            v.tensor_tensor(acc[k], acc[k], ys[k][:], ALU.add).then_inc(acc_done, 1)

                        walk(dve, passed, step, octets, 2)


_INS = ["x", "L0_conv_w1", "L0_conv_in_gamma", "L0_conv_in_beta", "L0_conv_w2", "L0_conv_b2",
        "L0_ffn_gate_w", "L0_ffn_gate_b", "L0_ffn_weight1", "L0_ffn_weight2", "L1_conv_bias",
        "L1_conv_up_filter", "L1_conv_down_filter", "L1_ffn_router_w", "L1_ffn_router_b",
        "L1_ffn_expert_w", "L1_ffn_expert_b"]


def kernel(**inputs):
    import concourse.bacc as _bacc
    from concourse.bass_utils import run_bass_kernel_spmd as _run

    nc = _bacc.Bacc("TRN2", target_bir_lowering=False, num_devices=1)
    arrays, args = {}, []
    for name in _INS:
        a = np.ascontiguousarray(inputs[name])
        arrays[f"in_{name}"] = a
        args.append(nc.dram_tensor(f"in_{name}", a.shape, mybir.dt.from_np(a.dtype), kind="ExternalInput").ap())
    args.append(nc.dram_tensor("out_0", (B, C, H, W), F32, kind="ExternalOutput").ap())
    metaformer_kernel(nc, *args)
    return _run(nc, [arrays], core_ids=[0]).results[0]["out_0"]
```
